# Optimizing a Trainium2 kernel written in Bass

```python
import numpy as np
import jax
import jax.numpy as jnp

def _softmax(x, axis=-1):
    return jax.nn.softmax(x, axis=axis)

def _gelu(x):
    return jax.nn.gelu(x, approximate=True)

def _silu(x):
    return jax.nn.silu(x)

def _sigmoid(x):
    return jax.nn.sigmoid(x)

def _layernorm(x, axis=-1, eps=1e-05):
    m = jnp.mean(x, axis=axis, keepdims=True)
    v = jnp.var(x, axis=axis, keepdims=True)
    return (x - m) / jnp.sqrt(v + eps)

def _scatter_add(tgt, idx, src, axis=0):
    return tgt.at[idx].add(src)

def _segment_sum(src, seg, n):
    return jax.ops.segment_sum(src, seg, n)
kernel_name = 'mk_audio_tower_d1_tok_audfeat256_r4_e70821'

def setup_inputs(seed: int=0):
    np.random.seed(seed)
    _w = jnp.asarray

    def _rec_inputs():
        import jax
        import jax.numpy as jnp
        _rk = jax.random.key(seed)
        x = -0.000392918 + 0.999932 * jax.random.normal(jax.random.fold_in(_rk, 1), (64, 250, 128), jnp.float32)
        return x
    x = _rec_inputs()

    def _L0_tok_setup():
        import jax, jax.numpy as jnp
        from jax import lax
        import numpy as np
        BN_EPS = 0.001

        @jax.custom_vjp
        def ste_sign(x):
            return jnp.where(x >= 0, 1.0, -1.0).astype(x.dtype)

        def _ste_fwd(x):
            return (ste_sign(x), x)

        def _ste_bwd(x, g):
            return (g * (jnp.abs(x) <= 1.0).astype(g.dtype),)
        ste_sign.defvjp(_ste_fwd, _ste_bwd)
        key = jax.random.key(seed)
        ks = jax.random.split(key, 6)
        x = jax.random.normal(ks[0], (64, 512, 128), dtype=jnp.float32)
        kernel = jax.random.normal(ks[1], (3, 128, 64), dtype=jnp.float32) * 0.05
        bias = jax.random.normal(ks[2], (64,), dtype=jnp.float32) * 0.01
        beta = jax.random.normal(ks[3], (64,), dtype=jnp.float32) * 0.01
        moving_mean = jax.random.normal(ks[4], (64,), dtype=jnp.float32) * 0.1
        moving_var = jax.random.uniform(ks[5], (64,), dtype=jnp.float32) + 0.5
        return {'x': x, 'kernel': kernel, 'bias': bias, 'beta': beta, 'moving_mean': moving_mean, 'moving_var': moving_var}
    _L0_tok_all = _L0_tok_setup()
    _L0_tok_in = {k: v for k, v in _L0_tok_all.items() if k in ('kernel', 'bias', 'beta', 'moving_mean', 'moving_var')}
    del _L0_tok_all

    def _L0_attn_setup():
        import jax, jax.numpy as jnp
        import numpy as np
        B, N, C, H = (4, 256, 64, 8)
        HD = C // H
        BN_EPS = 1e-05
        key = jax.random.key(seed)
        ks = jax.random.split(key, 6)

        def w(k, shape, sc=0.02):
            return jax.random.normal(k, shape, jnp.float32) * sc
        return {'x': jax.random.normal(ks[0], (B, N, C), jnp.float32), 'w_qkv': w(ks[1], (3 * C, C)), 'b_qkv': jnp.zeros((3 * C,), jnp.float32), 'w_proj': w(ks[2], (C, C)), 'b_proj': jnp.zeros((C,), jnp.float32), 'scale': jnp.float32(HD ** (-0.5)), 'riem_scale': jnp.float32(HD ** (-0.5)), 'grassman_scale': jnp.float32(HD ** (-0.5)), 'bn_gamma': jnp.ones((3 * H,), jnp.float32), 'bn_beta': jnp.zeros((3 * H,), jnp.float32), 'bn_mean': jnp.zeros((3 * H,), jnp.float32), 'bn_var': jnp.ones((3 * H,), jnp.float32), 'conv_w': w(ks[3], (H, 3 * H)), 'conv_b': jnp.zeros((H,), jnp.float32)}
    _L0_attn_all = _L0_attn_setup()
    _L0_attn_in = {k: v for k, v in _L0_attn_all.items() if k in ('w_qkv', 'b_qkv', 'w_proj', 'b_proj', 'scale', 'riem_scale', 'grassman_scale', 'bn_gamma', 'bn_beta', 'bn_mean', 'bn_var', 'conv_w', 'conv_b')}
    del _L0_attn_all

    def _L0_ffn_setup():
        import jax, jax.numpy as jnp
        import numpy as np
        C = 64
        HID = 256
        E = 8
        TEMP = 1.0
        key = jax.random.key(seed)
        ks = jax.random.split(key, 7)
        x = jax.random.normal(ks[0], (8, 4096, C), dtype=jnp.float32)
        W1 = jax.random.normal(ks[1], (C, HID), dtype=jnp.float32) * 0.02
        b1 = jnp.zeros((HID,), dtype=jnp.float32)
        Wg = jax.random.normal(ks[2], (HID, E), dtype=jnp.float32) * 0.02
        bg = jnp.zeros((E,), dtype=jnp.float32)
        Wd = jax.random.normal(ks[3], (E, HID, C), dtype=jnp.float32) * 0.02
        bd = jnp.zeros((E, C), dtype=jnp.float32)
        return {'x': x, 'W1': W1, 'b1': b1, 'Wg': Wg, 'bg': bg, 'Wd': Wd, 'bd': bd}
    _L0_ffn_all = _L0_ffn_setup()
    _L0_ffn_in = {k: v for k, v in _L0_ffn_all.items() if k in ('W1', 'b1', 'Wg', 'bg', 'Wd', 'bd')}
    del _L0_ffn_all
    return {'x': x, 'L0_tok_kernel': _L0_tok_in['kernel'], 'L0_tok_bias': _L0_tok_in['bias'], 'L0_tok_beta': _L0_tok_in['beta'], 'L0_tok_moving_mean': _L0_tok_in['moving_mean'], 'L0_tok_moving_var': _L0_tok_in['moving_var'], 'L0_attn_w_qkv': _L0_attn_in['w_qkv'], 'L0_attn_b_qkv': _L0_attn_in['b_qkv'], 'L0_attn_w_proj': _L0_attn_in['w_proj'], 'L0_attn_b_proj': _L0_attn_in['b_proj'], 'L0_attn_scale': _L0_attn_in['scale'], 'L0_attn_riem_scale': _L0_attn_in['riem_scale'], 'L0_attn_grassman_scale': _L0_attn_in['grassman_scale'], 'L0_attn_bn_gamma': _L0_attn_in['bn_gamma'], 'L0_attn_bn_beta': _L0_attn_in['bn_beta'], 'L0_attn_bn_mean': _L0_attn_in['bn_mean'], 'L0_attn_bn_var': _L0_attn_in['bn_var'], 'L0_attn_conv_w': _L0_attn_in['conv_w'], 'L0_attn_conv_b': _L0_attn_in['conv_b'], 'L0_ffn_W1': _L0_ffn_in['W1'], 'L0_ffn_b1': _L0_ffn_in['b1'], 'L0_ffn_Wg': _L0_ffn_in['Wg'], 'L0_ffn_bg': _L0_ffn_in['bg'], 'L0_ffn_Wd': _L0_ffn_in['Wd'], 'L0_ffn_bd': _L0_ffn_in['bd']}

def reference(x, L0_tok_kernel, L0_tok_bias, L0_tok_beta, L0_tok_moving_mean, L0_tok_moving_var, L0_attn_w_qkv, L0_attn_b_qkv, L0_attn_w_proj, L0_attn_b_proj, L0_attn_scale, L0_attn_riem_scale, L0_attn_grassman_scale, L0_attn_bn_gamma, L0_attn_bn_beta, L0_attn_bn_mean, L0_attn_bn_var, L0_attn_conv_w, L0_attn_conv_b, L0_ffn_W1, L0_ffn_b1, L0_ffn_Wg, L0_ffn_bg, L0_ffn_Wd, L0_ffn_bd):
    import jax
    import jax.numpy as jnp

    def _L0_tok_ref(x, kernel, bias, beta, moving_mean, moving_var):
        import jax, jax.numpy as jnp
        from jax import lax
        import numpy as np
        BN_EPS = 0.001

        @jax.custom_vjp
        def ste_sign(x):
            return jnp.where(x >= 0, 1.0, -1.0).astype(x.dtype)

        def _ste_fwd(x):
            return (ste_sign(x), x)

        def _ste_bwd(x, g):
            return (g * (jnp.abs(x) <= 1.0).astype(g.dtype),)
        ste_sign.defvjp(_ste_fwd, _ste_bwd)
        xq = ste_sign(x)
        kq = ste_sign(kernel)
        y = lax.conv_general_dilated(xq, kq, window_strides=(1,), padding='VALID', dimension_numbers=('NWC', 'WIO', 'NWC'))
        y = y + bias
        inv = lax.rsqrt(moving_var + BN_EPS)
        return (y - moving_mean) * inv + beta

    def _L0_attn_ref(x, w_qkv, b_qkv, w_proj, b_proj, scale, riem_scale, grassman_scale, bn_gamma, bn_beta, bn_mean, bn_var, conv_w, conv_b):
        import jax, jax.numpy as jnp
        import numpy as np
        B, N, C, H = (4, 256, 64, 8)
        HD = C // H
        BN_EPS = 1e-05
        b, n, c = x.shape
        h, hd = (H, c // H)
        qkv = (x @ w_qkv.T + b_qkv).reshape(b, n, 3, h, hd).transpose(2, 0, 3, 1, 4)
        q, k, v = (qkv[0], qkv[1], qkv[2])
        qgr, _ = jnp.linalg.qr(q)
        kgr, _ = jnp.linalg.qr(k)
        attn_grass = jnp.einsum('bhnd,bhmd->bhnm', qgr, kgr) ** 2 * grassman_scale
        dots = jnp.einsum('bhnd,bhmd->bhnm', q, k)
        attn_eucl = dots * scale
        attn_riem = dots ** 2 * riem_scale
        a = jnp.concatenate([attn_eucl, attn_riem, attn_grass], axis=1)
        inv = (bn_gamma * jax.lax.rsqrt(bn_var + BN_EPS))[:, None, None]
        a = (a - bn_mean[:, None, None]) * inv + bn_beta[:, None, None]
        a = jnp.einsum('oc,bcnm->bonm', conv_w, a) + conv_b[None, :, None, None]
        a = jax.nn.softmax(a, axis=-1)
        out = jnp.einsum('bhnm,bhmd->bhnd', a, v)
        out = out.transpose(0, 2, 1, 3).reshape(b, n, c)
        return out @ w_proj.T + b_proj

    def _L0_ffn_ref(x, W1, b1, Wg, bg, Wd, bd):
        import jax, jax.numpy as jnp
        import numpy as np
        C = 64
        HID = 256
        E = 8
        TEMP = 1.0
        orig_shape = x.shape
        xf = x.reshape(-1, orig_shape[-1])
        H = jax.nn.gelu(xf @ W1 + b1, approximate=False)
        probs = jax.nn.softmax((H @ Wg + bg) / TEMP, axis=-1)
        assign = jnp.argmax(probs, axis=-1)
        out = jnp.zeros_like(xf)
        for e in range(Wd.shape[0]):
            y = H @ Wd[e] + bd[e]
            sel = (assign == e)[:, None]
            out = out + jnp.where(sel, probs[:, e:e + 1] * y, 0.0)
        return out.reshape(orig_shape)
    h = _L0_tok_ref(x, L0_tok_kernel, L0_tok_bias, L0_tok_beta, L0_tok_moving_mean, L0_tok_moving_var)
    h = h + _L0_attn_ref(_layernorm(h, axis=-1), L0_attn_w_qkv, L0_attn_b_qkv, L0_attn_w_proj, L0_attn_b_proj, L0_attn_scale, L0_attn_riem_scale, L0_attn_grassman_scale, L0_attn_bn_gamma, L0_attn_bn_beta, L0_attn_bn_mean, L0_attn_bn_var, L0_attn_conv_w, L0_attn_conv_b)
    h = h + _L0_ffn_ref(_layernorm(h, axis=-1), L0_ffn_W1, L0_ffn_b1, L0_ffn_Wg, L0_ffn_bg, L0_ffn_Wd, L0_ffn_bd)
    return h

_drawn_inputs = setup_inputs


def setup_inputs(seed=0):
    import zlib

    import numpy as np

    out = dict(_drawn_inputs(seed))
    spreads = {'L0_attn_b_qkv': (0.0, 0.8),
     'L0_attn_b_proj': (0.0, 0.8),
     'L0_attn_bn_gamma': (1.0, 0.6),
     'L0_attn_bn_beta': (0.0, 2.0),
     'L0_attn_bn_mean': (0.0, 2.0),
     'L0_attn_bn_var': (1.0, 0.6),
     'L0_attn_conv_b': (0.0, 2.0),
     'L0_ffn_b1': (0.0, 0.8),
     'L0_ffn_bg': (0.0, 0.8),
     'L0_ffn_bd': (0.0, 2.0)}
    factors = {'L0_tok_bias': 64.0,
     'L0_tok_beta': 62.977,
     'L0_tok_moving_mean': 8.0,
     'L0_attn_w_qkv': 8.0,
     'L0_attn_w_proj': 8.0,
     'L0_attn_conv_w': 8.0,
     'L0_ffn_W1': 8.0,
     'L0_ffn_Wg': 8.0,
     'L0_ffn_Wd': 8.0}
    for name, (base, spread) in spreads.items():
        noise = np.random.default_rng([zlib.crc32(name.encode()), seed]).standard_normal(out[name].shape)
        drawn = base * np.exp(spread * noise) if base else spread * noise
        out[name] = jnp.asarray(drawn.astype(out[name].dtype))
    for name, factor in factors.items():
        out[name] = (out[name] * factor).astype(out[name].dtype)
    return out
```

```python
from contextlib import ExitStack

import numpy as np

import concourse.bass as bass
from concourse import mybir

F32 = mybir.dt.float32
BF16 = mybir.dt.bfloat16
ALU = mybir.AluOpType
ACT = mybir.ActivationFunctionType
AX = mybir.AxisListType

H, D = 8, 8
C = H * D
CIN = 128
TAPS = 3
TIN = 250
N = TIN - TAPS + 1
NT = N // 2
XT = TIN // 2
PW = 2 * N
E = 8
HID = 256
FT = 3
OG = 4
VW = 32
BN_EPS, TOK_EPS, LN_EPS = 1e-5, 1e-3, 1e-5

W_Q, W_K, W_QK, W_V, W_P, W_1, W_END = 0, 384, 768, 896, 960, 1024, 1280


def audio_tower(nc, x, w65, kconv, chan, wall, wbias, mixw, mixbn, cw, cbn, consts, out):
    B = x.shape[0]
    NP = B // 2
    NG = B // 4
    G16 = B // 16
    NTILE = 2 * B

    with ExitStack() as ctx:
        def sb(name, shape, dt=F32, stack=ctx):
            return stack.enter_context(nc.sbuf_tensor(name, shape, dt))

        def sem(name):
            return ctx.enter_context(nc.semaphore(name))

        zt_dram = nc.dram_tensor("zt_scratch", (NP, C, PW), F32, kind="Internal").ap()
        gram_dram = nc.dram_tensor("gram_scratch", (H, B, 2, D, D), F32, kind="Internal").ap()
        top_dram = nc.dram_tensor("top_scratch", (H, B, 2, D, D), F32, kind="Internal").ap()
        m_dram = nc.dram_tensor("m_scratch", (H, B, D, D), F32, kind="Internal").ap()

        ps = ctx.enter_context(nc.psum_tensor("ps", [128, 8, 512], F32))

        h_all = sb("h_all", [NT, NTILE, C])
        w = sb("w", [C + 1, W_END])
        ident = sb("ident", [128, 128])
        mask = sb("mask", [128, 16])
        eye8 = sb("eye8", [128, 64])
        mix = sb("mix", [128, 2, FT, H])
        shift_o = sb("shift_o", [NT, H])
        mc12 = sb("mc12", [C, B, 12])
        pri = sb("pri", [NT, E])
        wl = sb("wl", [128, 2, E + E * C])
        wb3 = sb("wb3", [128, E + E * C], BF16)
        ones3 = sb("ones3", [128, NT], BF16)

        with ExitStack() as st:
            chan_sb = sb("chan_sb", [NT, 4, C], stack=st)
            aff = sb("aff", [NT, 3, C], stack=st)
            kc = sb("kc", [CIN, TAPS * C], stack=st)
            kq = sb("kq", [CIN, TAPS * C], BF16, stack=st)
            mw = sb("mw", [128, 2, FT, H], stack=st)
            mbn = sb("mbn", [128, 4, 2 * FT], stack=st)
            minv = sb("minv", [128, 2 * FT], stack=st)
            cw_sb = sb("cw_sb", [NT, H, 25], stack=st)
            cbn_sb = sb("cbn_sb", [NT, 4, 24], stack=st)
            cinv = sb("cinv", [NT, 24], stack=st)
            wb_f = sb("wb_f", [1, 3, E + E * C], stack=st)
            wb_b = sb("wb_b", [1, 3, E + E * C], BF16, stack=st)
            xt = sb("xt", [XT, 2, 8, CIN], stack=st)
            xs = sb("xs", [CIN, 2, 500], BF16, stack=st)
            ysc = sb("ysc", [NT, 8, C], stack=st)
            hg = sb("hg", [NT, 8, C], stack=st)
            stat = sb("stat", [NT, 4, 8], stack=st)
            zc = sb("zc", [NT, 8, C], stack=st)
            zsq = sb("zsq", [NT, 8, C], stack=st)
            z = sb("z", [NT, 2, 8, C], stack=st)
            zt = sb("zt", [C + 1, 2, 8 * NT], stack=st)
            qkt = sb("qkt", [NT, 8, 128], stack=st)
            gm = sb("gm", [128, 4, 16, D], stack=st)
            gram = sb("gram", [128, B, D], stack=st)
            top = sb("top", [D, B, 128], stack=st)

            loaded, small_loaded = sem("loaded"), sem("small_loaded")
            a_vec, a_sqrt, a_ones = sem("a_vec"), sem("a_sqrt"), sem("a_ones")
            wb_moved = sem("wb_moved")
            x_in = [sem("x_in_even"), sem("x_in_odd")]
            xT_ready, xs_ready, y_ready = sem("xT_ready"), sem("xs_ready"), sem("y_ready")
            h_ready, zc_ready, zsq_ready = sem("h_ready"), sem("zc_ready"), sem("zsq_ready")
            var_ready, std_ready, z_ready = sem("var_ready"), sem("std_ready"), sem("z_ready")
            zT_ready, zt_ready = sem("zT_ready"), sem("zt_ready")
            zt_out = [sem("zt_out_even"), sem("zt_out_odd")]
            qk_ready, qkt_ready, gram_ready = sem("qk_ready"), sem("qkt_ready"), sem("gram_ready")
            gm_masked = sem("gm_masked")
            h_kept = sem("h_kept")
            ln_step, ln_rstd = sem("ln_step"), sem("ln_rstd")
            gm_ready, top_ready, gram_out = sem("gm_ready"), sem("top_ready"), sem("gram_out")

            def skewed(eng, front, back):
                front(0, 0)
                front(1, 1)
                back(0, 0)
                front(2, 0)
                back(1, 1)
                if NG > 4:
                    with eng.Fori(0, NG // 2 - 2) as i:
                        front(2 * i + 3, 1)
                        back(2 * i + 2, 0)
                        front(2 * i + 4, 0)
                        back(2 * i + 3, 1)
                front(NG - 1, 1)
                back(NG - 2, 0)
                back(NG - 1, 1)

            SETUP = 26

            with nc.Block() as block:
                @block.sync
                def _(sp):
                    for dst, src in ((w[:], w65), (kc[:], kconv), (chan_sb[:], chan[0:NT]), (mw[:], mixw),
                                     (mbn[:], mixbn), (cw_sb[:], cw[0:NT]), (cbn_sb[:], cbn[0:NT]),
                                     (ident[:], consts[:, 0:128]), (mask[:], consts[:, 128:144]),
                                     (eye8[:], consts[:, 144:208]), (pri[:], consts[0:NT, 208:216]),
                                     (wl[:], wall), (wb_f[:, 0, :], wbias)):
                        sp.dma_start(dst, src).then_inc(small_loaded, 16)

                    def load_x(g, par):
                        src = x[bass.ds(4 * g, 4)].rearrange("b (t p) c -> p (b t) c", p=XT)
                        sp.dma_start(xt[:, par], src).then_inc(x_in[par], 16)

                    def store_zt(g, par):
                        sp.wait_ge(zt_ready, 2 * g + 2)
                        for k in range(2):
                            sp.dma_start(zt_dram[bass.ds(2 * g + k, 1)].rearrange("a c n -> (a c) n"),
                                         zt[0:C, par, k * PW:(k + 1) * PW]).then_inc(zt_out[par], 16)

                    load_x(0, 0)
                    load_x(1, 1)
                    if NG > 2:
                        with sp.Fori(0, NG // 2 - 1) as i:
                            for par in range(2):
                                sp.wait_ge(xT_ready, 4 * i + 2 * par + 2)
                                load_x(2 * i + 2 + par, par)
                                store_zt(2 * i + par, par)
                    store_zt(NG - 2, 0)
                    store_zt(NG - 1, 1)
                    sp.wait_ge(a_vec, SETUP)
                    sp.wait_ge(a_ones, 3)
                    for k in range(3):
                        sp.dma_start(wb3[k:k + 1, :], wb_b[:, k, :]).then_inc(wb_moved, 16)
                    sp.wait_ge(gm_ready, NG)
                    sp.wait_ge(top_ready, NG)
                    for qk in range(2):
                        for h in range(H):
                            r = (qk * H + h) * D
                            sp.dma_start(gram_dram[h, :, qk].rearrange("b i j -> i b j"),
                                         gram[r:r + D, :, :]).then_inc(gram_out, 16)
                            sp.dma_start(top_dram[h, :, qk].rearrange("b i j -> i b j"),
                                         top[:, :, r:r + D]).then_inc(gram_out, 16)
                    sp.wait_ge(wb_moved, 48)
                    sp.wait_ge(zt_out[0], 16 * NG)
                    sp.wait_ge(zt_out[1], 16 * NG)
                    sp.wait_ge(gram_out, 2 * 16 * 2 * H)

                @block.tensor
                def _(pe):
                    pe.wait_ge(small_loaded, 16 * 13)

                    def front(g, par):
                        pe.wait_ge(x_in[par], 8 * g + 16 - 8 * par)
                        pe.wait_ge(xs_ready, 2 * g)
                        for k in range(8):
                            mm = pe.transpose(ps[:, k // 4, (k % 4) * XT:(k % 4 + 1) * XT], xt[:, par, k, :],
                                              ident[0:XT, 0:XT])
                            if k % 4 == 3:
                                mm.then_inc(xT_ready, 1)
                        pe.wait_ge(xs_ready, 2 * g + 2)
                        pe.wait_ge(h_ready, g)
                        for k in range(8):
                            for tap in range(TAPS):
                                at = (k // 2 % 2) * TIN + (k % 2) * NT + tap
                                mm = pe.matmul(ps[0:NT, 2, k * C:(k + 1) * C], xs[:, k // 4, at:at + NT],
                                               kq[:, tap * C:(tap + 1) * C], start=tap == 0, stop=tap == TAPS - 1)
                        mm.then_inc(y_ready, 1)

                    def back(g, par):
                        pe.wait_ge(z_ready, g + 1)
                        pe.wait_ge(zt_ready, 2 * g)
                        for k in range(4):
                            mm = pe.transpose(ps[:, 3, k * NT:(k + 1) * NT],
                                              z[:, par, 2 * k:2 * k + 2, :].rearrange("p t c -> p (t c)"), ident[0:NT, 0:NT])
                        mm.then_inc(zT_ready, 1)
                        pe.wait_ge(zt_ready, 2 * g + 2)
                        pe.wait_ge(qkt_ready, 2 * g)
                        for k in range(8):
                            mm = pe.matmul(ps[0:NT, 5 + k // 4, (k % 4) * 128:(k % 4 + 1) * 128],
                                           zt[:, par, k * NT:(k + 1) * NT], w[:, W_QK:W_QK + 128],
                                           start=True, stop=True)
                        mm.then_inc(qk_ready, 1)
                        pe.wait_ge(qkt_ready, 2 * g + 2)
                        pe.wait_ge(gm_ready, g)
                        for b in range(4):
                            for t in range(2):
                                mm = pe.matmul(ps[:, 7, b * 128:(b + 1) * 128], qkt[:, 2 * b + t, :],
                                               qkt[:, 2 * b + t, :], start=t == 0, stop=t == 1)
                        mm.then_inc(gram_ready, 1)

                    pe.wait_ge(a_vec, SETUP)
                    pe.wait_ge(a_ones, 3)
                    skewed(pe, front, back)

                @block.scalar
                def _(act):
                    act.wait_ge(small_loaded, 16 * 13)
                    act.wait_ge(a_vec, 4)
                    nc.scalar.activation(aff[:, 0, :], chan_sb[:, 3, :], ACT.Sqrt).then_inc(a_sqrt, 1)
                    nc.scalar.activation(minv[:], mbn[:, 1, :], ACT.Sqrt).then_inc(a_sqrt, 1)
                    nc.scalar.activation(cinv[:], cbn_sb[:, 1, :], ACT.Sqrt).then_inc(a_sqrt, 1)

                    def front(g, par):
                        act.wait_ge(var_ready, g + 1)
                        nc.scalar.activation(stat[:, 2, :], stat[:, 1, :], ACT.Sqrt, scale=1.0).then_inc(std_ready, 1)

                    def back(g, par):
                        act.wait_ge(zT_ready, g + 1)
                        if not (isinstance(g, int) and g < 2):
                            act.wait_ge(zt_out[par], 16 * g - 16 * par)
                        for k in range(2):
                            nc.scalar.copy(zt[0:C, par].rearrange("c (t k n) -> c t k n", k=2, n=NT)[:, :, k, :],
                                           ps[k * C:(k + 1) * C, 3, 0:PW].rearrange("c (t n) -> c t n", n=NT)
                                           ).then_inc(zt_ready, 1)
                        act.wait_ge(qk_ready, g + 1)
                        act.wait_ge(gram_ready, g)
                        act.wait_ge(top_ready, g)
                        for k in range(2):
                            nc.scalar.copy(qkt[:, 4 * k:4 * k + 4, :],
                                           ps[0:NT, 5 + k, :].rearrange("p (t c) -> p t c", c=128)).then_inc(qkt_ready, 1)

                    skewed(act, front, back)

                @block.gpsimd
                def _(pool):
                    nc.gpsimd.memset(wb3[:], 0.0).then_inc(a_ones, 1)
                    nc.gpsimd.memset(ones3[:], 0.0).then_inc(a_ones, 1)
                    pool.wait_ge(a_ones, 2)
                    nc.gpsimd.memset(ones3[0:3, :], 1.0).then_inc(a_ones, 1)

                    def front(g, par):
                        pool.wait_ge(ln_step, 4 * g + 1)
                        nc.gpsimd.tensor_copy(h_all[:, bass.ds(8 * g, 8), :], hg[:]).then_inc(h_kept, 1)
                        pool.wait_ge(zc_ready, g + 1)
                        nc.gpsimd.tensor_tensor(zsq[:], zc[:], zc[:], ALU.mult).then_inc(zsq_ready, 1)

                    def back(g, par):
                        pool.wait_ge(qkt_ready, 2 * g + 2)
                        nc.gpsimd.tensor_copy(top[:, bass.ds(4 * g, 4), :],
                                              qkt[0:D, 0:8:2, :]).then_inc(top_ready, 1)

                    skewed(pool, front, back)

                @block.vector
                def _(dve):
                    steps = [0]

                    def link(ins):
                        steps[0] += 1
                        ins.then_inc(a_vec, 1)
                        dve.wait_ge(a_vec, steps[0])

                    nv = nc.vector
                    link(nv.memset(zt[C:C + 1, :, :], 1.0))
                    dve.wait_ge(small_loaded, 16 * 13)
                    link(nv.tensor_scalar(chan_sb[:, 3, :], chan_sb[:, 3, :], TOK_EPS, None, ALU.add))
                    link(nv.tensor_scalar(mbn[:, 1, :], mbn[:, 1, :], BN_EPS, None, ALU.add))
                    link(nv.tensor_scalar(cbn_sb[:, 1, :], cbn_sb[:, 1, :], BN_EPS, None, ALU.add))
                    link(nv.tensor_scalar(kc[:], kc[:], 0.0, 0.5, ALU.is_ge, ALU.subtract))
                    link(nv.tensor_scalar(kq[:], kc[:], 4.0, None, ALU.mult))
                    dve.wait_ge(a_sqrt, 3)
                    link(nv.reciprocal(aff[:, 1, :], aff[:, 0, :]))
                    link(nv.tensor_tensor(aff[:, 2, :], chan_sb[:, 0, :], chan_sb[:, 2, :], ALU.subtract))
                    link(nv.tensor_tensor(aff[:, 2, :], aff[:, 2, :], aff[:, 1, :], ALU.mult))
                    link(nv.tensor_tensor(aff[:, 2, :], aff[:, 2, :], chan_sb[:, 1, :], ALU.add))
                    link(nv.reciprocal(minv[:], minv[:]))
                    for j in (0, 2, 3):
                        link(nv.tensor_tensor(minv[:], minv[:], mbn[:, j, :], ALU.mult))
                    mi = minv[:].rearrange("p (a t) -> p a t", a=2).unsqueeze(3).broadcast_to([128, 2, FT, H])
                    link(nv.tensor_tensor(mix[:], mw[:], mi, ALU.mult))
                    link(nv.reciprocal(cinv[:], cinv[:]))
                    link(nv.tensor_tensor(cinv[:], cinv[:], cbn_sb[:, 0, :], ALU.mult))
                    link(nv.tensor_tensor(cinv[:], cinv[:], cbn_sb[:, 2, :], ALU.mult))
                    link(nv.tensor_tensor(cinv[:], cbn_sb[:, 3, :], cinv[:], ALU.subtract))
                    link(nv.tensor_tensor(cw_sb[:, :, 0:24], cw_sb[:, :, 0:24],
                                          cinv[:].unsqueeze(1).broadcast_to([NT, H, 24]), ALU.mult))
                    link(nv.tensor_reduce(shift_o[:], cw_sb[:], AX.X, ALU.add))
                    link(nv.tensor_copy(wb_b[:, 0, :], wb_f[:, 0, :]))
                    link(nv.tensor_tensor(wb_f[:, 1, :], wb_f[:, 0, :], wb_b[:, 0, :], ALU.subtract))
                    link(nv.tensor_copy(wb_b[:, 1, :], wb_f[:, 1, :]))
                    link(nv.tensor_tensor(wb_f[:, 2, :], wb_f[:, 1, :], wb_b[:, 1, :], ALU.subtract))
                    link(nv.tensor_copy(wb_b[:, 2, :], wb_f[:, 2, :]))
                    assert steps[0] == SETUP, steps[0]

                    def row(ap):
                        return ap.unsqueeze(1).broadcast_to([NT, 8, C])

                    def col(ap):
                        return ap.unsqueeze(2).broadcast_to([NT, 8, C])

                    def front(g, par):
                        for k in range(2):
                            dve.wait_ge(xT_ready, 2 * g + 1 + k)
                            if k == 0:
                                dve.wait_ge(y_ready, g)
                            nv.tensor_scalar(xs[:, k, :], ps[:, k, 0:500], 0.0, 0.5, ALU.is_ge,
                                             ALU.subtract).then_inc(xs_ready, 1)
                        dve.wait_ge(y_ready, g + 1)
                        yv = ps[0:NT, 2, :].rearrange("p (t c) -> p t c", c=C)
                        dve.wait_ge(h_kept, g)
                        nv.tensor_tensor(ysc[:], yv, row(aff[:, 1, :]), ALU.mult).then_inc(h_ready, 1)
                        dve.wait_ge(h_ready, g + 1)
                        ht = hg[:]
                        nv.tensor_tensor(ht, ysc[:], row(aff[:, 2, :]), ALU.add).then_inc(ln_step, 1)
                        dve.wait_ge(ln_step, 4 * g + 1)
                        nv.tensor_reduce(stat[:, 0, :], ht, AX.X, ALU.add).then_inc(ln_step, 1)
                        dve.wait_ge(ln_step, 4 * g + 2)
                        nv.tensor_scalar(stat[:, 0, :], stat[:, 0, :], -1.0 / C, None, ALU.mult).then_inc(ln_step, 1)
                        dve.wait_ge(ln_step, 4 * g + 3)
                        nv.tensor_tensor(zc[:], ht, col(stat[:, 0, :]), ALU.add).then_inc(zc_ready, 1)
                        dve.wait_ge(zsq_ready, g + 1)
                        nv.tensor_reduce(stat[:, 3, :], zsq[:], AX.X, ALU.add).then_inc(ln_step, 1)
                        dve.wait_ge(ln_step, 4 * g + 4)
                        nv.tensor_scalar(stat[:, 1, :], stat[:, 3, :], 1.0 / C, LN_EPS, ALU.mult,
                                         ALU.add).then_inc(var_ready, 1)
                        dve.wait_ge(std_ready, g + 1)
                        nv.reciprocal(stat[:, 2, :], stat[:, 2, :]).then_inc(ln_rstd, 1)
                        dve.wait_ge(ln_rstd, g + 1)
                        if not (isinstance(g, int) and g < 2):
                            dve.wait_ge(zT_ready, g - 1)
                        nv.tensor_tensor(z[:, par], zc[:], col(stat[:, 2, :]), ALU.mult).then_inc(z_ready, 1)

                    def back(g, par):
                        dve.wait_ge(gram_ready, g + 1)
                        nv.tensor_tensor(gm[:], ps[:, 7, :].rearrange("p (b k j) -> p b k j", b=4, k=16),
                                         mask[:].unsqueeze(1).unsqueeze(3).broadcast_to([128, 4, 16, D]),
                                         ALU.mult).then_inc(gm_masked, 1)
                        dve.wait_ge(gm_masked, g + 1)
                        nv.tensor_reduce(gram[:, bass.ds(4 * g, 4), :], gm[:].rearrange("p b k j -> p b j k"),
                                         AX.X, ALU.add).then_inc(gm_ready, 1)

                    skewed(dve, front, back)

        with ExitStack() as st:
            GP = 2 * G16
            gw = sb("gw", [128, GP, D, 2 * D], stack=st)
            gl = sb("gl", [128, GP, D, D], stack=st)
            av = sb("av", [128, GP, D, D], stack=st)
            ri = sb("ri", [128, GP, D, D], stack=st)
            q8 = sb("q8", [128, GP, D, D], stack=st)
            tmp = sb("tmp", [128, GP, D, 2 * D], stack=st)
            fac = sb("fac", [128, GP, D], stack=st)
            piv = sb("piv", [128, GP, D], stack=st)
            rs = sb("rs", [128, GP, D], stack=st)
            sg = sb("sg", [128, GP, D], stack=st)
            ss = sb("ss", [128, G16, D], stack=st)
            mm_ = sb("mm_", [128, G16, D, D], stack=st)
            mt = sb("mt", [128, G16, D, D], stack=st)
            b_in, b_step, b_sqrt = sem("b_in"), sem("b_step"), sem("b_sqrt")
            m_out, m_in, m_wrap = sem("m_out"), sem("m_in"), sem("m_wrap")
            B_PIVOTS, B_STEPS = [0], [0]

            with nc.Block() as block:
                @block.vector
                def _(dve):
                    nv = nc.vector
                    steps = [0]

                    def link(ins):
                        steps[0] += 1
                        ins.then_inc(b_step, 1)
                        dve.wait_ge(b_step, steps[0])

                    dve.wait_ge(b_in, 16 * 2 * H)
                    link(nv.tensor_copy(gw[:, :, :, 0:D], gl[:]))
                    link(nv.tensor_copy(gw[:, :, :, D:], eye8[:].rearrange("p (i j) -> p i j", i=D)
                                        .unsqueeze(1).broadcast_to([128, GP, D, D])))
                    for d in range(D - 1):
                        n = D - 1 - d
                        link(nv.reciprocal(piv[:, :, d:d + 1], gw[:, :, d, d:d + 1]))
                        link(nv.tensor_tensor(fac[:, :, 0:n], gw[:, :, d + 1:, d],
                                              piv[:, :, d:d + 1].broadcast_to([128, GP, n]), ALU.mult))
                        link(nv.tensor_tensor(tmp[:, :, 0:n, :],
                                              fac[:, :, 0:n].unsqueeze(3).broadcast_to([128, GP, n, 2 * D]),
                                              gw[:, :, d:d + 1, :].broadcast_to([128, GP, n, 2 * D]), ALU.mult))
                        link(nv.tensor_tensor(gw[:, :, d + 1:, :], gw[:, :, d + 1:, :], tmp[:, :, 0:n, :],
                                              ALU.subtract))
                    link(nv.tensor_copy(piv[:], gw[:].rearrange("p g i j -> p g (i j)")[:, :, 0:128:17]))
                    B_PIVOTS[0] = steps[0]
                    dve.wait_ge(b_sqrt, 1)
                    link(nv.reciprocal(rs[:], rs[:]))
                    link(nv.tensor_tensor(sg[:], rs[:], rs[:], ALU.mult))
                    link(nv.tensor_tensor(sg[:], sg[:], piv[:], ALU.mult))
                    link(nv.tensor_scalar(sg[:], sg[:], -0.5, 1.5, ALU.mult, ALU.add))
                    link(nv.tensor_tensor(rs[:], rs[:], sg[:], ALU.mult))
                    link(nv.tensor_tensor(ri[:], gw[:, :, :, D:].rearrange("p g j i -> p g i j"),
                                          rs[:].unsqueeze(2).broadcast_to([128, GP, D, D]), ALU.mult))

                    def product(dst, part, left, right, G):
                        for i in range(D):
                            into = dst if i == 0 else part
                            link(nv.tensor_tensor(into, left(i).unsqueeze(3).broadcast_to([128, G, D, D]),
                                                  right(i).unsqueeze(2).broadcast_to([128, G, D, D]), ALU.mult))
                            if i:
                                link(nv.tensor_tensor(dst, dst, part, ALU.add))

                    product(q8[:], tmp[:, :, :, 0:D], lambda i: av[:, :, :, i], lambda i: ri[:, :, i, :], GP)
                    for d in range(D):
                        n = D - 1 - d
                        pivot = q8[:, :, d, d:d + 1]
                        link(nv.tensor_scalar(sg[:, :, d:d + 1], pivot, 0.0, 2.0, ALU.is_lt, ALU.mult))
                        link(nv.tensor_scalar(sg[:, :, d:d + 1], sg[:, :, d:d + 1], -1.0, None, ALU.add))
                        if not n:
                            break
                        link(nv.tensor_tensor(fac[:, :, 7:8], pivot, sg[:, :, d:d + 1], ALU.subtract))
                        link(nv.reciprocal(fac[:, :, 7:8], fac[:, :, 7:8]))
                        link(nv.tensor_tensor(fac[:, :, 0:n], q8[:, :, d + 1:, d],
                                              fac[:, :, 7:8].broadcast_to([128, GP, n]), ALU.mult))
                        link(nv.tensor_tensor(tmp[:, :, 0:n, 0:n],
                                              fac[:, :, 0:n].unsqueeze(3).broadcast_to([128, GP, n, n]),
                                              q8[:, :, d:d + 1, d + 1:].broadcast_to([128, GP, n, n]), ALU.mult))
                        link(nv.tensor_tensor(q8[:, :, d + 1:, d + 1:], q8[:, :, d + 1:, d + 1:],
                                              tmp[:, :, 0:n, 0:n], ALU.subtract))
                    link(nv.tensor_tensor(ss[:], sg[:, 0::2, :], sg[:, 1::2, :], ALU.mult))
                    link(nv.tensor_tensor(mt[:], ri[:, 0::2, :, :],
                                          ss[:].unsqueeze(2).broadcast_to([128, G16, D, D]), ALU.mult))
                    product(mm_[:], tmp[:, 0:G16, :, 0:D], lambda i: mt[:, :, :, i],
                            lambda i: ri[:, 1::2, :, i], G16)
                    B_STEPS[0] = steps[0]
                    dve.wait_ge(m_in, 16 * H)
                    nv.tensor_copy(mc12[:, :, D:12], mc12[:, :, 0:4]).then_inc(m_wrap, 1)

                @block.scalar
                def _(act):
                    act.wait_ge(b_step, B_PIVOTS[0])
                    nc.scalar.activation(rs[:], piv[:], ACT.Sqrt).then_inc(b_sqrt, 1)

                @block.sync
                def _(sp):
                    for h in range(H):
                        for dst, src in ((gl, gram_dram), (av, top_dram)):
                            sp.dma_start(dst[16 * h:16 * h + 16].rearrange("p (g k) i j -> p g (k i j)", k=2),
                                         src[h].rearrange("(g b) k i j -> b g (k i j)", b=16)).then_inc(b_in, 16)
                    sp.wait_ge(b_step, B_STEPS[0])
                    for h in range(H):
                        sp.dma_start(m_dram[h].rearrange("(g b) i j -> b g (i j)", b=16),
                                     mm_[16 * h:16 * h + 16].rearrange("p g i j -> p g (i j)")).then_inc(m_out, 16)
                    sp.wait_ge(m_out, 16 * H)
                    for h in range(H):
                        sp.dma_start(mc12[D * h:D * h + D, :, 0:D],
                                     m_dram[h].rearrange("b i j -> i b j")).then_inc(m_in, 16)
                    sp.wait_ge(m_in, 16 * H)
                    sp.wait_ge(m_wrap, 1)

        FEATURES, FINISH = 10, 6
        O_BANK, SIDE = 6, 7
        FEATURE_AT = {0: (0, 1), 1: (2, 3), 2: (4, 5), 3: (6, 7), 4: (8, 9)}
        FINISH_AT = {5: (0, 1), 6: (2, 3), 7: (4, 5)}
        T_Q1, T_Q2, T_Q3, T_G1, T_G2, T_G3, T_K1, T_K2, T_K3, T_V = range(10)

        def task_base(p):
            if isinstance(p, int) and p == 0:
                return FEATURES
            return 2 * FEATURES + (FEATURES + FINISH) * (p - 1)

        def slot_tasks(p, s, first, last):
            found = []
            if s in FEATURE_AT and not last:
                for k in FEATURE_AT[s]:
                    found.append((task_base(p) + k, "feature", k))
            if s in FINISH_AT and not first:
                for k in FINISH_AT[s]:
                    found.append((task_base(p) + k + (0 if last else FEATURES), "finish", k))
            return found + [None] * (2 - len(found))

        def pairs(eng, prologue, slot, epilogue):
            prologue()
            for s in range(8):
                slot(0, 0, s, True, False)
            with eng.Fori(0, NP // 2 - 1) as i:
                for par, p in ((1, 2 * i + 1), (0, 2 * i + 2)):
                    for s in range(8):
                        slot(p, par, s, False, False)
            for s in range(8):
                slot(NP - 1, 1, s, False, True)
            epilogue()

        with ExitStack() as st:
            ztc = sb("ztc", [C + 1, 2, PW], stack=st)
            qa = sb("qa", [128, PW], stack=st)
            ga = sb("ga", [128, PW], stack=st)
            ka = sb("ka", [128, PW], stack=st)
            mb = sb("mb", [128, 2, 2, 6, C], stack=st)
            fq = sb("fq", [128, 2, FT, PW], stack=st)
            fg = sb("fg", [128, 2, FT, PW], stack=st)
            fk = sb("fk", [128, 2, FT, PW], stack=st)
            part = sb("part", [128, 3, PW], stack=st)
            F = sb("F", [128, 2, OG, FT, PW], stack=st)
            prob = sb("prob", [NT, 2, OG, N], stack=st)
            probT = sb("probT", [NT, 2, 2, OG, N], stack=st)
            nmax = sb("nmax", [NT, 2, OG], stack=st)
            nms = sb("nms", [NT, 2, OG], stack=st)
            ebias = sb("ebias", [NT, 2, OG], stack=st)
            vx = sb("vx", [NT, 2, 4, H, VW], stack=st)
            oT = sb("oT", [128, 2, 2, PW], stack=st)
            rden = sb("rden", [NT, 2 * H], stack=st)
            otok = sb("otok", [NT, 2, C], stack=st)
            oc = sb("oc", [C + 1, N], stack=st)

            filled, v_filled = sem("filled"), sem("v_filled")
            zt_in = [sem("zt_in_even"), sem("zt_in_odd")]
            side_ready, side_free = sem("side_ready"), sem("side_free")
            mb_ready, sq_ready = sem("mb_ready"), sem("sq_ready")
            part_ready, part_used = sem("part_ready"), sem("part_used")
            l_ready, nmax_ready, nms_ready, ebias_ready = sem("l_ready"), sem("nmax_ready"), sem("nms_ready"), sem("ebias_ready")
            exp_done, t_ready = sem("exp_done"), sem("t_ready")
            ptA_ready, ptD_ready = sem("ptA_ready"), sem("ptD_ready")
            o_ready, oT_ready, rden_ready = sem("o_ready"), sem("oT_ready"), sem("rden_ready")

            with nc.Block() as block:
                @block.sync
                def _(sp):
                    def load(q, par):
                        sp.dma_start(ztc[0:C, par], zt_dram[bass.ds(q, 1)].rearrange("a c n -> (a c) n")
                                     ).then_inc(zt_in[par], 16)

                    load(0, 0)
                    load(1, 1)
                    sp.wait_ge(side_ready, FEATURES)
                    load(2, 0)
                    sp.wait_ge(side_ready, 2 * FEATURES)
                    load(3, 1)
                    with sp.Fori(0, NP // 2 - 2) as i:
                        for par in range(2):
                            p = 2 * i + par + 1
                            sp.wait_ge(side_ready, 2 * FEATURES + (FEATURES + FINISH) * (p - 1) + FEATURES)
                            load(p + 3, par)

                @block.tensor
                def _(pe):
                    def feature(count, k, q, par):
                        if k == T_Q1:
                            pe.wait_ge(zt_in[par], 8 * q + 16 - 8 * par)
                        if k == T_G1:
                            pe.wait_ge(mb_ready, q + 1)
                            pe.wait_ge(filled, 3)
                        pe.wait_ge(side_free, count)
                        if k in (T_Q1, T_Q2, T_Q3, T_K1, T_K2, T_K3):
                            at = W_Q + 128 * (k - T_Q1) if k <= T_Q3 else W_K + 128 * (k - T_K1)
                            mm = pe.matmul(ps[:, SIDE, 0:PW], w[:, at:at + 128], ztc[:, par], start=True, stop=True)
                        elif k in (T_G1, T_G2, T_G3):
                            for b in range(2):
                                n = 2 * (k - T_G1)
                                lhs = mb[:, par, b, n:n + 2, :].rearrange("p s c -> p (s c)")
                                mm = pe.matmul(ps[:, SIDE, b * N:(b + 1) * N], lhs, qa[:, b * N:(b + 1) * N],
                                               start=True, stop=True)
                        else:
                            for t in range(4):
                                mm = pe.matmul(ps[0:NT, SIDE, t * C:(t + 1) * C], ztc[:, par, t * NT:(t + 1) * NT],
                                               w[:, W_V:W_V + C], start=True, stop=True)
                        mm.then_inc(side_ready, 1)

                    def finish(count, k, q, par):
                        b = k // 3
                        if k == 0:
                            pe.wait_ge(oT_ready, 2 * q + 2)
                        pe.wait_ge(side_free, count)
                        if k % 3 == 0:
                            for t in range(2):
                                for og in range(2):
                                    at = (2 * t + og) * 128
                                    mm = pe.transpose(ps[0:NT, SIDE, at:at + 128],
                                                      oT[:, par, og, b * N + t * NT:b * N + (t + 1) * NT], ident[:])
                        elif k % 3 == 1:
                            mm = pe.transpose(ps[:, SIDE, 0:NT], otok[:].rearrange("p t c -> p (t c)"), ident[0:NT, 0:NT])
                        else:
                            for t in range(2):
                                mm = pe.matmul(ps[0:NT, SIDE, t * C:(t + 1) * C], oc[:, t * NT:(t + 1) * NT],
                                               w[:, W_P:W_P + C], start=True, stop=True)
                        mm.then_inc(side_ready, 1)

                    def side(task, p, par):
                        if task:
                            count, kind, k = task
                            if kind == "feature":
                                feature(count, k, p + 1, 1 - par)
                            else:
                                finish(count, k, p - 1, 1 - par)

                    def scores(s, par, heads):
                        og, b, t = s // 4, s // 2 % 2, s % 2
                        for o in heads:
                            for ft in range(FT):
                                mm = pe.matmul(ps[0:NT, 2 * (s % 2) + o // 2, (o % 2) * N:(o % 2 + 1) * N],
                                               F[:, og, o, ft, b * N + t * NT:b * N + (t + 1) * NT],
                                               fk[:, par, ft, b * N:(b + 1) * N], start=ft == 0, stop=ft == FT - 1)
                        return mm

                    def turn(S, sp_):
                        pe.wait_ge(exp_done, S + 1)
                        pe.wait_ge(ptA_ready, S)
                        pe.wait_ge(ptD_ready, S)
                        for mt in range(2):
                            for o in range(OG):
                                mm = pe.transpose(ps[0:NT, 4 + mt, o * NT:(o + 1) * NT],
                                                  prob[:, sp_, o, mt * NT:(mt + 1) * NT], ident[0:NT, 0:NT])
                        mm.then_inc(t_ready, 1)

                    def values(U, S, og, b, par):
                        pe.wait_ge(ptA_ready, S + 1)
                        pe.wait_ge(ptD_ready, S + 1)
                        if b == 0:
                            pe.wait_ge(oT_ready, U)
                        for mt in range(2):
                            for j in range(OG):
                                mm = pe.matmul(ps[32 * j:32 * j + VW, O_BANK, b * N:(b + 1) * N],
                                               vx[:, par, 2 * b + mt, OG * og + j, :], probT[:, b, mt, j, :],
                                               start=mt == 0, stop=mt == 1)
                        if b == 1:
                            mm.then_inc(o_ready, 1)

                    def slot(p, par, s, first, last):
                        S = 8 * p + s
                        tasks = slot_tasks(p, s, first, last)
                        if s % 4 == 0:
                            pe.wait_ge(part_used, 12 * (2 * p + s // 4 + 1))
                        if s == 0:
                            pe.wait_ge(sq_ready, 3 * p + 3)
                        if not (first and s < 2):
                            pe.wait_ge(exp_done, S - 1)
                        scores(s, par, (0, 1))
                        side(tasks[0], p, par)
                        scores(s, par, (2, 3)).then_inc(l_ready, 1)
                        if not (first and s == 0):
                            turn(S - 1, (s - 1) % 2)
                        side(tasks[1], p, par)
                        if s == 1 and not first:
                            values(2 * p - 1, S - 2, 1, 1, 1 - par)
                        if s == 3:
                            values(2 * p, S - 2, 0, 0, par)
                        if s == 5:
                            values(2 * p, S - 2, 0, 1, par)
                        if s == 7:
                            values(2 * p + 1, S - 2, 1, 0, par)

                    def prologue():
                        pe.wait_ge(filled, 2)
                        for k in range(FEATURES):
                            feature(k, k, 0, 0)

                    def epilogue():
                        turn(8 * NP - 1, 1)
                        values(2 * NP - 1, 8 * NP - 1, 1, 1, 1)
                        for k in range(FINISH):
                            finish(task_base(NP - 1) + FINISH + k, k, NP - 1, 1)

                    pairs(pe, prologue, slot, epilogue)

                @block.scalar
                def _(act):
                    def mixed(n, og, o, ft, par):
                        if not (isinstance(n, int) and n < 3):
                            act.wait_ge(part_used, n - 2)
                        nc.scalar.activation(part[:, ft], fq[:, par, ft, :], ACT.Copy,
                                             scale=mix[:, 0, ft, OG * og + o:OG * og + o + 1]).then_inc(part_ready, 1)

                    def feature(count, k, q, par):
                        if k in (T_Q1, T_K1, T_G1):
                            act.wait_ge(side_ready, count + 1)
                            if k != T_G1:
                                nc.scalar.copy((fq if k == T_Q1 else fk)[C:, par, 2, :], ps[C:, SIDE, 0:PW])
                            nc.scalar.copy({T_Q1: qa, T_K1: ka, T_G1: ga}[k][:], ps[:, SIDE, 0:PW]).then_inc(side_free, 1)
                        if k == T_V:
                            act.wait_ge(side_ready, count + 1)
                            nc.scalar.copy(vx[:, par, :, :, 0:D],
                                           ps[0:NT, SIDE, 0:4 * C].rearrange("p (t h d) -> p t h d", t=4, h=H)
                                           ).then_inc(side_free, 1)

                    def finish(count, k, q, par):
                        if k % 3 == 1:
                            act.wait_ge(side_ready, count + 1)
                            nc.scalar.copy(oc[0:C, 0:NT], ps[0:C, SIDE, 0:NT])
                            nc.scalar.copy(oc[0:C, NT:N], ps[C:, SIDE, 0:NT]).then_inc(side_free, 1)

                    def side(task, p, par):
                        if task:
                            count, kind, k = task
                            (feature if kind == "feature" else finish)(count, k, p + 1 if kind == "feature" else p - 1, 1 - par)

                    def exps(S, sp_):
                        act.wait_ge(ebias_ready, S + 1)
                        for o in range(OG):
                            ins = nc.scalar.activation(prob[:, sp_, o, :],
                                                       ps[0:NT, 2 * sp_ + o // 2, (o % 2) * N:(o % 2 + 1) * N],
                                                       ACT.Exp, bias=ebias[:, sp_, o:o + 1])
                        ins.then_inc(exp_done, 1)

                    def copy_turned(S, b, t):
                        act.wait_ge(t_ready, S + 1)
                        nc.scalar.copy(probT[:, b, 0, :, t * NT:(t + 1) * NT],
                                       ps[0:NT, 4, 0:4 * NT].rearrange("p (o n) -> p o n", o=OG)).then_inc(ptA_ready, 1)

                    def copy_out(U, par, og):
                        act.wait_ge(o_ready, U + 1)
                        nc.scalar.copy(oT[:, par, og, :], ps[:, O_BANK, 0:PW]).then_inc(oT_ready, 1)

                    def slot(p, par, s, first, last):
                        S = 8 * p + s
                        tasks = slot_tasks(p, s, first, last)
                        if not (first and s == 0):
                            exps(S - 1, (s - 1) % 2)
                        if s < 4 or not last:
                            base = 12 * (2 * p + 1 + s // 4)
                            if s == 4:
                                act.wait_ge(sq_ready, 3 * p + 5)
                                act.wait_ge(side_free, task_base(p) + T_G3 + 1)
                            for ft in range(FT):
                                mixed(base + 3 * (s % 4) + ft, 1 - s // 4, s % 4, ft, par if s < 4 else 1 - par)
                        if s == 2 and not first:
                            copy_out(2 * p - 1, 1 - par, 1)
                        if s == 6:
                            copy_out(2 * p, par, 0)
                        side(tasks[0], p, par)
                        if not (first and s == 0):
                            copy_turned(S - 1, (s - 1) % 4 // 2, (s - 1) % 2)
                        side(tasks[1], p, par)

                    def prologue():
                        act.wait_ge(v_filled, 2)
                        for k in range(FEATURES):
                            feature(k, k, 0, 0)
                            if k == T_G3:
                                act.wait_ge(sq_ready, 2)
                                act.wait_ge(side_free, T_G3 + 1)
                                for n in range(12):
                                    mixed(n, 0, n // 3, n % 3, 0)

                    def epilogue():
                        exps(8 * NP - 1, 1)
                        copy_turned(8 * NP - 1, 1, 1)
                        copy_out(2 * NP - 1, 1, 1)
                        for k in range(FINISH):
                            finish(task_base(NP - 1) + FINISH + k, k, NP - 1, 1)

                    pairs(act, prologue, slot, epilogue)

                @block.gpsimd
                def _(pool):
                    gp = nc.gpsimd

                    def expand(q, par):
                        for n, sh in enumerate((0, 0, 1, 2, 3, 4)):
                            ins = gp.tensor_tensor(
                                mb[0:C, par, :, n, :].rearrange("p b (h j) -> p b h j", h=H),
                                mc12[:, bass.ds(2 * q, 2), sh:sh + D].unsqueeze(2).broadcast_to([C, 2, H, D]),
                                mask[0:C, 0:H].unsqueeze(1).unsqueeze(3).broadcast_to([C, 2, H, D]), ALU.mult)
                        ins.then_inc(mb_ready, 1)

                    def squares(count, dst, src, par, whole):
                        pool.wait_ge(side_free, count + 1)
                        if whole:
                            gp.tensor_tensor(dst[:, par, 2, :], src[:], src[:], ALU.mult).then_inc(sq_ready, 1)
                        else:
                            gp.tensor_tensor(dst[0:C, par, 2, :], src[0:C, :], src[0:C, :], ALU.mult).then_inc(sq_ready, 1)

                    def bias(S, sp_, og):
                        pool.wait_ge(nmax_ready, S + 1)
                        sh = shift_o[:, OG * og:OG * og + OG]
                        gp.tensor_tensor(nms[:, sp_], nmax[:, sp_], sh, ALU.subtract).then_inc(nms_ready, 1)
                        pool.wait_ge(nms_ready, S + 1)
                        gp.tensor_tensor(ebias[:, sp_], nms[:, sp_], sh, ALU.add).then_inc(ebias_ready, 1)

                    def slot(p, par, s, first, last):
                        S = 8 * p + s
                        base = task_base(p)
                        nxt = 1 - par
                        if s == 0 and not last:
                            expand(p + 1, nxt)
                        if s == 2 and not last:
                            squares(base + T_G1, fg, ga, nxt, True)
                        bias(S, s % 2, s // 4)
                        if s == 0 and not last:
                            squares(base + T_Q1, fq, qa, nxt, False)
                        if s == 3 and not last:
                            squares(base + T_K1, fk, ka, nxt, False)

                    def prologue():
                        gp.memset(vx[:], 0.0).then_inc(v_filled, 1)
                        pool.wait_ge(v_filled, 1)
                        gp.memset(vx[:, :, :, :, D:D + 1], 1.0).then_inc(v_filled, 1)
                        expand(0, 0)
                        squares(T_Q1, fq, qa, 0, False)
                        squares(T_G1, fg, ga, 0, True)
                        squares(T_K1, fk, ka, 0, False)

                    pairs(pool, prologue, slot, lambda: None)

                @block.vector
                def _(dve):
                    nv = nc.vector

                    def mixed(n, og, o, ft, par):
                        dve.wait_ge(part_ready, n + 1)
                        ins = nv.scalar_tensor_tensor(out=F[:, og, o, ft, :], in0=fg[:, par, ft, :],
                                                      scalar=mix[:, 1, ft, OG * og + o:OG * og + o + 1],
                                                      in1=part[:, ft], op0=ALU.mult, op1=ALU.add)
                        ins.then_inc(part_used, 1)

                    def feature(count, k, q, par):
                        found = {T_Q2: (fq, qa, 0), T_Q3: (fq, qa, 1), T_G2: (fg, ga, 0), T_G3: (fg, ga, 1),
                                 T_K2: (fk, ka, 0), T_K3: (fk, ka, 1)}.get(k)
                        if found:
                            dst, src, ft = found
                            dve.wait_ge(side_ready, count + 1)
                            if ft == 0:
                                dve.wait_ge(side_free, count)
                            nv.tensor_tensor(dst[:, par, ft, :], ps[:, SIDE, 0:PW], src[:], ALU.mult).then_inc(side_free, 1)

                    def finish(count, k, q, par):
                        b = k // 3
                        if k % 3 == 0:
                            dve.wait_ge(side_ready, count + 1)
                            v = ps[0:NT, SIDE, :].rearrange("p (a v) -> p a v", v=VW)
                            nv.reciprocal(rden[:].unsqueeze(2), v[:, :, D:D + 1]).then_inc(rden_ready, 1)
                            dve.wait_ge(rden_ready, 2 * q + b + 1)
                            nv.tensor_tensor(otok[:].rearrange("p t (h d) -> p (t h) d", h=H), v[:, :, 0:D],
                                             rden[:].unsqueeze(2).broadcast_to([NT, 2 * H, D]), ALU.mult
                                             ).then_inc(side_free, 1)
                        if k % 3 == 2:
                            dve.wait_ge(side_ready, count + 1)
                            ht = h_all[:, bass.ds(4 * q + 2 * b, 2), :]
                            nv.tensor_tensor(ht, ht, ps[0:NT, SIDE, 0:2 * C].rearrange("p (t c) -> p t c", c=C),
                                             ALU.add).then_inc(side_free, 1)

                    def side(task, p, par):
                        if task:
                            count, kind, k = task
                            (feature if kind == "feature" else finish)(count, k, p + 1 if kind == "feature" else p - 1, 1 - par)

                    def row_max(S, sp_):
                        dve.wait_ge(l_ready, S + 1)
                        nv.tensor_reduce(nmax[:, sp_].rearrange("p (a o) -> p a o", a=2),
                                         ps[0:NT, 2 * sp_:2 * sp_ + 2, 0:PW].rearrange("p a (o n) -> p a o n", o=2),
                                         AX.X, ALU.max, negate=True).then_inc(nmax_ready, 1)

                    def copy_turned(S, b, t):
                        dve.wait_ge(t_ready, S + 1)
                        nv.tensor_copy(probT[:, b, 1, :, t * NT:(t + 1) * NT],
                                       ps[0:NT, 5, 0:4 * NT].rearrange("p (o n) -> p o n", o=OG)).then_inc(ptD_ready, 1)

                    def slot(p, par, s, first, last):
                        S = 8 * p + s
                        tasks = slot_tasks(p, s, first, last)
                        if s < 4 or not last:
                            base = 12 * (2 * p + 1 + s // 4)
                            if s == 4:
                                dve.wait_ge(sq_ready, 3 * p + 5)
                            for ft in range(FT):
                                mixed(base + 3 * (s % 4) + ft, 1 - s // 4, s % 4, ft, par if s < 4 else 1 - par)
                        side(tasks[0], p, par)
                        row_max(S, s % 2)
                        if not (first and s == 0):
                            copy_turned(S - 1, (s - 1) % 4 // 2, (s - 1) % 2)
                        side(tasks[1], p, par)

                    def prologue():
                        nv.memset(ztc[C:C + 1], 1.0).then_inc(filled, 1)
                        nv.memset(oc[C:C + 1, :], 1.0).then_inc(filled, 1)
                        nv.memset(mb[C:, :, :, :, :], 0.0).then_inc(filled, 1)
                        for k in range(FEATURES):
                            feature(k, k, 0, 0)
                            if k == T_G3:
                                dve.wait_ge(sq_ready, 2)
                                for n in range(12):
                                    mixed(n, 0, n // 3, n % 3, 0)

                    def epilogue():
                        copy_turned(8 * NP - 1, 1, 1)
                        for k in range(FINISH):
                            finish(task_base(NP - 1) + FINISH + k, k, NP - 1, 1)

                    pairs(dve, prologue, slot, epilogue)

        NCH = 4
        CH = NTILE // NCH
        with ExitStack() as st:
            zc2 = sb("zc2", [NT, NTILE, C], stack=st)
            sq2 = sb("sq2", [NT, 2, CH, C], stack=st)
            mean2 = sb("mean2", [NT, NTILE], stack=st)
            var2 = sb("var2", [NT, NTILE], stack=st)
            z2 = sb("z2", [NT, 2, 4, C], stack=st)
            z2t = sb("z2t", [C + 1, 2, PW], stack=st)
            hid = sb("hid", [128, 2, 2, PW], stack=st)
            lg = sb("lg", [NT, NTILE, E], stack=st)
            gmax = sb("gmax", [NT, 2], stack=st)
            score = sb("score", [NT, E], stack=st)
            pick = sb("pick", [NT, 2], stack=st)
            emask = sb("emask", [NT, E], stack=st)
            chosen = sb("chosen", [NT, E, C], stack=st)
            gexp = sb("gexp", [NT, NTILE, E], stack=st)
            d_step, d_cent, d_sq, d_sqrt = sem("d_step"), sem("d_cent"), sem("d_sq"), sem("d_sqrt")
            d_ones, z2_ready, z2T_ready, z2t_ready = sem("d_ones"), sem("z2_ready"), sem("z2T_ready"), sem("z2t_ready")
            hid_ready, gelu_done, y2_ready = sem("hid_ready"), sem("gelu_done"), sem("y2_ready")
            y2_free, gexp_ready, res_ready, stored = sem("y2_free"), sem("gexp_ready"), sem("res_ready"), sem("stored")
            d_pick, d_tail = sem("d_pick"), sem("d_tail")
            D_STATS = 4 * NCH

            def by_parity(eng, front, back):
                front(0, 0)
                front(1, 1)
                back(0, 0)
                with eng.Fori(0, NP // 2 - 1) as i:
                    front(2 * i + 2, 0)
                    back(2 * i + 1, 1)
                    front(2 * i + 3, 1)
                    back(2 * i + 2, 0)
                back(NP - 1, 1)

            with nc.Block() as block:
                @block.vector
                def _(dve):
                    nv = nc.vector
                    nv.memset(z2t[C:C + 1], 1.0).then_inc(d_ones, 1)
                    for c in range(NCH):
                        at = slice(c * CH, (c + 1) * CH)
                        nv.tensor_reduce(mean2[:, at], h_all[:, at, :], AX.X, ALU.add).then_inc(d_step, 1)
                        dve.wait_ge(d_step, 2 * c + 1)
                        nv.tensor_scalar(mean2[:, at], mean2[:, at], -1.0 / C, None, ALU.mult).then_inc(d_step, 1)
                    for c in range(NCH):
                        at = slice(c * CH, (c + 1) * CH)
                        dve.wait_ge(d_sq, c + 1)
                        nv.tensor_reduce(var2[:, at], sq2[:, c % 2], AX.X, ALU.add).then_inc(d_step, 1)
                        dve.wait_ge(d_step, 2 * NCH + 2 * c + 1)
                        nv.tensor_scalar(var2[:, at], var2[:, at], 1.0 / C, LN_EPS, ALU.mult, ALU.add).then_inc(d_step, 1)
                    dve.wait_ge(d_sqrt, 1)
                    nv.reciprocal(var2[:], var2[:]).then_inc(d_step, 1)

                    def choose(T, yb):
                        dve.wait_ge(y2_ready, T + 1)
                        gates = ps[0:NT, 3 + 2 * yb, 0:E]
                        gmx = gmax[:, yb:yb + 1]
                        nv.tensor_reduce(gmx, gates, AX.X, ALU.max).then_inc(d_pick, 1)
                        dve.wait_ge(d_pick, 4 * T + 1)
                        nv.tensor_scalar(lg[:, bass.ds(T, 1), :].rearrange("p a e -> p (a e)"), gates, gmx, None, ALU.subtract)
                        nv.scalar_tensor_tensor(out=score[:], in0=gates, scalar=gmx, in1=pri[:],
                                                op0=ALU.is_ge, op1=ALU.mult).then_inc(d_pick, 1)
                        dve.wait_ge(d_pick, 4 * T + 2)
                        nv.tensor_reduce(pick[:, yb:yb + 1], score[:], AX.X, ALU.max).then_inc(d_pick, 1)
                        dve.wait_ge(d_pick, 4 * T + 3)
                        nv.tensor_scalar(emask[:], pri[:], pick[:, yb:yb + 1], None, ALU.is_equal).then_inc(d_pick, 1)
                        dve.wait_ge(d_pick, 4 * T + 4)
                        nv.tensor_tensor(chosen[:].rearrange("p (a e) c -> p a e c", a=2),
                                         ps[0:NT, 3 + 2 * yb:5 + 2 * yb, E:E + 4 * C].rearrange("p a (e c) -> p a e c", e=4),
                                         emask[:].rearrange("p (a e) -> p a e", a=2).unsqueeze(3).broadcast_to([NT, 2, 4, C]),
                                         ALU.mult).then_inc(y2_free, 1)
                        dve.wait_ge(y2_free, T + 1)
                        nv.tensor_reduce(zc2[:, bass.ds(T, 1), :].rearrange("p a c -> p (a c)"),
                                         chosen[:].rearrange("p e c -> p c e"), AX.X, ALU.add).then_inc(d_tail, 1)

                    with dve.Fori(0, NP) as g:
                        for k in range(4):
                            if k == 0:
                                dve.wait_ge(z2_ready, g + 1)
                            choose(4 * g + k, k % 2)

                    dve.wait_ge(gexp_ready, 1)
                    nv.tensor_reduce(mean2[:], gexp[:], AX.X, ALU.add).then_inc(d_step, 1)
                    dve.wait_ge(d_step, D_STATS + 2)
                    nv.reciprocal(mean2[:], mean2[:]).then_inc(d_step, 1)
                    dve.wait_ge(d_step, D_STATS + 3)
                    dve.wait_ge(d_tail, NTILE)
                    for c in range(NCH):
                        at = slice(c * CH, (c + 1) * CH)
                        nv.tensor_tensor(zc2[:, at, :], zc2[:, at, :],
                                         mean2[:, at].unsqueeze(2).broadcast_to([NT, CH, C]), ALU.mult).then_inc(d_step, 1)
                        dve.wait_ge(d_step, D_STATS + 4 + c)
                        nv.tensor_tensor(h_all[:, at, :], h_all[:, at, :], zc2[:, at, :], ALU.add).then_inc(res_ready, 1)

                @block.gpsimd
                def _(pool):
                    gp = nc.gpsimd
                    for c in range(NCH):
                        at = slice(c * CH, (c + 1) * CH)
                        pool.wait_ge(d_step, 2 * c + 2)
                        gp.tensor_tensor(zc2[:, at, :], h_all[:, at, :],
                                         mean2[:, at].unsqueeze(2).broadcast_to([NT, CH, C]), ALU.add).then_inc(d_cent, 1)
                    pool.wait_ge(d_step, D_STATS + 1)

                    def scale(g, par):
                        if not (isinstance(g, int) and g < 2):
                            pool.wait_ge(z2T_ready, g - 1)
                        gp.tensor_tensor(z2[:, par], zc2[:, bass.ds(4 * g, 4), :],
                                         var2[:, bass.ds(4 * g, 4)].unsqueeze(2).broadcast_to([NT, 4, C]),
                                         ALU.mult).then_inc(z2_ready, 1)

                    scale(0, 0)
                    scale(1, 1)
                    with pool.Fori(0, NP // 2 - 1) as i:
                        for par in range(2):
                            scale(2 * i + 2 + par, par)

                @block.scalar
                def _(act):
                    for c in range(NCH):
                        act.wait_ge(d_cent, c + 1)
                        if c >= 2:
                            act.wait_ge(d_step, 2 * NCH + 2 * (c - 2) + 1)
                        nc.scalar.activation(sq2[:, c % 2], zc2[:, c * CH:(c + 1) * CH, :], ACT.Square).then_inc(d_sq, 1)
                    act.wait_ge(d_step, D_STATS)
                    nc.scalar.activation(var2[:], var2[:], ACT.Sqrt).then_inc(d_sqrt, 1)

                    def front(g, par):
                        act.wait_ge(z2T_ready, g + 1)
                        for k in range(2):
                            nc.scalar.copy(z2t[0:C, par].rearrange("c (t k n) -> c t k n", k=2, n=NT)[:, :, k, :],
                                           ps[k * C:(k + 1) * C, 0, 0:N].rearrange("c (t n) -> c t n", n=NT)
                                           ).then_inc(z2t_ready, 1)
                        act.wait_ge(hid_ready, g + 1)
                        if not (isinstance(g, int) and g < 2):
                            act.wait_ge(y2_ready, 4 * g - 4)
                        nc.scalar.activation(hid[:, par], ps[:, 1:3, 0:PW], ACT.Gelu).then_inc(gelu_done, 1)

                    front(0, 0)
                    front(1, 1)
                    with act.Fori(0, NP // 2 - 1) as i:
                        for par in range(2):
                            front(2 * i + 2 + par, par)
                    act.wait_ge(y2_free, NTILE)
                    nc.scalar.activation(gexp[:], lg[:], ACT.Exp).then_inc(gexp_ready, 1)

                @block.tensor
                def _(pe):
                    pe.wait_ge(d_ones, 1)

                    def front(g, par):
                        pe.wait_ge(z2_ready, g + 1)
                        pe.wait_ge(z2t_ready, 2 * g)
                        for t in range(2):
                            mm = pe.transpose(ps[:, 0, t * NT:(t + 1) * NT],
                                              z2[:, par, 2 * t:2 * t + 2, :].rearrange("p t c -> p (t c)"), ident[0:NT, 0:NT])
                        mm.then_inc(z2T_ready, 1)
                        pe.wait_ge(z2t_ready, 2 * g + 2)
                        pe.wait_ge(gelu_done, g)
                        for c in range(2):
                            mm = pe.matmul(ps[:, 1 + c, 0:PW], w[:, W_1 + 128 * c:W_1 + 128 * (c + 1)], z2t[:, par],
                                           start=True, stop=True)
                        mm.then_inc(hid_ready, 1)

                    def back(g, par):
                        pe.wait_ge(gelu_done, g + 1)
                        for k in range(4):
                            if not (isinstance(g, int) and g == 0 and k < 2):
                                pe.wait_ge(y2_free, 4 * g + k - 1)
                            for a, (lo, hi) in enumerate(((0, E + 4 * C), (E + 4 * C, E + 8 * C))):
                                off = 0 if a == 0 else E
                                dst = ps[0:NT, 3 + 2 * (k % 2) + a, off:off + hi - lo]
                                pe.matmul(dst, ones3[:], wb3[:, lo:hi], start=True, stop=False)
                                for c in range(2):
                                    mm = pe.matmul(dst, hid[:, par, c, k * NT:(k + 1) * NT], wl[:, c, lo:hi],
                                                   start=False, stop=c == 1)
                            mm.then_inc(y2_ready, 1)

                    by_parity(pe, front, back)

                @block.sync
                def _(sp):
                    nb = CH // 2
                    for c in range(NCH):
                        sp.wait_ge(res_ready, c + 1)
                        sp.dma_start(out[c * nb:(c + 1) * nb].rearrange("b (t p) c -> p (b t) c", t=2),
                                     h_all[:, c * CH:(c + 1) * CH, :]).then_inc(stored, 16)
                    sp.wait_ge(stored, 16 * NCH)


def kernel(**inputs):
    import concourse.bacc as bacc
    from concourse.bass_utils import run_bass_kernel_spmd as run

    a = {k: np.asarray(v) for k, v in inputs.items()}
    arrays = lay_out(a)
    B = a["x"].shape[0]
    nc = bacc.Bacc("TRN2", target_bir_lowering=False, num_devices=1)
    args = [nc.dram_tensor(n, v.shape, mybir.dt.from_np(v.dtype), kind="ExternalInput").ap()
            for n, v in arrays.items()]
    o = nc.dram_tensor("out_dram", (B, N, C), F32, kind="ExternalOutput").ap()
    audio_tower(nc, *args, o)
    r = run(nc, [arrays], core_ids=[0])
    return r.results[0]["out_dram"]


def lay_out(a):
    f = np.float32
    row = np.arange(128)
    half, h, d = row // C, row % C // D, row % D

    def with_bias(wm, bias):
        return np.concatenate([wm, bias[None]], 0)

    wqkv = with_bias(a["L0_attn_w_qkv"].T, a["L0_attn_b_qkv"])
    twice = h * D + d
    cols = [twice] + [h * D + (d + 2 * t + 1 + half) % D for t in range(2)]
    cols = np.concatenate(cols)
    w65 = np.concatenate([wqkv[:, cols], wqkv[:, C + cols], wqkv[:, 0:2 * C], wqkv[:, 2 * C:],
                          with_bias(a["L0_attn_w_proj"].T, a["L0_attn_b_proj"]),
                          with_bias(a["L0_ffn_W1"], a["L0_ffn_b1"])], 1)
    kconv = a["L0_tok_kernel"].transpose(1, 0, 2).reshape(CIN, TAPS * C)
    chan = np.stack([a["L0_tok_bias"], a["L0_tok_beta"], a["L0_tok_moving_mean"], a["L0_tok_moving_var"]])
    chan = np.broadcast_to(chan, (128, 4, C))
    wall = np.concatenate([a["L0_ffn_Wg"]] + list(a["L0_ffn_Wd"]), 1).reshape(2, 128, E + E * C).transpose(1, 0, 2)
    wbias = np.concatenate([a["L0_ffn_bg"], a["L0_ffn_bd"].reshape(-1)])[None]

    low = half == 1
    channel = np.stack([np.stack([H + h, H + h, np.where(low, h, H + h)], 1), np.repeat(2 * H + h[:, None], FT, 1)], 1)
    pairs_counted = np.ones((128, 2, FT), f)
    pairs_counted[:, :, 0] = 2
    pairs_counted[~low, :, 1] = 2
    pairs_counted[low, 1, 2] = 0
    scales = np.broadcast_to(a["L0_attn_riem_scale"], (128, 2, FT)).copy()
    scales[:, 1] = a["L0_attn_grassman_scale"]
    scales[low, 0, 2] = a["L0_attn_scale"]
    mixw = a["L0_attn_conv_w"].T[channel]
    flat = channel.reshape(128, 2 * FT)
    mixbn = np.stack([a["L0_attn_bn_gamma"][flat], a["L0_attn_bn_var"][flat], scales.reshape(128, -1),
                      pairs_counted.reshape(128, -1)], 1)
    cw = np.broadcast_to(with_bias(a["L0_attn_conv_w"].T, a["L0_attn_conv_b"]).T, (128, H, 25))
    cbn = np.broadcast_to(np.stack([a["L0_attn_bn_gamma"], a["L0_attn_bn_var"], a["L0_attn_bn_mean"],
                                    a["L0_attn_bn_beta"]]), (128, 4, 24))
    consts = np.zeros((128, 216), f)
    consts[:, 0:128] = np.eye(128)
    consts[row, 128 + row // D] = 1
    consts[:, 144:208] = np.eye(D).reshape(-1)
    consts[:, 208:216] = np.arange(E, 0, -1)
    named = dict(x=a["x"], w65=w65, kconv=kconv, chan=chan, wall=wall, wbias=wbias, mixw=mixw, mixbn=mixbn,
                 cw=cw, cbn=cbn, consts=consts)
    return {f"in_{k}_dram": np.ascontiguousarray(v) for k, v in named.items()}
```

```python
from contextlib import ExitStack

import numpy as np

import concourse.bass as bass
from concourse import mybir

F32 = mybir.dt.float32
F32R = mybir.dt.float32r
BF16 = mybir.dt.bfloat16
ALU = mybir.AluOpType
ACT = mybir.ActivationFunctionType
AX = mybir.AxisListType

H, D = 8, 8
C = H * D
CIN = 128
TAPS = 3
TIN = 250
N = TIN - TAPS + 1
NT = N // 2
XT = TIN // 2
PW = 2 * N
E = 8
HID = 256
FT = 3
OG = 4
UH = 2
VW = D + 1
SLOT = 32
BN_EPS, TOK_EPS, LN_EPS = 1e-5, 1e-3, 1e-5

W_QK, W_P, W_1, W_END = 0, 128, 192, 448
V_Q, V_K, V_V, V_END = 0, FT * 128, 2 * FT * 128, 2 * FT * 128 + C


def audio_tower(nc, x, w65, w128, fbias, vbias, kconv, chan, wall, wbias, mixw, mixbn, cw, cbn, consts, out):
    B = x.shape[0]
    NP = B // 2
    NG = B // 4
    G16 = B // 16
    NTILE = 2 * B

    with ExitStack() as ctx:
        def sb(name, shape, dt=F32, stack=ctx):
            return stack.enter_context(nc.sbuf_tensor(name, shape, dt))

        def sem(name):
            return ctx.enter_context(nc.semaphore(name))

        zt_dram = nc.dram_tensor("zt_scratch", (NP, 2, C, PW), F32, kind="Internal").ap()
        gram_dram = nc.dram_tensor("gram_scratch", (H, B, 2, D, D), F32, kind="Internal").ap()
        top_dram = nc.dram_tensor("top_scratch", (H, B, 2, D, D), F32, kind="Internal").ap()
        m_dram = nc.dram_tensor("m_scratch", (H, B, D, D), F32, kind="Internal").ap()

        ps = ctx.enter_context(nc.psum_tensor("ps", [128, 8, 512], F32))

        h_all = sb("h_all", [NT, NTILE, C])
        w = sb("w", [C + 1, W_END])
        ident = sb("ident", [128, 128])
        mask = sb("mask", [128, 16])
        eye8 = sb("eye8", [128, 64])
        bmask = sb("bmask", [128, H])
        mix = sb("mix", [128, 2, FT, H])
        shift_o = sb("shift_o", [NT, H])
        mch = sb("mch", [128, B, 12], F32R)
        mcl = sb("mcl", [C, B, 12], F32R)
        whi = sb("whi", [128, V_END], F32R)
        wlo = sb("wlo", [128, V_END], F32R)
        fb = sb("fb", [128, 2 * FT])
        vb = sb("vb", [NT, C])
        pri = sb("pri", [NT, E])
        wl = sb("wl", [128, 2, E + E * C])
        wb3 = sb("wb3", [128, E + E * C], BF16)
        ones3 = sb("ones3", [128, NT], BF16)

        with ExitStack() as st:
            chan_sb = sb("chan_sb", [NT, 4, C], stack=st)
            aff = sb("aff", [NT, 3, C], stack=st)
            kc = sb("kc", [CIN, TAPS * C], stack=st)
            kq = sb("kq", [CIN, TAPS * C], BF16, stack=st)
            mw = sb("mw", [128, 2, FT, H], stack=st)
            mbn = sb("mbn", [128, 4, 2 * FT], stack=st)
            minv = sb("minv", [128, 2 * FT], stack=st)
            cw_sb = sb("cw_sb", [NT, H, 25], stack=st)
            cbn_sb = sb("cbn_sb", [NT, 4, 24], stack=st)
            cinv = sb("cinv", [NT, 24], stack=st)
            wb_f = sb("wb_f", [1, 3, E + E * C], stack=st)
            wb_b = sb("wb_b", [1, 3, E + E * C], BF16, stack=st)
            xt = sb("xt", [XT, 2, 8, CIN], stack=st)
            xs = sb("xs", [CIN, 2, 500], BF16, stack=st)
            ysc = sb("ysc", [NT, 8, C], stack=st)
            hg = sb("hg", [NT, 8, C], stack=st)
            stat = sb("stat", [NT, 4, 8], stack=st)
            zc = sb("zc", [NT, 8, C], stack=st)
            zsq = sb("zsq", [NT, 8, C], stack=st)
            z = sb("z", [NT, 2, 8, C], stack=st)
            zt = sb("zt", [C + 1, 2, 8 * NT], stack=st)
            zh = sb("zh", [C, 2, 8 * NT], F32R, stack=st)
            zl = sb("zl", [C, 2, 8 * NT], F32R, stack=st)
            wf = sb("wf", [128, V_END], stack=st)
            qkt = sb("qkt", [NT, 8, 128], stack=st)
            gm = sb("gm", [128, 4, 16, D], stack=st)
            gram = sb("gram", [128, B, D], stack=st)
            top = sb("top", [D, B, 128], stack=st)

            loaded, small_loaded = sem("loaded"), sem("small_loaded")
            a_vec, a_sqrt, a_ones = sem("a_vec"), sem("a_sqrt"), sem("a_ones")
            wb_moved = sem("wb_moved")
            x_in = [sem("x_in_even"), sem("x_in_odd")]
            xT_ready, xs_ready, y_ready = sem("xT_ready"), sem("xs_ready"), sem("y_ready")
            h_ready, zc_ready, zsq_ready = sem("h_ready"), sem("zc_ready"), sem("zsq_ready")
            var_ready, std_ready, z_ready = sem("var_ready"), sem("std_ready"), sem("z_ready")
            zT_ready, zt_ready = sem("zT_ready"), sem("zt_ready")
            zh_ready, zl_ready = sem("zh_ready"), sem("zl_ready")
            zt_out = [sem("zt_out_even"), sem("zt_out_odd")]
            qk_ready, qkt_ready, gram_ready = sem("qk_ready"), sem("qkt_ready"), sem("gram_ready")
            gm_masked = sem("gm_masked")
            h_kept = sem("h_kept")
            ln_step, ln_rstd = sem("ln_step"), sem("ln_rstd")
            gm_ready, top_ready, gram_out = sem("gm_ready"), sem("top_ready"), sem("gram_out")

            def skewed(eng, front, back):
                front(0, 0)
                front(1, 1)
                back(0, 0)
                front(2, 0)
                back(1, 1)
                if NG > 4:
                    with eng.Fori(0, NG // 2 - 2) as i:
                        front(2 * i + 3, 1)
                        back(2 * i + 2, 0)
                        front(2 * i + 4, 0)
                        back(2 * i + 3, 1)
                front(NG - 1, 1)
                back(NG - 2, 0)
                back(NG - 1, 1)

            SETUP = 29

            with nc.Block() as block:
                @block.sync
                def _(sp):
                    for dst, src in ((w[:], w65), (kc[:], kconv), (chan_sb[:], chan[0:NT]), (mw[:], mixw),
                                     (mbn[:], mixbn), (cw_sb[:], cw[0:NT]), (cbn_sb[:], cbn[0:NT]),
                                     (ident[:], consts[:, 0:128]), (mask[:], consts[:, 128:144]),
                                     (eye8[:], consts[:, 144:208]), (pri[:], consts[0:NT, 208:216]),
                                     (wl[:], wall), (wb_f[:, 0, :], wbias), (wf[:], w128), (fb[:], fbias),
                                     (vb[:], vbias[0:NT]), (bmask[:], consts[:, 216:224])):
                        sp.dma_start(dst, src).then_inc(small_loaded, 16)

                    def load_x(g, par):
                        src = x[bass.ds(4 * g, 4)].rearrange("b (t p) c -> p (b t) c", p=XT)
                        sp.dma_start(xt[:, par], src).then_inc(x_in[par], 16)

                    def store_zt(g, par):
                        sp.wait_ge(zl_ready, g + 1)
                        for k, src in enumerate((zh, zl)):
                            sp.dma_start(zt_dram[bass.ds(2 * g, 2), k].rearrange("a c n -> c a n"),
                                         src[:, par].bitcast(F32).rearrange("c (a n) -> c a n", a=2)).then_inc(zt_out[par], 16)

                    load_x(0, 0)
                    load_x(1, 1)
                    if NG > 2:
                        with sp.Fori(0, NG // 2 - 1) as i:
                            for par in range(2):
                                sp.wait_ge(xT_ready, 4 * i + 2 * par + 2)
                                load_x(2 * i + 2 + par, par)
                                store_zt(2 * i + par, par)
                    store_zt(NG - 2, 0)
                    store_zt(NG - 1, 1)
                    sp.wait_ge(a_vec, SETUP)
                    sp.wait_ge(a_ones, 3)
                    for k in range(3):
                        sp.dma_start(wb3[k:k + 1, :], wb_b[:, k, :]).then_inc(wb_moved, 16)
                    sp.wait_ge(gm_ready, NG)
                    sp.wait_ge(top_ready, NG)
                    for qk in range(2):
                        for h in range(H):
                            r = (qk * H + h) * D
                            sp.dma_start(gram_dram[h, :, qk].rearrange("b i j -> i b j"),
                                         gram[r:r + D, :, :]).then_inc(gram_out, 16)
                            sp.dma_start(top_dram[h, :, qk].rearrange("b i j -> i b j"),
                                         top[:, :, r:r + D]).then_inc(gram_out, 16)
                    sp.wait_ge(wb_moved, 48)
                    sp.wait_ge(zt_out[0], 16 * NG)
                    sp.wait_ge(zt_out[1], 16 * NG)
                    sp.wait_ge(gram_out, 2 * 16 * 2 * H)

                @block.tensor
                def _(pe):
                    pe.wait_ge(small_loaded, 16 * 17)

                    def front(g, par):
                        pe.wait_ge(x_in[par], 8 * g + 16 - 8 * par)
                        pe.wait_ge(xs_ready, 2 * g)
                        for k in range(8):
                            mm = pe.transpose(ps[:, k // 4, (k % 4) * XT:(k % 4 + 1) * XT], xt[:, par, k, :],
                                              ident[0:XT, 0:XT])
                            if k % 4 == 3:
                                mm.then_inc(xT_ready, 1)
                        pe.wait_ge(xs_ready, 2 * g + 2)
                        pe.wait_ge(h_ready, g)
                        for k in range(8):
                            for tap in range(TAPS):
                                at = (k // 2 % 2) * TIN + (k % 2) * NT + tap
                                mm = pe.matmul(ps[0:NT, 2, k * C:(k + 1) * C], xs[:, k // 4, at:at + NT],
                                               kq[:, tap * C:(tap + 1) * C], start=tap == 0, stop=tap == TAPS - 1)
                        mm.then_inc(y_ready, 1)

                    def back(g, par):
                        pe.wait_ge(z_ready, g + 1)
                        pe.wait_ge(zt_ready, 2 * g)
                        for k in range(4):
                            mm = pe.transpose(ps[:, 3, k * NT:(k + 1) * NT],
                                              z[:, par, 2 * k:2 * k + 2, :].rearrange("p t c -> p (t c)"), ident[0:NT, 0:NT])
                        mm.then_inc(zT_ready, 1)
                        pe.wait_ge(zt_ready, 2 * g + 2)
                        pe.wait_ge(qkt_ready, 2 * g)
                        for k in range(8):
                            mm = pe.matmul(ps[0:NT, 5 + k // 4, (k % 4) * 128:(k % 4 + 1) * 128],
                                           zt[:, par, k * NT:(k + 1) * NT], w[:, W_QK:W_QK + 128],
                                           start=True, stop=True)
                        mm.then_inc(qk_ready, 1)
                        pe.wait_ge(qkt_ready, 2 * g + 2)
                        pe.wait_ge(gm_ready, g)
                        for b in range(4):
                            for t in range(2):
                                mm = pe.matmul(ps[:, 7, b * 128:(b + 1) * 128], qkt[:, 2 * b + t, :],
                                               qkt[:, 2 * b + t, :], start=t == 0, stop=t == 1)
                        mm.then_inc(gram_ready, 1)

                    pe.wait_ge(a_vec, SETUP)
                    pe.wait_ge(a_ones, 3)
                    skewed(pe, front, back)

                @block.scalar
                def _(act):
                    act.wait_ge(small_loaded, 16 * 17)
                    act.wait_ge(a_vec, 4)
                    nc.scalar.activation(aff[:, 0, :], chan_sb[:, 3, :], ACT.Sqrt).then_inc(a_sqrt, 1)
                    nc.scalar.activation(minv[:], mbn[:, 1, :], ACT.Sqrt).then_inc(a_sqrt, 1)
                    nc.scalar.activation(cinv[:], cbn_sb[:, 1, :], ACT.Sqrt).then_inc(a_sqrt, 1)

                    def front(g, par):
                        act.wait_ge(var_ready, g + 1)
                        nc.scalar.activation(stat[:, 2, :], stat[:, 1, :], ACT.Sqrt, scale=1.0).then_inc(std_ready, 1)

                    def back(g, par):
                        act.wait_ge(zT_ready, g + 1)
                        if not (isinstance(g, int) and g < 2):
                            act.wait_ge(zl_ready, g - 1)
                        for k in range(2):
                            nc.scalar.copy(zt[0:C, par].rearrange("c (t k n) -> c t k n", k=2, n=NT)[:, :, k, :],
                                           ps[k * C:(k + 1) * C, 3, 0:PW].rearrange("c (t n) -> c t n", n=NT)
                                           ).then_inc(zt_ready, 1)
                        act.wait_ge(zt_ready, 2 * g + 2)
                        if not (isinstance(g, int) and g < 2):
                            act.wait_ge(zt_out[par], 16 * g - 16 * par)
                        nc.scalar.copy(zh[:, par], zt[0:C, par]).then_inc(zh_ready, 1)
                        act.wait_ge(qk_ready, g + 1)
                        act.wait_ge(gram_ready, g)
                        act.wait_ge(top_ready, g)
                        for k in range(2):
                            nc.scalar.copy(qkt[:, 4 * k:4 * k + 4, :],
                                           ps[0:NT, 5 + k, :].rearrange("p (t c) -> p t c", c=128)).then_inc(qkt_ready, 1)

                    skewed(act, front, back)

                @block.gpsimd
                def _(pool):
                    nc.gpsimd.memset(wb3[:], 0.0).then_inc(a_ones, 1)
                    nc.gpsimd.memset(ones3[:], 0.0).then_inc(a_ones, 1)
                    pool.wait_ge(a_ones, 2)
                    nc.gpsimd.memset(ones3[0:3, :], 1.0).then_inc(a_ones, 1)

                    def front(g, par):
                        pool.wait_ge(ln_step, 4 * g + 1)
                        nc.gpsimd.tensor_copy(h_all[:, bass.ds(8 * g, 8), :], hg[:]).then_inc(h_kept, 1)
                        pool.wait_ge(zc_ready, g + 1)
                        nc.gpsimd.tensor_tensor(zsq[:], zc[:], zc[:], ALU.mult).then_inc(zsq_ready, 1)

                    def back(g, par):
                        pool.wait_ge(zh_ready, g + 1)
                        nc.gpsimd.tensor_tensor(zl[:, par], zt[0:C, par], zh[:, par].bitcast(F32),
                                                ALU.subtract).then_inc(zl_ready, 1)
                        pool.wait_ge(qkt_ready, 2 * g + 2)
                        nc.gpsimd.tensor_copy(top[:, bass.ds(4 * g, 4), :],
                                              qkt[0:D, 0:8:2, :]).then_inc(top_ready, 1)

                    skewed(pool, front, back)

                @block.vector
                def _(dve):
                    steps = [0]

                    def link(ins):
                        steps[0] += 1
                        ins.then_inc(a_vec, 1)
                        dve.wait_ge(a_vec, steps[0])

                    nv = nc.vector
                    link(nv.memset(zt[C:C + 1, :, :], 1.0))
                    dve.wait_ge(small_loaded, 16 * 17)
                    link(nv.tensor_scalar(chan_sb[:, 3, :], chan_sb[:, 3, :], TOK_EPS, None, ALU.add))
                    link(nv.tensor_scalar(mbn[:, 1, :], mbn[:, 1, :], BN_EPS, None, ALU.add))
                    link(nv.tensor_scalar(cbn_sb[:, 1, :], cbn_sb[:, 1, :], BN_EPS, None, ALU.add))
                    link(nv.tensor_copy(whi[:], wf[:]))
                    link(nv.memset(wlo[C:, :].bitcast(F32), 0.0))
                    link(nv.tensor_tensor(wlo[0:C, :], wf[0:C, :], whi[0:C, :].bitcast(F32), ALU.subtract))
                    link(nv.tensor_scalar(kc[:], kc[:], 0.0, 0.5, ALU.is_ge, ALU.subtract))
                    link(nv.tensor_scalar(kq[:], kc[:], 4.0, None, ALU.mult))
                    dve.wait_ge(a_sqrt, 3)
                    link(nv.reciprocal(aff[:, 1, :], aff[:, 0, :]))
                    link(nv.tensor_tensor(aff[:, 2, :], chan_sb[:, 0, :], chan_sb[:, 2, :], ALU.subtract))
                    link(nv.tensor_tensor(aff[:, 2, :], aff[:, 2, :], aff[:, 1, :], ALU.mult))
                    link(nv.tensor_tensor(aff[:, 2, :], aff[:, 2, :], chan_sb[:, 1, :], ALU.add))
                    link(nv.reciprocal(minv[:], minv[:]))
                    for j in (0, 2, 3):
                        link(nv.tensor_tensor(minv[:], minv[:], mbn[:, j, :], ALU.mult))
                    mi = minv[:].rearrange("p (a t) -> p a t", a=2).unsqueeze(3).broadcast_to([128, 2, FT, H])
                    link(nv.tensor_tensor(mix[:], mw[:], mi, ALU.mult))
                    link(nv.reciprocal(cinv[:], cinv[:]))
                    link(nv.tensor_tensor(cinv[:], cinv[:], cbn_sb[:, 0, :], ALU.mult))
                    link(nv.tensor_tensor(cinv[:], cinv[:], cbn_sb[:, 2, :], ALU.mult))
                    link(nv.tensor_tensor(cinv[:], cbn_sb[:, 3, :], cinv[:], ALU.subtract))
                    link(nv.tensor_tensor(cw_sb[:, :, 0:24], cw_sb[:, :, 0:24],
                                          cinv[:].unsqueeze(1).broadcast_to([NT, H, 24]), ALU.mult))
                    link(nv.tensor_reduce(shift_o[:], cw_sb[:], AX.X, ALU.add))
                    link(nv.tensor_copy(wb_b[:, 0, :], wb_f[:, 0, :]))
                    link(nv.tensor_tensor(wb_f[:, 1, :], wb_f[:, 0, :], wb_b[:, 0, :], ALU.subtract))
                    link(nv.tensor_copy(wb_b[:, 1, :], wb_f[:, 1, :]))
                    link(nv.tensor_tensor(wb_f[:, 2, :], wb_f[:, 1, :], wb_b[:, 1, :], ALU.subtract))
                    link(nv.tensor_copy(wb_b[:, 2, :], wb_f[:, 2, :]))
                    assert steps[0] == SETUP, steps[0]

                    def row(ap):
                        return ap.unsqueeze(1).broadcast_to([NT, 8, C])

                    def col(ap):
                        return ap.unsqueeze(2).broadcast_to([NT, 8, C])

                    def front(g, par):
                        for k in range(2):
                            dve.wait_ge(xT_ready, 2 * g + 1 + k)
                            if k == 0:
                                dve.wait_ge(y_ready, g)
                            nv.tensor_scalar(xs[:, k, :], ps[:, k, 0:500], 0.0, 0.5, ALU.is_ge,
                                             ALU.subtract).then_inc(xs_ready, 1)
                        dve.wait_ge(y_ready, g + 1)
                        yv = ps[0:NT, 2, :].rearrange("p (t c) -> p t c", c=C)
                        dve.wait_ge(h_kept, g)
                        nv.tensor_tensor(ysc[:], yv, row(aff[:, 1, :]), ALU.mult).then_inc(h_ready, 1)
                        dve.wait_ge(h_ready, g + 1)
                        ht = hg[:]
                        nv.tensor_tensor(ht, ysc[:], row(aff[:, 2, :]), ALU.add).then_inc(ln_step, 1)
                        dve.wait_ge(ln_step, 4 * g + 1)
                        nv.tensor_reduce(stat[:, 0, :], ht, AX.X, ALU.add).then_inc(ln_step, 1)
                        dve.wait_ge(ln_step, 4 * g + 2)
                        nv.tensor_scalar(stat[:, 0, :], stat[:, 0, :], -1.0 / C, None, ALU.mult).then_inc(ln_step, 1)
                        dve.wait_ge(ln_step, 4 * g + 3)
                        nv.tensor_tensor(zc[:], ht, col(stat[:, 0, :]), ALU.add).then_inc(zc_ready, 1)
                        dve.wait_ge(zsq_ready, g + 1)
                        nv.tensor_reduce(stat[:, 3, :], zsq[:], AX.X, ALU.add).then_inc(ln_step, 1)
                        dve.wait_ge(ln_step, 4 * g + 4)
                        nv.tensor_scalar(stat[:, 1, :], stat[:, 3, :], 1.0 / C, LN_EPS, ALU.mult,
                                         ALU.add).then_inc(var_ready, 1)
                        dve.wait_ge(std_ready, g + 1)
                        nv.reciprocal(stat[:, 2, :], stat[:, 2, :]).then_inc(ln_rstd, 1)
                        dve.wait_ge(ln_rstd, g + 1)
                        if not (isinstance(g, int) and g < 2):
                            dve.wait_ge(zT_ready, g - 1)
                        nv.tensor_tensor(z[:, par], zc[:], col(stat[:, 2, :]), ALU.mult).then_inc(z_ready, 1)

                    def back(g, par):
                        dve.wait_ge(gram_ready, g + 1)
                        nv.tensor_tensor(gm[:], ps[:, 7, :].rearrange("p (b k j) -> p b k j", b=4, k=16),
                                         mask[:].unsqueeze(1).unsqueeze(3).broadcast_to([128, 4, 16, D]),
                                         ALU.mult).then_inc(gm_masked, 1)
                        dve.wait_ge(gm_masked, g + 1)
                        nv.tensor_reduce(gram[:, bass.ds(4 * g, 4), :], gm[:].rearrange("p b k j -> p b j k"),
                                         AX.X, ALU.add).then_inc(gm_ready, 1)

                    skewed(dve, front, back)

        with ExitStack() as st:
            GP = 2 * G16
            gw = sb("gw", [128, GP, D, 2 * D], stack=st)
            mc = sb("mc", [128, B, 12], stack=st)
            gl = sb("gl", [128, GP, D, D], stack=st)
            av = sb("av", [128, GP, D, D], stack=st)
            ri = sb("ri", [128, GP, D, D], stack=st)
            q8 = sb("q8", [128, GP, D, D], stack=st)
            tmp = sb("tmp", [128, GP, D, 2 * D], stack=st)
            fac = sb("fac", [128, GP, D], stack=st)
            piv = sb("piv", [128, GP, D], stack=st)
            rs = sb("rs", [128, GP, D], stack=st)
            sg = sb("sg", [128, GP, D], stack=st)
            ss = sb("ss", [128, G16, D], stack=st)
            mm_ = sb("mm_", [128, G16, D, D], stack=st)
            mt = sb("mt", [128, G16, D, D], stack=st)
            b_in, b_step, b_sqrt = sem("b_in"), sem("b_step"), sem("b_sqrt")
            m_out, m_in, m_wrap = sem("m_out"), sem("m_in"), sem("m_wrap")
            B_PIVOTS, B_STEPS = [0], [0]

            with nc.Block() as block:
                @block.vector
                def _(dve):
                    nv = nc.vector
                    steps = [0]

                    def link(ins):
                        steps[0] += 1
                        ins.then_inc(b_step, 1)
                        dve.wait_ge(b_step, steps[0])

                    dve.wait_ge(b_in, 16 * 2 * H)
                    link(nv.tensor_copy(gw[:, :, :, 0:D], gl[:]))
                    link(nv.tensor_copy(gw[:, :, :, D:], eye8[:].rearrange("p (i j) -> p i j", i=D)
                                        .unsqueeze(1).broadcast_to([128, GP, D, D])))
                    for d in range(D - 1):
                        n = D - 1 - d
                        link(nv.reciprocal(piv[:, :, d:d + 1], gw[:, :, d, d:d + 1]))
                        link(nv.tensor_tensor(fac[:, :, 0:n], gw[:, :, d + 1:, d],
                                              piv[:, :, d:d + 1].broadcast_to([128, GP, n]), ALU.mult))
                        link(nv.tensor_tensor(tmp[:, :, 0:n, :],
                                              fac[:, :, 0:n].unsqueeze(3).broadcast_to([128, GP, n, 2 * D]),
                                              gw[:, :, d:d + 1, :].broadcast_to([128, GP, n, 2 * D]), ALU.mult))
                        link(nv.tensor_tensor(gw[:, :, d + 1:, :], gw[:, :, d + 1:, :], tmp[:, :, 0:n, :],
                                              ALU.subtract))
                    link(nv.tensor_copy(piv[:], gw[:].rearrange("p g i j -> p g (i j)")[:, :, 0:128:17]))
                    B_PIVOTS[0] = steps[0]
                    dve.wait_ge(b_sqrt, 1)
                    link(nv.reciprocal(rs[:], rs[:]))
                    link(nv.tensor_tensor(sg[:], rs[:], rs[:], ALU.mult))
                    link(nv.tensor_tensor(sg[:], sg[:], piv[:], ALU.mult))
                    link(nv.tensor_scalar(sg[:], sg[:], -0.5, 1.5, ALU.mult, ALU.add))
                    link(nv.tensor_tensor(rs[:], rs[:], sg[:], ALU.mult))
                    link(nv.tensor_tensor(ri[:], gw[:, :, :, D:].rearrange("p g j i -> p g i j"),
                                          rs[:].unsqueeze(2).broadcast_to([128, GP, D, D]), ALU.mult))

                    def product(dst, part, left, right, G):
                        for i in range(D):
                            into = dst if i == 0 else part
                            link(nv.tensor_tensor(into, left(i).unsqueeze(3).broadcast_to([128, G, D, D]),
                                                  right(i).unsqueeze(2).broadcast_to([128, G, D, D]), ALU.mult))
                            if i:
                                link(nv.tensor_tensor(dst, dst, part, ALU.add))

                    product(q8[:], tmp[:, :, :, 0:D], lambda i: av[:, :, :, i], lambda i: ri[:, :, i, :], GP)
                    for d in range(D):
                        n = D - 1 - d
                        pivot = q8[:, :, d, d:d + 1]
                        link(nv.tensor_scalar(sg[:, :, d:d + 1], pivot, 0.0, 2.0, ALU.is_lt, ALU.mult))
                        link(nv.tensor_scalar(sg[:, :, d:d + 1], sg[:, :, d:d + 1], -1.0, None, ALU.add))
                        if not n:
                            break
                        link(nv.tensor_tensor(fac[:, :, 7:8], pivot, sg[:, :, d:d + 1], ALU.subtract))
                        link(nv.reciprocal(fac[:, :, 7:8], fac[:, :, 7:8]))
                        link(nv.tensor_tensor(fac[:, :, 0:n], q8[:, :, d + 1:, d],
                                              fac[:, :, 7:8].broadcast_to([128, GP, n]), ALU.mult))
                        link(nv.tensor_tensor(tmp[:, :, 0:n, 0:n],
                                              fac[:, :, 0:n].unsqueeze(3).broadcast_to([128, GP, n, n]),
                                              q8[:, :, d:d + 1, d + 1:].broadcast_to([128, GP, n, n]), ALU.mult))
                        link(nv.tensor_tensor(q8[:, :, d + 1:, d + 1:], q8[:, :, d + 1:, d + 1:],
                                              tmp[:, :, 0:n, 0:n], ALU.subtract))
                    link(nv.tensor_tensor(ss[:], sg[:, 0::2, :], sg[:, 1::2, :], ALU.mult))
                    link(nv.tensor_tensor(mt[:], ri[:, 0::2, :, :],
                                          ss[:].unsqueeze(2).broadcast_to([128, G16, D, D]), ALU.mult))
                    product(mm_[:], tmp[:, 0:G16, :, 0:D], lambda i: mt[:, :, :, i],
                            lambda i: ri[:, 1::2, :, i], G16)
                    B_STEPS[0] = steps[0]
                    dve.wait_ge(m_in, 16 * 2 * H)
                    nv.tensor_copy(mc[:, :, D:12], mc[:, :, 0:4]).then_inc(m_wrap, 1)
                    dve.wait_ge(m_wrap, 1)
                    nv.tensor_copy(mch[:], mc[:]).then_inc(m_wrap, 1)
                    dve.wait_ge(m_wrap, 2)
                    nv.tensor_tensor(mcl[:], mc[0:C], mch[0:C].bitcast(F32), ALU.subtract).then_inc(m_wrap, 1)

                @block.scalar
                def _(act):
                    act.wait_ge(b_step, B_PIVOTS[0])
                    nc.scalar.activation(rs[:], piv[:], ACT.Sqrt).then_inc(b_sqrt, 1)

                @block.sync
                def _(sp):
                    for h in range(H):
                        for dst, src in ((gl, gram_dram), (av, top_dram)):
                            sp.dma_start(dst[16 * h:16 * h + 16].rearrange("p (g k) i j -> p g (k i j)", k=2),
                                         src[h].rearrange("(g b) k i j -> b g (k i j)", b=16)).then_inc(b_in, 16)
                    sp.wait_ge(b_step, B_STEPS[0])
                    for h in range(H):
                        sp.dma_start(m_dram[h].rearrange("(g b) i j -> b g (i j)", b=16),
                                     mm_[16 * h:16 * h + 16].rearrange("p g i j -> p g (i j)")).then_inc(m_out, 16)
                    sp.wait_ge(m_out, 16 * H)
                    for h in range(2 * H):
                        sp.dma_start(mc[D * h:D * h + D, :, 0:D],
                                     m_dram[h % H].rearrange("b i j -> i b j")).then_inc(m_in, 16)
                    sp.wait_ge(m_in, 16 * 2 * H)
                    sp.wait_ge(m_wrap, 3)

        FEATURES, FINISH = 10, 6
        NS, UNITS = 16, H // UH
        TILES = UH * FT
        ALL_TILES = TILES * UNITS * NP
        T_BANK, O_BANK, SIDE = 4, 6, 7
        T_Q1, T_Q2, T_Q3, T_V, T_G1, T_G2, T_G3, T_K1, T_K2, T_K3 = range(FEATURES)
        STEPS_AT = ((1, 2), (3,), (4, 5), (6,))

        def task_base(p):
            if isinstance(p, int) and p == 0:
                return FEATURES
            return 2 * FEATURES + (FEATURES + FINISH) * (p - 1)

        def slot_task(p, par, s, first, last, feature, finish):
            if s < FEATURES:
                if not last:
                    feature(task_base(p) + s, s, p + 1, 1 - par)
            elif not first:
                k = s - FEATURES
                finish(task_base(p) + k + (0 if last else FEATURES), k, p - 1, 1 - par)

        def steps(p, s, do):
            for k in STEPS_AT[s % 4]:
                do(p, (s // 4 + 1) * TILES + k)

        def tile_of(p, k):
            n = TILES * UNITS * p + k
            shift, k = divmod(k, TILES * UNITS)
            unit, k = divmod(k, TILES)
            exists = n >= 0 and n < ALL_TILES if isinstance(n, int) else True
            return n, exists, shift, unit, k // FT, k % FT

        ON_POOL = (0, 2, 3, 5)

        def is_on_pool(k):
            return k % TILES in ON_POOL

        def lows(p, k, on_pool):
            share = len(ON_POOL) if on_pool else TILES - len(ON_POOL)
            return share * (UNITS * p + k // TILES) + sum(is_on_pool(j) == on_pool for j in range(k % TILES + 1))

        def pairs(eng, prologue, slot, epilogue):
            prologue()
            for s in range(NS):
                slot(0, 0, s, True, False)
            with eng.Fori(0, NP // 2 - 1) as i:
                for par, p in ((1, 2 * i + 1), (0, 2 * i + 2)):
                    for s in range(NS):
                        slot(p, par, s, False, False)
            for s in range(NS):
                slot(NP - 1, 1, s, False, True)
            epilogue()

        with ExitStack() as st:
            zs = sb("zs", [128, 2, PW], F32R, stack=st)
            qa = sb("qa", [128, PW], stack=st)
            ga = sb("ga", [128, PW], stack=st)
            qs = sb("qs", [128, PW], F32R, stack=st)
            mbh = sb("mbh", [128, 2, 6, C], F32R, stack=st)
            mbl = sb("mbl", [128, 2, 6, C], F32R, stack=st)
            fq = sb("fq", [128, 2, FT, PW], stack=st)
            fg = sb("fg", [128, 2, FT, PW], stack=st)
            kx = sb("kx", [128, 2, PW], stack=st)
            fkh = sb("fkh", [128, 2, FT, PW], F32R, stack=st)
            fkl = sb("fkl", [128, 2, FT, PW], F32R, stack=st)
            fx = sb("fx", [128, 4, PW], stack=st)
            Fh = sb("Fh", [128, 2, UH, FT, PW], F32R, stack=st)
            Fl = sb("Fl", [128, 2, UH, FT, PW], F32R, stack=st)
            prob = sb("prob", [NT, 2, UH, N], stack=st)
            probT = sb("probT", [NT, 2, 2, OG, N], stack=st)
            nmax = sb("nmax", [NT, 2, UH], stack=st)
            nms = sb("nms", [NT, 2, UH], stack=st)
            ebias = sb("ebias", [NT, 2, UH], stack=st)
            vx = sb("vx", [NT, 2, 4, H, VW], stack=st)
            oT = sb("oT", [128, 2, 2, PW], stack=st)
            rden = sb("rden", [NT, 2 * H], stack=st)
            otok = sb("otok", [NT, 2, C], stack=st)
            oc = sb("oc", [C + 1, N], stack=st)

            filled = sem("filled")
            zs_in = [sem("zs_in_even"), sem("zs_in_odd")]
            side_ready, side_free = sem("side_ready"), sem("side_free")
            mb_ready, qs_ready, kh_ready, kl_ready = (
                sem("mb_ready"), sem("qs_ready"), sem("kh_ready"), sem("kl_ready"))
            part_ready, mixed_ready, hi_ready = sem("part_ready"), sem("mixed_ready"), sem("hi_ready")
            lo_ready = {True: sem("lo_on_pool"), False: sem("lo_on_dve")}
            l_ready, nmax_ready, nms_ready, ebias_ready = (
                sem("l_ready"), sem("nmax_ready"), sem("nms_ready"), sem("ebias_ready"))
            exp_done, t_ready, pt_ready = sem("exp_done"), sem("t_ready"), sem("pt_ready")
            o_ready, oT_ready, rden_ready = sem("o_ready"), sem("oT_ready"), sem("rden_ready")

            with nc.Block() as block:
                @block.sync
                def _(sp):
                    def load(q, par):
                        sp.dma_start(zs[:, par].bitcast(F32), zt_dram[bass.ds(q, 1)].rearrange("a k c n -> (a k c) n")
                                     ).then_inc(zs_in[par], 16)

                    load(0, 0)
                    load(1, 1)
                    sp.wait_ge(side_ready, FEATURES)
                    load(2, 0)
                    sp.wait_ge(side_ready, 2 * FEATURES)
                    load(3, 1)
                    with sp.Fori(0, NP // 2 - 2) as i:
                        for par in range(2):
                            p = 2 * i + par + 1
                            sp.wait_ge(side_ready, 2 * FEATURES + (FEATURES + FINISH) * (p - 1) + FEATURES)
                            load(p + 3, par)

                @block.tensor
                def _(pe):
                    def feature(count, k, q, par):
                        if k == T_Q1:
                            pe.wait_ge(zs_in[par], 8 * q + 16 - 8 * par)
                        if k == T_G1:
                            pe.wait_ge(mb_ready, q + 1)
                            pe.wait_ge(qs_ready, q + 1)
                        pe.wait_ge(side_free, count)
                        if k in (T_Q1, T_Q2, T_Q3, T_K1, T_K2, T_K3):
                            at = V_Q + 128 * (k - T_Q1) if k <= T_Q3 else V_K + 128 * (k - T_K1)
                            pe.matmul(ps[:, SIDE, 0:PW], whi[:, at:at + 128], zs[:, par], start=True, stop=False)
                            mm = pe.matmul(ps[:, SIDE, 0:PW], wlo[:, at:at + 128], zs[:, par], start=False, stop=True)
                        elif k in (T_G1, T_G2, T_G3):
                            n = 2 * (k - T_G1)
                            for b in range(2):
                                for m in (mbh, mbl):
                                    mm = pe.matmul(ps[:, SIDE, b * N:(b + 1) * N],
                                                   m[:, b, n:n + 2, :].rearrange("p s c -> p (s c)"),
                                                   qs[:, b * N:(b + 1) * N], start=m is mbh, stop=m is mbl)
                        else:
                            for t in range(4):
                                for m in (whi, wlo):
                                    mm = pe.matmul(ps[0:NT, SIDE, t * C:(t + 1) * C], zs[:, par, t * NT:(t + 1) * NT],
                                                   m[:, V_V:V_V + C], start=m is whi, stop=m is wlo)
                        mm.then_inc(side_ready, 1)

                    def finish(count, k, q, par):
                        b = k // 3
                        if k == 0:
                            pe.wait_ge(oT_ready, 2 * q + 2)
                        pe.wait_ge(side_free, count)
                        if k % 3 == 0:
                            for t in range(2):
                                for og in range(2):
                                    at = (2 * t + og) * 128
                                    mm = pe.transpose(ps[0:NT, SIDE, at:at + 128],
                                                      oT[:, par, og, b * N + t * NT:b * N + (t + 1) * NT], ident[:])
                        elif k % 3 == 1:
                            mm = pe.transpose(ps[:, SIDE, 0:NT], otok[:].rearrange("p t c -> p (t c)"), ident[0:NT, 0:NT])
                        else:
                            for t in range(2):
                                mm = pe.matmul(ps[0:NT, SIDE, t * C:(t + 1) * C], oc[:, t * NT:(t + 1) * NT],
                                               w[:, W_P:W_P + C], start=True, stop=True)
                        mm.then_inc(side_ready, 1)

                    def scores(s, par, o):
                        u, b, t = s // 4, s // 2 % 2, s % 2
                        dst = ps[0:NT, s % 4, o * N:(o + 1) * N]
                        terms = [(F_, k_, ft) for F_, k_ in ((Fh, fkh), (Fh, fkl), (Fl, fkh)) for ft in range(FT)]
                        for n, (F_, k_, ft) in enumerate(terms):
                            mm = pe.matmul(dst, F_[:, u % 2, o, ft, b * N + t * NT:b * N + (t + 1) * NT],
                                           k_[:, par, ft, b * N:(b + 1) * N], start=n == 0, stop=n == len(terms) - 1)
                        return mm

                    def turn(S, tb):
                        pe.wait_ge(exp_done, S + 1)
                        if not (isinstance(S, int) and S < 2):
                            pe.wait_ge(pt_ready, S - 1)
                        for mt in range(2):
                            for o in range(UH):
                                at = (UH * mt + o) * NT
                                mm = pe.transpose(ps[0:NT, T_BANK + tb, at:at + NT],
                                                  prob[:, tb, o, mt * NT:(mt + 1) * NT], ident[0:NT, 0:NT])
                        mm.then_inc(t_ready, 1)

                    def values(G, S, og, b, par):
                        pe.wait_ge(pt_ready, S + 1)
                        if b == 0:
                            pe.wait_ge(oT_ready, G)
                        for mt in range(2):
                            for j in range(OG):
                                mm = pe.matmul(ps[SLOT * j:SLOT * j + VW, O_BANK, b * N:(b + 1) * N],
                                               vx[:, par, 2 * b + mt, OG * og + j, :], probT[:, b, mt, j, :],
                                               start=mt == 0, stop=mt == 1)
                        if b == 1:
                            mm.then_inc(o_ready, 1)

                    def slot(p, par, s, first, last):
                        S = NS * p + s
                        u = s // 4
                        if s == 0:
                            pe.wait_ge(kl_ready, FT * p + FT)
                        if s % 4 == 0:
                            for on_pool, lo in lo_ready.items():
                                pe.wait_ge(lo, lows(p, TILES * u + FT - 1, on_pool))
                        if not (first and s < 4):
                            pe.wait_ge(exp_done, S - 3)
                        scores(s, par, 0)
                        slot_task(p, par, s, first, last, feature, finish)
                        if s % 4 == 0:
                            for on_pool, lo in lo_ready.items():
                                pe.wait_ge(lo, lows(p, TILES * u + TILES - 1, on_pool))
                        if s in (0, 2) and not first:
                            values(2 * p - 1, S - 3, 1, s // 2, 1 - par)
                        if s in (8, 10):
                            values(2 * p, S - 3, 0, (s - 8) // 2, par)
                        scores(s, par, 1).then_inc(l_ready, 1)
                        if not (first and s < 2):
                            turn(S - 2, s % 2)

                    def prologue():
                        pe.wait_ge(filled, 4)
                        for k in range(FEATURES):
                            feature(k, k, 0, 0)

                    def epilogue():
                        turn(NS * NP - 2, 0)
                        values(2 * NP - 1, NS * NP - 3, 1, 0, 1)
                        turn(NS * NP - 1, 1)
                        values(2 * NP - 1, NS * NP - 1, 1, 1, 1)
                        for k in range(FINISH):
                            finish(task_base(NP - 1) + FINISH + k, k, NP - 1, 1)

                    pairs(pe, prologue, slot, epilogue)

                @block.scalar
                def _(act):
                    def scaled(p, k, par):
                        n, exists, shift, u, o, ft = tile_of(p, k)
                        if not exists:
                            return
                        if not (isinstance(n, int) and n < 4):
                            act.wait_ge(lo_ready[is_on_pool(k - 4)], lows(p, k - 4, is_on_pool(k - 4)))
                        head = UH * u + o
                        nc.scalar.activation(fx[:, k % 4], fq[:, (par + shift) % 2, ft, :], ACT.Copy,
                                             scale=mix[:, 0, ft, head:head + 1]).then_inc(part_ready, 1)

                    def feature(count, k, q, par):
                        if k not in (T_Q1, T_K1, T_G1):
                            return
                        act.wait_ge(side_ready, count + 1)
                        if k == T_G1:
                            nc.scalar.activation(fg[:, par, 2, :], ps[:, SIDE, 0:PW], ACT.Square)
                            nc.scalar.copy(ga[:], ps[:, SIDE, 0:PW]).then_inc(side_free, 1)
                        else:
                            bias = fb[:, 0:1] if k == T_Q1 else fb[:, FT:FT + 1]
                            tile2 = fq[:, par, 2, :] if k == T_Q1 else kx[:, 0, :]
                            nc.scalar.activation(tile2[C:], ps[C:, SIDE, 0:PW], ACT.Identity, bias=bias[C:])
                            nc.scalar.activation(tile2[0:C], ps[0:C, SIDE, 0:PW], ACT.Square, bias=bias[0:C])
                            if k == T_Q1:
                                nc.scalar.activation(qs[:], ps[:, SIDE, 0:PW], ACT.Identity, bias=bias)
                            nc.scalar.activation(qa[:], ps[:, SIDE, 0:PW], ACT.Identity, bias=bias).then_inc(side_free, 1)

                    def finish(count, k, q, par):
                        if k % 3 == 1:
                            act.wait_ge(side_ready, count + 1)
                            nc.scalar.copy(oc[0:C, 0:NT], ps[0:C, SIDE, 0:NT])
                            nc.scalar.copy(oc[0:C, NT:N], ps[C:, SIDE, 0:NT]).then_inc(side_free, 1)

                    def exps(S, sp_, bank):
                        act.wait_ge(ebias_ready, S + 1)
                        if not (isinstance(S, int) and S < 2):
                            act.wait_ge(t_ready, S - 1)
                        for o in range(UH):
                            ins = nc.scalar.activation(prob[:, sp_, o, :], ps[0:NT, bank, o * N:(o + 1) * N],
                                                       ACT.Exp, bias=ebias[:, sp_, o:o + 1])
                        ins.then_inc(exp_done, 1)

                    def copy_turned(S, s):
                        act.wait_ge(t_ready, S + 1)
                        u, b, t = s // 4, s // 2 % 2, s % 2
                        j = UH * (u % 2)
                        nc.scalar.copy(probT[:, b, :, j:j + UH, t * NT:(t + 1) * NT],
                                       ps[0:NT, T_BANK + s % 2, 0:2 * UH * NT].rearrange("p (m o n) -> p m o n", m=2, o=UH)
                                       ).then_inc(pt_ready, 1)

                    def copy_out(G, par, og):
                        act.wait_ge(o_ready, G + 1)
                        nc.scalar.copy(oT[:, par, og, :], ps[:, O_BANK, 0:PW]).then_inc(oT_ready, 1)

                    def slot(p, par, s, first, last):
                        S = NS * p + s
                        if s == 10 and not last:
                            act.wait_ge(side_free, task_base(p) + T_G3 + 1)

                        steps(p, s, lambda p, k: scaled(p, k + 1, par))
                        if not (first and s == 0):
                            exps(S - 1, (s - 1) % 2, (s - 1) % 4)
                        if s == 3 and not first:
                            copy_out(2 * p - 1, 1 - par, 1)
                        if s == 11:
                            copy_out(2 * p, par, 0)
                        slot_task(p, par, s, first, last, feature, finish)
                        if not (first and s < 2):
                            copy_turned(S - 2, (s - 2) % NS)

                    def prologue():
                        for k in range(FEATURES):
                            feature(k, k, 0, 0)
                            if k == T_G3:
                                act.wait_ge(side_free, T_G3 + 1)
                                for n in range(-1, 7):
                                    scaled(0, n + 1, 0)

                    def epilogue():
                        exps(NS * NP - 1, 1, 3)
                        copy_turned(NS * NP - 2, NS - 2)
                        copy_turned(NS * NP - 1, NS - 1)
                        copy_out(2 * NP - 1, 1, 1)
                        for k in range(FINISH):
                            finish(task_base(NP - 1) + FINISH + k, k, NP - 1, 1)

                    pairs(act, prologue, slot, epilogue)

                @block.gpsimd
                def _(pool):
                    gp = nc.gpsimd

                    def low(p, k, par):
                        n, exists, shift, u, o, ft = tile_of(p, k)
                        if exists and is_on_pool(k):
                            pool.wait_ge(hi_ready, n + 1)
                            gp.tensor_tensor(Fl[:, u % 2, o, ft, :], fx[:, k % 4], Fh[:, u % 2, o, ft, :].bitcast(F32),
                                             ALU.subtract).then_inc(lo_ready[True], 1)

                    def expand(q, third):
                        pieces = [(dst, src, rows, n, sh) for dst, src, rows in ((mbh, mch, 128), (mbl, mcl, C))
                                  for n, sh in enumerate((0, 0, 1, 2, 3, 4))]
                        for dst, src, rows, n, sh in pieces[4 * third:4 * third + 4]:
                            ins = gp.tensor_tensor(
                                dst[0:rows, :, n, :].rearrange("p b (h j) -> p b h j", h=H),
                                src[:].bitcast(F32)[:, bass.ds(2 * q, 2), sh:sh + D].unsqueeze(2)
                                .broadcast_to([rows, 2, H, D]),
                                bmask[0:rows].unsqueeze(1).unsqueeze(3).broadcast_to([rows, 2, H, D]), ALU.mult)
                        if third == 2:
                            ins.then_inc(mb_ready, 1)

                    def bias(S, sp_, u):
                        pool.wait_ge(nmax_ready, S + 1)
                        sh = shift_o[:, UH * u:UH * u + UH]
                        gp.tensor_tensor(nms[:, sp_], nmax[:, sp_], sh, ALU.subtract).then_inc(nms_ready, 1)
                        pool.wait_ge(nms_ready, S + 1)
                        if not (isinstance(S, int) and S < 2):
                            pool.wait_ge(exp_done, S - 1)
                        gp.tensor_tensor(ebias[:, sp_], nms[:, sp_], sh, ALU.add).then_inc(ebias_ready, 1)

                    def feature(count, k, q, par):
                        if k in (T_K2, T_K3):
                            for n, ft in ((0, 2), (1, 0)) if k == T_K2 else ((2, 1),):
                                pool.wait_ge(kh_ready, FT * q + n + 1)
                                gp.tensor_tensor(fkl[:, par, ft, :], kx[:, n % 2], fkh[:, par, ft, :].bitcast(F32),
                                                 ALU.subtract).then_inc(kl_ready, 1)

                    def slot(p, par, s, first, last):
                        S = NS * p + s
                        steps(p, s, lambda p, k: low(p, k - 1, par))
                        bias(S, s % 2, s // 4)
                        if s < 3 and not last:
                            expand(p + 1, s)
                        slot_task(p, par, s, first, last, feature, lambda *_: None)

                    def prologue():
                        for third in range(3):
                            expand(0, third)
                        for k in range(FEATURES):
                            feature(k, k, 0, 0)
                            if k == T_G3:
                                for n in range(0, 7):
                                    low(0, n - 1, 0)

                    pairs(pool, prologue, slot, lambda: None)

                @block.vector
                def _(dve):
                    nv = nc.vector

                    def mixed(p, k, par):
                        n, exists, shift, u, o, ft = tile_of(p, k)
                        if exists:
                            dve.wait_ge(part_ready, n + 1)
                            head = UH * u + o
                            nv.scalar_tensor_tensor(out=fx[:, k % 4], in0=fg[:, (par + shift) % 2, ft, :],
                                                    scalar=mix[:, 1, ft, head:head + 1], in1=fx[:, k % 4],
                                                    op0=ALU.mult, op1=ALU.add).then_inc(mixed_ready, 1)

                    def high(p, k, par):
                        n, exists, shift, u, o, ft = tile_of(p, k)
                        if exists:
                            dve.wait_ge(mixed_ready, n + 1)
                            nv.tensor_copy(Fh[:, u % 2, o, ft, :], fx[:, k % 4]).then_inc(hi_ready, 1)

                    def low(p, k, par):
                        n, exists, shift, u, o, ft = tile_of(p, k)
                        if exists and not is_on_pool(k):
                            dve.wait_ge(hi_ready, n + 1)
                            nv.tensor_tensor(Fl[:, u % 2, o, ft, :], fx[:, k % 4], Fh[:, u % 2, o, ft, :].bitcast(F32),
                                             ALU.subtract).then_inc(lo_ready[False], 1)

                    def step(p, k, par):
                        mixed(p, k, par)
                        low(p, k - 2, par)
                        high(p, k - 1, par)

                    def split_k(q, par, n, ft):
                        nv.tensor_copy(fkh[:, par, ft, :], kx[:, n % 2]).then_inc(kh_ready, 1)

                    def feature(count, k, q, par):
                        found = {T_Q2: (fq[:, par, 0, :], qa, 1), T_Q3: (fq[:, par, 1, :], qa, 2),
                                 T_G2: (fg[:, par, 0, :], ga, None), T_G3: (fg[:, par, 1, :], ga, None),
                                 T_K2: (kx[:, 1, :], qa, FT + 1), T_K3: (kx[:, 0, :], qa, FT + 2)}.get(k)
                        if found:
                            dst, src, bias = found
                            dve.wait_ge(side_ready, count + 1)
                            dve.wait_ge(side_free, count)
                            if k == T_K3:
                                dve.wait_ge(kl_ready, FT * q + 1)
                            if bias is None:
                                nv.tensor_tensor(dst, ps[:, SIDE, 0:PW], src[:], ALU.mult).then_inc(side_free, 1)
                            else:
                                nv.scalar_tensor_tensor(out=dst, in0=ps[:, SIDE, 0:PW], scalar=fb[:, bias:bias + 1],
                                                        in1=src[:], op0=ALU.add, op1=ALU.mult).then_inc(side_free, 1)
                        if k == T_Q2:
                            nv.tensor_tensor(qs[C:], qa[C:], qs[C:].bitcast(F32), ALU.subtract).then_inc(qs_ready, 1)
                        if k == T_K2:
                            split_k(q, par, 0, 2)
                        if k in (T_K2, T_K3):
                            dve.wait_ge(side_free, count + 1)
                            split_k(q, par, k - T_K1, k - T_K2)
                        if k == T_V:
                            dve.wait_ge(side_ready, count + 1)
                            nv.tensor_tensor(vx[:, par, :, :, 0:D],
                                             ps[0:NT, SIDE, 0:4 * C].rearrange("p (t h d) -> p t h d", t=4, h=H),
                                             vb[:].rearrange("p (h d) -> p h d", h=H).unsqueeze(1)
                                             .broadcast_to([NT, 4, H, D]), ALU.add).then_inc(side_free, 1)

                    def finish(count, k, q, par):
                        b = k // 3
                        if k % 3 == 0:
                            dve.wait_ge(side_ready, count + 1)
                            v = ps[0:NT, SIDE, :].rearrange("p (a v) -> p a v", v=SLOT)
                            nv.reciprocal(rden[:].unsqueeze(2), v[:, :, D:D + 1]).then_inc(rden_ready, 1)
                            dve.wait_ge(rden_ready, 2 * q + b + 1)
                            nv.tensor_tensor(otok[:].rearrange("p t (h d) -> p (t h) d", h=H), v[:, :, 0:D],
                                             rden[:].unsqueeze(2).broadcast_to([NT, 2 * H, D]), ALU.mult
                                             ).then_inc(side_free, 1)
                        if k % 3 == 2:
                            dve.wait_ge(side_ready, count + 1)
                            ht = h_all[:, bass.ds(4 * q + 2 * b, 2), :]
                            nv.tensor_tensor(ht, ht, ps[0:NT, SIDE, 0:2 * C].rearrange("p (t c) -> p t c", c=C),
                                             ALU.add).then_inc(side_free, 1)

                    def row_max(S, sp_, bank):
                        dve.wait_ge(l_ready, S + 1)
                        if not (isinstance(S, int) and S < 2):
                            dve.wait_ge(nms_ready, S - 1)
                        nv.tensor_reduce(nmax[:, sp_], ps[0:NT, bank, 0:PW].rearrange("p (o n) -> p o n", o=UH),
                                         AX.X, ALU.max, negate=True).then_inc(nmax_ready, 1)

                    def slot(p, par, s, first, last):
                        S = NS * p + s

                        steps(p, s, lambda p, k: step(p, k, par))
                        slot_task(p, par, s, first, last, feature, finish)
                        row_max(S, s % 2, s % 4)

                    def prologue():
                        nv.memset(mbl[C:].bitcast(F32), 0.0).then_inc(filled, 1)
                        nv.memset(oc[C:C + 1, :], 1.0).then_inc(filled, 1)
                        nv.memset(vx[:, :, :, :, D:VW], 1.0).then_inc(filled, 1)
                        nv.memset(ps[:, O_BANK, :], 0.0).then_inc(filled, 1)
                        for k in range(FEATURES):
                            feature(k, k, 0, 0)
                            if k == T_G3:
                                for n in range(0, 7):
                                    step(0, n, 0)

                    def epilogue():
                        for k in range(FINISH):
                            finish(task_base(NP - 1) + FINISH + k, k, NP - 1, 1)

                    pairs(dve, prologue, slot, epilogue)

        NCH = 4
        CH = NTILE // NCH
        with ExitStack() as st:
            zc2 = sb("zc2", [NT, NTILE, C], stack=st)
            sq2 = sb("sq2", [NT, 2, CH, C], stack=st)
            mean2 = sb("mean2", [NT, NTILE], stack=st)
            var2 = sb("var2", [NT, NTILE], stack=st)
            z2 = sb("z2", [NT, 2, 4, C], stack=st)
            z2t = sb("z2t", [C + 1, 2, PW], stack=st)
            hid = sb("hid", [128, 2, 2, PW], stack=st)
            lg = sb("lg", [NT, NTILE, E], stack=st)
            gmax = sb("gmax", [NT, 2], stack=st)
            score = sb("score", [NT, E], stack=st)
            pick = sb("pick", [NT, 2], stack=st)
            emask = sb("emask", [NT, E], stack=st)
            chosen = sb("chosen", [NT, E, C], stack=st)
            gexp = sb("gexp", [NT, NTILE, E], stack=st)
            d_step, d_cent, d_sq, d_sqrt = sem("d_step"), sem("d_cent"), sem("d_sq"), sem("d_sqrt")
            d_ones, z2_ready, z2T_ready, z2t_ready = sem("d_ones"), sem("z2_ready"), sem("z2T_ready"), sem("z2t_ready")
            hid_ready, gelu_done, y2_ready = sem("hid_ready"), sem("gelu_done"), sem("y2_ready")
            y2_free, gexp_ready, res_ready, stored = sem("y2_free"), sem("gexp_ready"), sem("res_ready"), sem("stored")
            d_pick, d_tail = sem("d_pick"), sem("d_tail")
            D_STATS = 4 * NCH

            def by_parity(eng, front, back):
                front(0, 0)
                front(1, 1)
                back(0, 0)
                with eng.Fori(0, NP // 2 - 1) as i:
                    front(2 * i + 2, 0)
                    back(2 * i + 1, 1)
                    front(2 * i + 3, 1)
                    back(2 * i + 2, 0)
                back(NP - 1, 1)

            with nc.Block() as block:
                @block.vector
                def _(dve):
                    nv = nc.vector
                    nv.memset(z2t[C:C + 1], 1.0).then_inc(d_ones, 1)
                    for c in range(NCH):
                        at = slice(c * CH, (c + 1) * CH)
                        nv.tensor_reduce(mean2[:, at], h_all[:, at, :], AX.X, ALU.add).then_inc(d_step, 1)
                        dve.wait_ge(d_step, 2 * c + 1)
                        nv.tensor_scalar(mean2[:, at], mean2[:, at], -1.0 / C, None, ALU.mult).then_inc(d_step, 1)
                    for c in range(NCH):
                        at = slice(c * CH, (c + 1) * CH)
                        dve.wait_ge(d_sq, c + 1)
                        nv.tensor_reduce(var2[:, at], sq2[:, c % 2], AX.X, ALU.add).then_inc(d_step, 1)
                        dve.wait_ge(d_step, 2 * NCH + 2 * c + 1)
                        nv.tensor_scalar(var2[:, at], var2[:, at], 1.0 / C, LN_EPS, ALU.mult, ALU.add).then_inc(d_step, 1)
                    dve.wait_ge(d_sqrt, 1)
                    nv.reciprocal(var2[:], var2[:]).then_inc(d_step, 1)

                    def choose(T, yb):
                        dve.wait_ge(y2_ready, T + 1)
                        gates = ps[0:NT, 3 + 2 * yb, 0:E]
                        gmx = gmax[:, yb:yb + 1]
                        nv.tensor_reduce(gmx, gates, AX.X, ALU.max).then_inc(d_pick, 1)
                        dve.wait_ge(d_pick, 4 * T + 1)
                        nv.tensor_scalar(lg[:, bass.ds(T, 1), :].rearrange("p a e -> p (a e)"), gates, gmx, None, ALU.subtract)
                        nv.scalar_tensor_tensor(out=score[:], in0=gates, scalar=gmx, in1=pri[:],
                                                op0=ALU.is_ge, op1=ALU.mult).then_inc(d_pick, 1)
                        dve.wait_ge(d_pick, 4 * T + 2)
                        nv.tensor_reduce(pick[:, yb:yb + 1], score[:], AX.X, ALU.max).then_inc(d_pick, 1)
                        dve.wait_ge(d_pick, 4 * T + 3)
                        nv.tensor_scalar(emask[:], pri[:], pick[:, yb:yb + 1], None, ALU.is_equal).then_inc(d_pick, 1)
                        dve.wait_ge(d_pick, 4 * T + 4)
                        nv.tensor_tensor(chosen[:].rearrange("p (a e) c -> p a e c", a=2),
                                         ps[0:NT, 3 + 2 * yb:5 + 2 * yb, E:E + 4 * C].rearrange("p a (e c) -> p a e c", e=4),
                                         emask[:].rearrange("p (a e) -> p a e", a=2).unsqueeze(3).broadcast_to([NT, 2, 4, C]),
                                         ALU.mult).then_inc(y2_free, 1)
                        dve.wait_ge(y2_free, T + 1)
                        nv.tensor_reduce(zc2[:, bass.ds(T, 1), :].rearrange("p a c -> p (a c)"),
                                         chosen[:].rearrange("p e c -> p c e"), AX.X, ALU.add).then_inc(d_tail, 1)

                    with dve.Fori(0, NP) as g:
                        for k in range(4):
                            if k == 0:
                                dve.wait_ge(z2_ready, g + 1)
                            choose(4 * g + k, k % 2)

                    dve.wait_ge(gexp_ready, 1)
                    nv.tensor_reduce(mean2[:], gexp[:], AX.X, ALU.add).then_inc(d_step, 1)
                    dve.wait_ge(d_step, D_STATS + 2)
                    nv.reciprocal(mean2[:], mean2[:]).then_inc(d_step, 1)
                    dve.wait_ge(d_step, D_STATS + 3)
                    dve.wait_ge(d_tail, NTILE)
                    for c in range(NCH):
                        at = slice(c * CH, (c + 1) * CH)
                        nv.tensor_tensor(zc2[:, at, :], zc2[:, at, :],
                                         mean2[:, at].unsqueeze(2).broadcast_to([NT, CH, C]), ALU.mult).then_inc(d_step, 1)
                        dve.wait_ge(d_step, D_STATS + 4 + c)
                        nv.tensor_tensor(h_all[:, at, :], h_all[:, at, :], zc2[:, at, :], ALU.add).then_inc(res_ready, 1)

                @block.gpsimd
                def _(pool):
                    gp = nc.gpsimd
                    for c in range(NCH):
                        at = slice(c * CH, (c + 1) * CH)
                        pool.wait_ge(d_step, 2 * c + 2)
                        gp.tensor_tensor(zc2[:, at, :], h_all[:, at, :],
                                         mean2[:, at].unsqueeze(2).broadcast_to([NT, CH, C]), ALU.add).then_inc(d_cent, 1)
                    pool.wait_ge(d_step, D_STATS + 1)

                    def scale(g, par):
                        if not (isinstance(g, int) and g < 2):
                            pool.wait_ge(z2T_ready, g - 1)
                        gp.tensor_tensor(z2[:, par], zc2[:, bass.ds(4 * g, 4), :],
                                         var2[:, bass.ds(4 * g, 4)].unsqueeze(2).broadcast_to([NT, 4, C]),
                                         ALU.mult).then_inc(z2_ready, 1)

                    scale(0, 0)
                    scale(1, 1)
                    with pool.Fori(0, NP // 2 - 1) as i:
                        for par in range(2):
                            scale(2 * i + 2 + par, par)

                @block.scalar
                def _(act):
                    for c in range(NCH):
                        act.wait_ge(d_cent, c + 1)
                        if c >= 2:
                            act.wait_ge(d_step, 2 * NCH + 2 * (c - 2) + 1)
                        nc.scalar.activation(sq2[:, c % 2], zc2[:, c * CH:(c + 1) * CH, :], ACT.Square).then_inc(d_sq, 1)
                    act.wait_ge(d_step, D_STATS)
                    nc.scalar.activation(var2[:], var2[:], ACT.Sqrt).then_inc(d_sqrt, 1)

                    def front(g, par):
                        act.wait_ge(z2T_ready, g + 1)
                        for k in range(2):
                            nc.scalar.copy(z2t[0:C, par].rearrange("c (t k n) -> c t k n", k=2, n=NT)[:, :, k, :],
                                           ps[k * C:(k + 1) * C, 0, 0:N].rearrange("c (t n) -> c t n", n=NT)
                                           ).then_inc(z2t_ready, 1)
                        act.wait_ge(hid_ready, g + 1)
                        if not (isinstance(g, int) and g < 2):
                            act.wait_ge(y2_ready, 4 * g - 4)
                        nc.scalar.activation(hid[:, par], ps[:, 1:3, 0:PW], ACT.Gelu).then_inc(gelu_done, 1)

                    front(0, 0)
                    front(1, 1)
                    with act.Fori(0, NP // 2 - 1) as i:
                        for par in range(2):
                            front(2 * i + 2 + par, par)
                    act.wait_ge(y2_free, NTILE)
                    nc.scalar.activation(gexp[:], lg[:], ACT.Exp).then_inc(gexp_ready, 1)

                @block.tensor
                def _(pe):
                    pe.wait_ge(d_ones, 1)

                    def front(g, par):
                        pe.wait_ge(z2_ready, g + 1)
                        pe.wait_ge(z2t_ready, 2 * g)
                        for t in range(2):
                            mm = pe.transpose(ps[:, 0, t * NT:(t + 1) * NT],
                                              z2[:, par, 2 * t:2 * t + 2, :].rearrange("p t c -> p (t c)"), ident[0:NT, 0:NT])
                        mm.then_inc(z2T_ready, 1)
                        pe.wait_ge(z2t_ready, 2 * g + 2)
                        pe.wait_ge(gelu_done, g)
                        for c in range(2):
                            mm = pe.matmul(ps[:, 1 + c, 0:PW], w[:, W_1 + 128 * c:W_1 + 128 * (c + 1)], z2t[:, par],
                                           start=True, stop=True)
                        mm.then_inc(hid_ready, 1)

                    def back(g, par):
                        pe.wait_ge(gelu_done, g + 1)
                        for k in range(4):
                            if not (isinstance(g, int) and g == 0 and k < 2):
                                pe.wait_ge(y2_free, 4 * g + k - 1)
                            for a, (lo, hi) in enumerate(((0, E + 4 * C), (E + 4 * C, E + 8 * C))):
                                off = 0 if a == 0 else E
                                dst = ps[0:NT, 3 + 2 * (k % 2) + a, off:off + hi - lo]
                                pe.matmul(dst, ones3[:], wb3[:, lo:hi], start=True, stop=False)
                                for c in range(2):
                                    mm = pe.matmul(dst, hid[:, par, c, k * NT:(k + 1) * NT], wl[:, c, lo:hi],
                                                   start=False, stop=c == 1)
                            mm.then_inc(y2_ready, 1)

                    by_parity(pe, front, back)

                @block.sync
                def _(sp):
                    nb = CH // 2
                    for c in range(NCH):
                        sp.wait_ge(res_ready, c + 1)
                        sp.dma_start(out[c * nb:(c + 1) * nb].rearrange("b (t p) c -> p (b t) c", t=2),
                                     h_all[:, c * CH:(c + 1) * CH, :]).then_inc(stored, 16)
                    sp.wait_ge(stored, 16 * NCH)


def kernel(**inputs):
    import concourse.bacc as bacc
    from concourse.bass_utils import run_bass_kernel_spmd as run

    a = {k: np.asarray(v) for k, v in inputs.items()}
    arrays = lay_out(a)
    B = a["x"].shape[0]
    nc = bacc.Bacc("TRN2", target_bir_lowering=False, num_devices=1)
    args = [nc.dram_tensor(n, v.shape, mybir.dt.from_np(v.dtype), kind="ExternalInput").ap()
            for n, v in arrays.items()]
    o = nc.dram_tensor("out_dram", (B, N, C), F32, kind="ExternalOutput").ap()
    audio_tower(nc, *args, o)
    r = run(nc, [arrays], core_ids=[0])
    return r.results[0]["out_dram"]


def lay_out(a):
    f = np.float32
    row = np.arange(128)
    half, h, d = row // C, row % C // D, row % D

    def with_bias(wm, bias):
        return np.concatenate([wm, bias[None]], 0)

    wqkv = with_bias(a["L0_attn_w_qkv"].T, a["L0_attn_b_qkv"])
    twice = h * D + d
    cols = [twice] + [h * D + (d + 2 * t + 1 + half) % D for t in range(2)]
    cols = np.concatenate(cols)
    wf = np.concatenate([wqkv[:, cols], wqkv[:, C + cols], wqkv[:, 2 * C:]], 1)
    w128 = np.concatenate([wf[:C], wf[:C]], 0)
    fbias = wf[C, :2 * FT * 128].reshape(2 * FT, 128).T
    vbias = np.broadcast_to(wf[C, 2 * FT * 128:], (128, C))
    w65 = np.concatenate([wqkv[:, 0:2 * C],
                          with_bias(a["L0_attn_w_proj"].T, a["L0_attn_b_proj"]),
                          with_bias(a["L0_ffn_W1"], a["L0_ffn_b1"])], 1)
    kconv = a["L0_tok_kernel"].transpose(1, 0, 2).reshape(CIN, TAPS * C)
    chan = np.stack([a["L0_tok_bias"], a["L0_tok_beta"], a["L0_tok_moving_mean"], a["L0_tok_moving_var"]])
    chan = np.broadcast_to(chan, (128, 4, C))
    wall = np.concatenate([a["L0_ffn_Wg"]] + list(a["L0_ffn_Wd"]), 1).reshape(2, 128, E + E * C).transpose(1, 0, 2)
    wbias = np.concatenate([a["L0_ffn_bg"], a["L0_ffn_bd"].reshape(-1)])[None]

    low = half == 1
    channel = np.stack([np.stack([H + h, H + h, np.where(low, h, H + h)], 1), np.repeat(2 * H + h[:, None], FT, 1)], 1)
    pairs_counted = np.ones((128, 2, FT), f)
    pairs_counted[:, :, 0] = 2
    pairs_counted[~low, :, 1] = 2
    pairs_counted[low, 1, 2] = 0
    scales = np.broadcast_to(a["L0_attn_riem_scale"], (128, 2, FT)).copy()
    scales[:, 1] = a["L0_attn_grassman_scale"]
    scales[low, 0, 2] = a["L0_attn_scale"]
    mixw = a["L0_attn_conv_w"].T[channel]
    flat = channel.reshape(128, 2 * FT)
    mixbn = np.stack([a["L0_attn_bn_gamma"][flat], a["L0_attn_bn_var"][flat], scales.reshape(128, -1),
                      pairs_counted.reshape(128, -1)], 1)
    cw = np.broadcast_to(with_bias(a["L0_attn_conv_w"].T, a["L0_attn_conv_b"]).T, (128, H, 25))
    cbn = np.broadcast_to(np.stack([a["L0_attn_bn_gamma"], a["L0_attn_bn_var"], a["L0_attn_bn_mean"],
                                    a["L0_attn_bn_beta"]]), (128, 4, 24))
    consts = np.zeros((128, 224), f)
    consts[:, 0:128] = np.eye(128)
    consts[row, 128 + row // D] = 1
    consts[:, 144:208] = np.eye(D).reshape(-1)
    consts[row, 216 + h] = 1
    consts[:, 208:216] = np.arange(E, 0, -1)
    named = dict(x=a["x"], w65=w65, w128=w128, fbias=fbias, vbias=vbias, kconv=kconv, chan=chan, wall=wall, wbias=wbias, mixw=mixw, mixbn=mixbn,
                 cw=cw, cbn=cbn, consts=consts)
    return {f"in_{k}_dram": np.ascontiguousarray(v) for k, v in named.items()}
```

```python
from contextlib import ExitStack

import numpy as np

import concourse.bass as bass
from concourse import mybir

F32 = mybir.dt.float32
F32R = mybir.dt.float32r
BF16 = mybir.dt.bfloat16
ALU = mybir.AluOpType
ACT = mybir.ActivationFunctionType
AX = mybir.AxisListType

H, D = 8, 8
C = H * D
CIN = 128
TAPS = 3
TIN = 250
N = TIN - TAPS + 1
NT = N // 2
XT = TIN // 2
PW = 2 * N
E = 8
HID = 256
FT = 3
OG = 4
UH = 2
VW = D + 1
SLOT = 32
BN_EPS, TOK_EPS, LN_EPS = 1e-5, 1e-3, 1e-5

V_Q, V_K, V_V, V_END = 0, FT * 128, 2 * FT * 128, 2 * FT * 128 + C
B_QK, B_END = E + E * C, E + E * C + 4 * C


def audio_tower(nc, x, wproj, w128, wqk, w1, fbias, vbias, kconv, chan, wall, wbias, mixw, mixbn, cw, cbn, consts, out):
    B = x.shape[0]
    NP = B // 2
    NG = B // 4
    G16 = B // 16
    NTILE = 2 * B

    with ExitStack() as ctx:
        def sb(name, shape, dt=F32, stack=ctx):
            return stack.enter_context(nc.sbuf_tensor(name, shape, dt))

        def sem(name):
            return ctx.enter_context(nc.semaphore(name))

        zt_dram = nc.dram_tensor("zt_scratch", (NP, 2, 2, C, 2, NT), F32, kind="Internal").ap()
        gram_dram = nc.dram_tensor("gram_scratch", (2, B, C + 1, C), F32, kind="Internal").ap()
        top_dram = nc.dram_tensor("top_scratch", (2, D, B, C), F32, kind="Internal").ap()
        m_dram = nc.dram_tensor("m_scratch", (B, H, D, D), F32, kind="Internal").ap()

        ps = ctx.enter_context(nc.psum_tensor("ps", [128, 8, 512], F32))

        h_all = sb("h_all", [NT, NTILE, C])
        mean2 = sb("mean2", [NT, NTILE])
        var2 = sb("var2", [NT, NTILE])
        wp = sb("wp", [C + 1, C])
        ident = sb("ident", [128, 128])
        eye8 = sb("eye8", [128, 64])
        bmask = sb("bmask", [128, H])
        mix = sb("mix", [128, 2, FT, H])
        shift_o = sb("shift_o", [NT, H])
        mch = sb("mch", [128, B, 12], F32R)
        mcl = sb("mcl", [C, B, 12], F32R)
        whi = sb("whi", [128, V_END], F32R)
        wlo = sb("wlo", [128, V_END], F32R)
        fb = sb("fb", [128, 2 * FT + 2])
        vb = sb("vb", [NT, C])
        pri = sb("pri", [NT, E])
        wb3 = sb("wb3", [128, B_END], BF16)
        ones3 = sb("ones3", [128, NT], BF16)

        with ExitStack() as st:
            chan_sb = sb("chan_sb", [NT, 4, C], stack=st)
            aff = sb("aff", [NT, 3, C], stack=st)
            kc = sb("kc", [CIN, TAPS * C], stack=st)
            kq = sb("kq", [CIN, TAPS * C], BF16, stack=st)
            mw = sb("mw", [128, 2, FT, H], stack=st)
            mbn = sb("mbn", [128, 4, 2 * FT], stack=st)
            minv = sb("minv", [128, 2 * FT], stack=st)
            cw_sb = sb("cw_sb", [NT, H, 25], stack=st)
            cbn_sb = sb("cbn_sb", [NT, 4, 24], stack=st)
            cinv = sb("cinv", [NT, 24], stack=st)
            wb_f = sb("wb_f", [1, 3, B_END], stack=st)
            wb_b = sb("wb_b", [1, 3, B_END], BF16, stack=st)
            xt = sb("xt", [XT, 2, 8, CIN], stack=st)
            xs = sb("xs", [CIN, 2, 2, 2 * TIN], BF16, stack=st)
            ysc = sb("ysc", [NT, 2, 8, C], stack=st)
            hg = sb("hg", [NT, 2, 8, C], stack=st)
            stat = sb("stat", [NT, 2, 5, 8], stack=st)
            zc = sb("zc", [NT, 2, 8, C], stack=st)
            zsq = sb("zsq", [NT, 2, 8, C], stack=st)
            z = sb("z", [NT, 2, 8, C], stack=st)
            zh = sb("zh", [128, 2, 4 * NT], F32R, stack=st)
            zl = sb("zl", [128, 2, 4 * NT], F32R, stack=st)
            qkt = sb("qkt", [NT, 2, 8, 2 * C], stack=st)
            graw = sb("graw", [128, 2, 4, C], stack=st)
            wqk_f = sb("wqk_f", [128, 4 * C], stack=st)
            wqkh = sb("wqkh", [128, 4 * C], F32R, stack=st)
            wqkl = sb("wqkl", [128, 4 * C], F32R, stack=st)
            wf = sb("wf", [128, V_END], stack=st)
            urgent_loaded, small_loaded = sem("urgent_loaded"), sem("small_loaded")
            a_early, a_late = sem("a_early"), sem("a_late")
            a_sqrt, late_sqrt, a_ones = sem("a_sqrt"), sem("late_sqrt"), sem("a_ones")
            wb_moved = sem("wb_moved")
            x_in = [sem("x_in_even"), sem("x_in_odd")]
            xT_ready, xs_ready, y_ready = sem("xT_ready"), sem("xs_ready"), sem("y_ready")
            ysc_ready, hg_ready, h_kept = sem("ysc_ready"), sem("hg_ready"), sem("h_kept")
            sum_ready, mean_ready, zc_ready = sem("sum_ready"), sem("mean_ready"), sem("zc_ready")
            zsq_ready, ssq_ready, var_ready = sem("zsq_ready"), sem("ssq_ready"), sem("var_ready")
            std_ready, rstd_ready, z_ready = sem("std_ready"), sem("rstd_ready"), sem("z_ready")
            zT_ready, zh_ready, zl_ready = sem("zT_ready"), sem("zh_ready"), sem("zl_ready")
            qk_ready, qkt_ready = sem("qk_ready"), sem("qkt_ready")
            gram_ready, graw_ready = sem("gram_ready"), sem("graw_ready")
            zt_out = [sem("zt_out_even"), sem("zt_out_odd")]
            top_out = [sem("top_out_even"), sem("top_out_odd")]
            gram_out = [sem("gram_out_even"), sem("gram_out_odd")]
            XT_BANK, Y_BANK, ZT_BANK, QK_BANK, G_BANK = 0, 2, 3, 4, 6
            DEPTH = 8

            def pipeline(eng, parts):
                def slot(i, odd):
                    for lag, do in parts:
                        g = i - lag
                        if not isinstance(i, int) or 0 <= g < NG:
                            do(g, (odd + lag) % 2)

                start = min(DEPTH, NG)
                for i in range(start):
                    slot(i, i % 2)
                if NG > start:
                    with eng.Fori(0, (NG - start) // 2) as i:
                        for odd in range(2):
                            slot(2 * i + start + odd, odd)
                for i in range(NG, NG + max(lag for lag, _ in parts)):
                    slot(i, i % 2)

            EARLY, LATE = 6, 23

            with nc.Block() as block:
                @block.sync
                def _(sp):
                    def load_x(g, par):
                        if not (isinstance(g, int) and g < 2):
                            sp.wait_ge(xT_ready, 2 * g - 2)
                        src = x[bass.ds(4 * g, 4)].rearrange("b (t p) c -> p (b t) c", p=XT)
                        sp.dma_start(xt[:, par], src).then_inc(x_in[par], 16)

                    def store_z(g, par):
                        sp.wait_ge(zl_ready, g + 1)
                        for k, src in enumerate((zh, zl)):
                            sp.dma_start(zt_dram[bass.ds(2 * g, 2), k].rearrange("a t c b n -> (t c) a (b n)"),
                                         src[:, par].bitcast(F32).rearrange("p (a n) -> p a n", a=2)
                                         ).then_inc(zt_out[par], 16)

                    def store_top(g, par):
                        sp.wait_ge(qkt_ready, 2 * g + 2)
                        for k in range(2):
                            sp.dma_start(top_dram[k, :, bass.ds(4 * g, 4), :],
                                         qkt[0:D, par, 0:8:2, k * C:(k + 1) * C]).then_inc(top_out[par], 16)

                    def store_gram(g, par):
                        sp.wait_ge(graw_ready, g + 1)
                        for k in range(2):
                            sp.dma_start(gram_dram[k, bass.ds(4 * g, 4), 0:C, :].rearrange("b r c -> r b c"),
                                         graw[k * C:(k + 1) * C, par]).then_inc(gram_out[par], 16)

                    def bias_parts(g, par):
                        if isinstance(g, int) and g == 1:
                            sp.wait_ge(a_late, 5)
                            sp.wait_ge(a_ones, 3)
                            for k in range(3):
                                sp.dma_start(wb3[k:k + 1, :], wb_b[:, k, :]).then_inc(wb_moved, 16)

                    sp.dma_start(ident[:], consts[:, 0:128]).then_inc(urgent_loaded, 16)
                    sp.dma_start(chan_sb[:], chan[0:NT]).then_inc(urgent_loaded, 16)
                    sp.dma_start(kc[:], kconv).then_inc(urgent_loaded, 16)
                    pipeline(sp, ((0, load_x), (2, bias_parts), (6, store_z), (7, store_top), (8, store_gram)))
                    for done in zt_out + top_out + gram_out:
                        sp.wait_ge(done, 16 * NG)

                @block.tensor
                def _(pe):
                    pe.wait_ge(urgent_loaded, 16 * 3)

                    def turn_x(g, par):
                        pe.wait_ge(x_in[par], 8 * g + 16 - 8 * par)
                        pe.wait_ge(xs_ready, 2 * g)
                        for k in range(8):
                            mm = pe.transpose(ps[:, XT_BANK + k // 4, (k % 4) * XT:(k % 4 + 1) * XT], xt[:, par, k, :],
                                              ident[0:XT, 0:XT])
                            if k % 4 == 3:
                                mm.then_inc(xT_ready, 1)

                    def conv(g, par):
                        pe.wait_ge(a_early, 3)
                        pe.wait_ge(xs_ready, 2 * g + 2)
                        pe.wait_ge(ysc_ready, g)
                        for k in range(8):
                            for tap in range(TAPS):
                                at = (k // 2 % 2) * TIN + (k % 2) * NT + tap
                                mm = pe.matmul(ps[0:NT, Y_BANK, k * C:(k + 1) * C], xs[:, par, k // 4, at:at + NT],
                                               kq[:, tap * C:(tap + 1) * C], start=tap == 0, stop=tap == TAPS - 1)
                        mm.then_inc(y_ready, 1)

                    def turn_z(g, par):
                        pe.wait_ge(z_ready, g + 1)
                        pe.wait_ge(zl_ready, g)
                        for k in range(4):
                            mm = pe.transpose(ps[:, ZT_BANK, k * NT:(k + 1) * NT],
                                              z[:, par, 2 * k:2 * k + 2, :].rearrange("p t c -> p (t c)"), ident[0:NT, 0:NT])
                        mm.then_inc(zT_ready, 1)

                    def project(g, par):
                        if isinstance(g, int) and g == 0:
                            pe.wait_ge(a_late, 7)
                            pe.wait_ge(wb_moved, 48)
                        pe.wait_ge(zl_ready, g + 1)
                        pe.wait_ge(qkt_ready, 2 * g)
                        for k in range(4):
                            dst = ps[0:NT, QK_BANK + k // 2, (k % 2) * 4 * C:(k % 2 + 1) * 4 * C]
                            at = slice(k * NT, (k + 1) * NT)
                            pe.matmul(dst, ones3[:], wb3[:, B_QK:B_END], start=True, stop=False)
                            pe.matmul(dst, zl[:, par, at], wqkh[:], start=False, stop=False)
                            pe.matmul(dst, zh[:, par, at], wqkl[:], start=False, stop=False)
                            mm = pe.matmul(dst, zh[:, par, at], wqkh[:], start=False, stop=True)
                        mm.then_inc(qk_ready, 1)

                    def grams(g, par):
                        pe.wait_ge(qkt_ready, 2 * g + 2)
                        pe.wait_ge(graw_ready, g)
                        for b in range(4):
                            for t in range(2):
                                for k in range(2):
                                    at = slice(k * C, (k + 1) * C)
                                    mm = pe.matmul(ps[at, G_BANK, b * C:(b + 1) * C], qkt[:, par, 2 * b + t, at],
                                                   qkt[:, par, 2 * b + t, at], start=t == 0, stop=t == 1)
                        mm.then_inc(gram_ready, 1)

                    pipeline(pe, ((0, turn_x), (1, conv), (4, turn_z), (5, project), (6, grams)))

                @block.scalar
                def _(act):
                    act.wait_ge(a_early, 1)
                    nc.scalar.activation(aff[:, 0, :], chan_sb[:, 3, :], ACT.Sqrt).then_inc(a_sqrt, 1)
                    for dst, src in ((wb_f[:, 0, :], wbias), (wqk_f[:], wqk), (mw[:], mixw),
                                     (mbn[:], mixbn), (cw_sb[:], cw[0:NT]), (cbn_sb[:], cbn[0:NT]), (wf[:], w128),
                                     (wp[:], wproj), (eye8[:], consts[:, 144:208]), (pri[:], consts[0:NT, 208:216]),
                                     (fb[:], fbias), (vb[:], vbias[0:NT]), (bmask[:], consts[:, 216:224])):
                        act.dma_start(dst, src).then_inc(small_loaded, 16)

                    def mixing(g, par):
                        if isinstance(g, int) and g == 2:
                            act.wait_ge(a_late, 9)
                            nc.scalar.activation(minv[:], mbn[:, 1, :], ACT.Sqrt).then_inc(late_sqrt, 1)
                            nc.scalar.activation(cinv[:], cbn_sb[:, 1, :], ACT.Sqrt).then_inc(late_sqrt, 1)

                    def keep_h(g, par):
                        act.wait_ge(hg_ready, g + 1)
                        nc.scalar.copy(h_all[:, bass.ds(8 * g, 8), :], hg[:, par]).then_inc(h_kept, 1)

                    def deviation(g, par):
                        act.wait_ge(var_ready, g + 1)
                        nc.scalar.activation(stat[:, par, 4, :], stat[:, par, 3, :], ACT.Sqrt).then_inc(std_ready, 1)

                    def squares(g, par):
                        act.wait_ge(zc_ready, g + 1)
                        if not (isinstance(g, int) and g < 2):
                            act.wait_ge(ssq_ready, g - 1)
                        nc.scalar.activation(zsq[:, par], zc[:, par], ACT.Square).then_inc(zsq_ready, 1)

                    def split_z(g, par):
                        act.wait_ge(zT_ready, g + 1)
                        if not (isinstance(g, int) and g < 2):
                            act.wait_ge(zt_out[par], 16 * g - 16 * par)
                        nc.scalar.copy(zh[:, par], ps[:, ZT_BANK, 0:4 * NT]).then_inc(zh_ready, 1)

                    def keep_qk(g, par):
                        act.wait_ge(qk_ready, g + 1)
                        if not (isinstance(g, int) and g < 2):
                            act.wait_ge(gram_ready, g - 1)
                            act.wait_ge(top_out[par], 16 * g - 16 * par)
                        for k in range(2):
                            nc.scalar.copy(qkt[:, par, 4 * k:4 * k + 4, :],
                                           ps[0:NT, QK_BANK + k, :].rearrange("p (t c) -> p t c", t=4)
                                           ).then_inc(qkt_ready, 1)

                    def keep_gram(g, par):
                        act.wait_ge(gram_ready, g + 1)
                        if not (isinstance(g, int) and g < 2):
                            act.wait_ge(gram_out[par], 16 * g - 16 * par)
                        nc.scalar.copy(graw[:, par], ps[:, G_BANK, 0:4 * C].rearrange("p (b c) -> p b c", b=4)
                                       ).then_inc(graw_ready, 1)

                    pipeline(act, ((3, deviation), (2, keep_h), (1, mixing), (4, split_z), (5, keep_qk), (6, keep_gram),
                                   (2, squares)))

                @block.gpsimd
                def _(pool):
                    gp = nc.gpsimd
                    gp.memset(wb3[:], 0.0).then_inc(a_ones, 1)
                    gp.memset(ones3[:], 0.0).then_inc(a_ones, 1)
                    pool.wait_ge(a_ones, 2)
                    gp.memset(ones3[0:3, :], 1.0).then_inc(a_ones, 1)

                    def col(ap):
                        return ap.unsqueeze(2).broadcast_to([NT, 8, C])

                    def center(g, par):
                        pool.wait_ge(mean_ready, g + 1)
                        gp.tensor_tensor(zc[:, par], hg[:, par], col(stat[:, par, 1, :]), ALU.add).then_inc(zc_ready, 1)

                    def scale(g, par):
                        pool.wait_ge(rstd_ready, g + 1)
                        if not (isinstance(g, int) and g < 2):
                            pool.wait_ge(zT_ready, g - 1)
                        gp.tensor_tensor(z[:, par], zc[:, par], col(stat[:, par, 4, :]), ALU.mult).then_inc(z_ready, 1)

                    def shift(g, par):
                        pool.wait_ge(ysc_ready, g + 1)
                        if not (isinstance(g, int) and g < 2):
                            pool.wait_ge(h_kept, g - 1)
                        gp.tensor_tensor(hg[:, par], ysc[:, par], aff[:, 2, :].unsqueeze(1).broadcast_to([NT, 8, C]),
                                         ALU.add).then_inc(hg_ready, 1)

                    pipeline(pool, ((2, center), (3, scale), (1, shift)))

                @block.vector
                def _(dve):
                    nv = nc.vector

                    def linker(done):
                        steps = [0]

                        def link(ins):
                            steps[0] += 1
                            ins.then_inc(done, 1)
                            dve.wait_ge(done, steps[0])

                        return link, steps

                    link, early = linker(a_early)
                    dve.wait_ge(urgent_loaded, 16 * 3)
                    link(nv.tensor_scalar(chan_sb[:, 3, :], chan_sb[:, 3, :], TOK_EPS, None, ALU.add))
                    link(nv.tensor_scalar(kc[:], kc[:], 0.0, 0.5, ALU.is_ge, ALU.subtract))
                    link(nv.tensor_scalar(kq[:], kc[:], 4.0, None, ALU.mult))
                    dve.wait_ge(a_sqrt, 1)
                    link(nv.reciprocal(aff[:, 1, :], aff[:, 0, :]))
                    link(nv.tensor_tensor(aff[:, 2, :], chan_sb[:, 0, :], chan_sb[:, 2, :], ALU.subtract))
                    link(nv.tensor_tensor(aff[:, 2, :], aff[:, 2, :], aff[:, 1, :], ALU.mult))
                    link(nv.tensor_tensor(aff[:, 2, :], aff[:, 2, :], chan_sb[:, 1, :], ALU.add))
                    assert early[0] == EARLY + 1, early[0]

                    link_late, late = linker(a_late)

                    def bias_parts():
                        link = link_late
                        link(nv.tensor_copy(wb_b[:, 0, :], wb_f[:, 0, :]))
                        link(nv.tensor_tensor(wb_f[:, 1, :], wb_f[:, 0, :], wb_b[:, 0, :], ALU.subtract))
                        link(nv.tensor_copy(wb_b[:, 1, :], wb_f[:, 1, :]))
                        link(nv.tensor_tensor(wb_f[:, 2, :], wb_f[:, 1, :], wb_b[:, 1, :], ALU.subtract))
                        link(nv.tensor_copy(wb_b[:, 2, :], wb_f[:, 2, :]))

                    def qk_parts():
                        link = link_late
                        link(nv.tensor_copy(wqkh[:], wqk_f[:]))
                        link(nv.tensor_tensor(wqkl[:], wqk_f[:], wqkh[:].bitcast(F32), ALU.subtract))
                        link(nv.tensor_scalar(mbn[:, 1, :], mbn[:, 1, :], BN_EPS, None, ALU.add))
                        link(nv.tensor_scalar(cbn_sb[:, 1, :], cbn_sb[:, 1, :], BN_EPS, None, ALU.add))

                    def feature_parts():
                        link = link_late
                        link(nv.tensor_copy(whi[:], wf[:]))
                        link(nv.memset(wlo[C:, :].bitcast(F32), 0.0))
                        link(nv.tensor_tensor(wlo[0:C, :], wf[0:C, :], whi[0:C, :].bitcast(F32), ALU.subtract))

                    def mixing():
                        link = link_late
                        dve.wait_ge(late_sqrt, 2)
                        link(nv.reciprocal(minv[:], minv[:]))
                        for j in (0, 2, 3):
                            link(nv.tensor_tensor(minv[:], minv[:], mbn[:, j, :], ALU.mult))
                        mi = minv[:].rearrange("p (a t) -> p a t", a=2).unsqueeze(3).broadcast_to([128, 2, FT, H])
                        link(nv.tensor_tensor(mix[:], mw[:], mi, ALU.mult))
                        link(nv.reciprocal(cinv[:], cinv[:]))
                        link(nv.tensor_tensor(cinv[:], cinv[:], cbn_sb[:, 0, :], ALU.mult))
                        link(nv.tensor_tensor(cinv[:], cinv[:], cbn_sb[:, 2, :], ALU.mult))
                        link(nv.tensor_tensor(cinv[:], cbn_sb[:, 3, :], cinv[:], ALU.subtract))
                        link(nv.tensor_tensor(cw_sb[:, :, 0:24], cw_sb[:, :, 0:24],
                                              cinv[:].unsqueeze(1).broadcast_to([NT, H, 24]), ALU.mult))
                        link(nv.tensor_reduce(shift_o[:], cw_sb[:], AX.X, ALU.add))
                        assert late[0] == LATE, late[0]

                    def weights(g, par):
                        if isinstance(g, int) and g < 4:
                            if g == 0:
                                dve.wait_ge(small_loaded, 16 * 13)
                            (bias_parts, qk_parts, feature_parts, mixing)[g]()

                    def signs(g, par):
                        if not (isinstance(g, int) and g < 2):
                            dve.wait_ge(y_ready, g - 1)
                        for k in range(2):
                            dve.wait_ge(xT_ready, 2 * g + 1 + k)
                            nv.tensor_scalar(xs[:, par, k, :], ps[:, XT_BANK + k, 0:2 * TIN], 0.0, 0.5, ALU.is_ge,
                                             ALU.subtract).then_inc(xs_ready, 1)

                    def batch_norm(g, par):
                        dve.wait_ge(y_ready, g + 1)
                        if not (isinstance(g, int) and g < 2):
                            dve.wait_ge(hg_ready, g - 1)
                        nv.tensor_tensor(ysc[:, par], ps[0:NT, Y_BANK, :].rearrange("p (t c) -> p t c", c=C),
                                         aff[:, 1, :].unsqueeze(1).broadcast_to([NT, 8, C]), ALU.mult
                                         ).then_inc(ysc_ready, 1)

                    def mean(g, par):
                        dve.wait_ge(hg_ready, g + 1)
                        nv.tensor_reduce(stat[:, par, 0, :], hg[:, par], AX.X, ALU.add).then_inc(sum_ready, 1)
                        dve.wait_ge(sum_ready, g + 1)
                        if not (isinstance(g, int) and g < 2):
                            dve.wait_ge(zc_ready, g - 1)
                        nv.tensor_scalar(stat[:, par, 1, :], stat[:, par, 0, :], -1.0 / C, None, ALU.mult
                                         ).then_inc(mean_ready, 1)

                    def variance(g, par):
                        dve.wait_ge(zsq_ready, g + 1)
                        nv.tensor_reduce(stat[:, par, 2, :], zsq[:, par], AX.X, ALU.add).then_inc(ssq_ready, 1)
                        dve.wait_ge(ssq_ready, g + 1)
                        nv.tensor_scalar(stat[:, par, 3, :], stat[:, par, 2, :], 1.0 / C, LN_EPS, ALU.mult,
                                         ALU.add).then_inc(var_ready, 1)

                    def inverse(g, par):
                        dve.wait_ge(std_ready, g + 1)
                        nv.reciprocal(stat[:, par, 4, :], stat[:, par, 4, :]).then_inc(rstd_ready, 1)

                    def split_z(g, par):
                        dve.wait_ge(zh_ready, g + 1)
                        nv.tensor_tensor(zl[:, par], ps[:, ZT_BANK, 0:4 * NT], zh[:, par].bitcast(F32),
                                         ALU.subtract).then_inc(zl_ready, 1)

                    pipeline(dve, ((3, variance), (2, mean), (3, inverse), (0, signs), (1, batch_norm), (4, split_z),
                                   (1, weights)))

        FEATURES, FINISH = 10, 4
        NS, UNITS = 16, H // UH
        TILES = UH * FT
        ALL_TILES = TILES * UNITS * NP
        T_BANK, O_BANK, SIDE = 4, 6, 7
        T_Q1, T_Q2, T_Q3, T_V, T_G1, T_G2, T_G3, T_K1, T_K2, T_K3 = range(FEATURES)
        PROLOGUE = (T_Q1, T_Q2, T_Q3, T_V, T_K1, T_K2, T_K3, T_G1, T_G2, T_G3)
        STEPS_AT = ((1, 2), (3,), (4, 5), (6,))

        def task_base(p):
            if isinstance(p, int) and p == 0:
                return FEATURES
            return 2 * FEATURES + (FEATURES + FINISH) * (p - 1)

        def slot_task(p, par, s, first, last, feature, finish):
            if s < FEATURES:
                if not last:
                    feature(task_base(p) + s, s, p + 1, 1 - par)
            elif not first and s < FEATURES + FINISH:
                k = s - FEATURES
                finish(task_base(p) + k + (0 if last else FEATURES), k, p - 1, 1 - par)

        def steps(p, s, do):
            for k in STEPS_AT[s % 4]:
                do(p, (s // 4 + 1) * TILES + k)

        def tile_of(p, k):
            n = TILES * UNITS * p + k
            shift, k = divmod(k, TILES * UNITS)
            unit, k = divmod(k, TILES)
            exists = n >= 0 and n < ALL_TILES if isinstance(n, int) else True
            return n, exists, shift, unit, k // FT, k % FT

        ON_POOL = (0, 1, 2, 3, 5)

        def is_on_pool(k):
            return k % TILES in ON_POOL

        def lows(p, k, on_pool):
            share = len(ON_POOL) if on_pool else TILES - len(ON_POOL)
            return share * (UNITS * p + k // TILES) + sum(is_on_pool(j) == on_pool for j in range(k % TILES + 1))

        def pairs(eng, prologue, slot, epilogue):
            prologue()
            for s in range(NS):
                slot(0, 0, s, True, False)
            with eng.Fori(0, NP // 2 - 1) as i:
                for par, p in ((1, 2 * i + 1), (0, 2 * i + 2)):
                    for s in range(NS):
                        slot(p, par, s, False, False)
            for s in range(NS):
                slot(NP - 1, 1, s, False, True)
            epilogue()

        with ExitStack() as st:
            zs = sb("zs", [128, 2, PW], F32R, stack=st)
            qa = sb("qa", [128, PW], stack=st)
            ga = sb("ga", [128, PW], stack=st)
            qs = sb("qs", [128, PW], F32R, stack=st)
            mbh = sb("mbh", [128, 2, 6, C], F32R, stack=st)
            mbl = sb("mbl", [128, 2, 6, C], F32R, stack=st)
            fq = sb("fq", [128, 2, FT, PW], stack=st)
            fg = sb("fg", [128, 2, FT, PW], stack=st)
            kx = sb("kx", [128, 2, PW], stack=st)
            fkh = sb("fkh", [128, 2, FT, PW], F32R, stack=st)
            fkl = sb("fkl", [128, 2, FT, PW], F32R, stack=st)
            fx = sb("fx", [128, 4, PW], stack=st)
            Fh = sb("Fh", [128, 2, UH, FT, PW], F32R, stack=st)
            Fl = sb("Fl", [128, 2, UH, FT, PW], F32R, stack=st)
            prob = sb("prob", [NT, 2, UH, N], stack=st)
            probT = sb("probT", [NT, 2, 2, OG, N], stack=st)
            nmax = sb("nmax", [NT, 2, UH], stack=st)
            nms = sb("nms", [NT, 2, UH], stack=st)
            ebias = sb("ebias", [NT, 2, UH], stack=st)
            vx = sb("vx", [NT, 2, 4, H, VW], stack=st)
            oT = sb("oT", [128, 2, 2, PW], stack=st)
            rden = sb("rden", [NT, 2 * H], stack=st)
            otok = sb("otok", [NT, 4, C], stack=st)
            oc = sb("oc", [C + 1, PW], stack=st)
            hn = sb("hn", [NT, 4, C], stack=st)
            hc = sb("hc", [NT, 4, C], stack=st)
            stat2 = sb("stat2", [NT, 4, 4], stack=st)

            GP = 2 * G16

            def carver(space):
                taken = [0]

                def carve(*shape):
                    at, n = taken[0], int(np.prod(shape))
                    taken[0] += n
                    names = "abc"[:len(shape)]
                    return space[:, at:at + n].rearrange(f"p ({' '.join(names)}) -> p {' '.join(names)}",
                                                         **dict(zip(names, shape)))

                return carve

            carve = carver(fg[:].rearrange("p a f n -> p (a f n)"))
            gw = carve(GP, D, 2 * D)
            gl, av = carve(GP, D, D), carve(GP, D, D)
            ri = carve(GP, D, D)
            fac, piv, rs, sg, sn = [carve(GP, D) for _ in range(5)]
            ss = carve(G16, D)
            carve = carver(fx[:].rearrange("p a n -> p (a n)"))
            q8 = carve(GP, D, D)
            tmp = carve(GP, D, D)
            mc = carve(B, 12)
            carve = carver(fq[:, 1].rearrange("p f n -> p (f n)"))
            mm_, mt = carve(G16, D, D), carve(G16, D, D)
            b_in, top_in, b_step, b_sqrt = sem("b_in"), sem("top_in"), sem("b_step"), sem("b_sqrt")
            m_out, m_in, m_wrap = sem("m_out"), sem("m_in"), sem("m_wrap")
            PIVOTS_DONE, M_DONE = 31, 113

            filled = sem("filled")
            zs_in = [sem("zs_in_even"), sem("zs_in_odd")]
            side_ready, side_free = sem("side_ready"), sem("side_free")
            tile2_ready = {T_Q1: sem("q2_ready"), T_G1: sem("g2_ready"), T_K1: sem("k2_ready")}
            mb_ready, qs_ready, kh_ready, kl_ready = (
                sem("mb_ready"), sem("qs_ready"), sem("kh_ready"), sem("kl_ready"))
            part_ready, mixed_ready, hi_ready = sem("part_ready"), sem("mixed_ready"), sem("hi_ready")
            lo_ready = {True: sem("lo_on_pool"), False: sem("lo_on_dve")}
            l_ready, nmax_ready, nms_ready, ebias_ready = (
                sem("l_ready"), sem("nmax_ready"), sem("nms_ready"), sem("ebias_ready"))
            exp_done, t_ready, pt_ready = sem("exp_done"), sem("t_ready"), sem("pt_ready")
            o_ready, oT_ready, rden_ready = sem("o_ready"), sem("oT_ready"), sem("rden_ready")
            hsum_ready, mean2_ready, h2_kept = sem("hsum_ready"), sem("mean2_ready"), sem("h2_kept")
            hc_ready, hsq_ready, hssq_ready, var2_ready = (
                sem("hc_ready"), sem("hsq_ready"), sem("hssq_ready"), sem("var2_ready"))
            var2_kept = sem("var2_kept")

            with nc.Block() as block:
                @block.sync
                def _(sp):
                    def load(q, par):
                        for k in range(2):
                            dst = zs[C * k:C * k + C, par].bitcast(F32).rearrange("c (b t n) -> c b t n", b=2, t=2)
                            for t in range(2):
                                sp.dma_start(dst[:, :, t, :], zt_dram[bass.ds(q, 1), k, t].rearrange("a c b n -> (a c) b n")
                                             ).then_inc(zs_in[par], 16)

                    for k in range(2):
                        blocks = gram_dram[k].rearrange("b r c -> (b r c)").rearrange("(m s) -> m s", s=D * C + D)
                        for g in range(G16):
                            sp.dma_start(gl[:, 2 * g + k],
                                         blocks[128 * g:128 * g + 128, 0:D * C].rearrange("m (i c) -> m i c", c=C)[:, :, 0:D]
                                         ).then_inc(b_in, 16)
                    load(0, 0)
                    load(1, 1)
                    sp.wait_ge(b_step, M_DONE)
                    sp.dma_start(m_dram.rearrange("(g b) h i j -> (b h) g (i j)", b=16),
                                 mm_[:].rearrange("p g i j -> p g (i j)")).then_inc(m_out, 16)
                    sp.wait_ge(m_out, 16)
                    for half in range(2):
                        sp.dma_start(mc[half * C:(half + 1) * C, :, 0:D],
                                     m_dram.rearrange("b h i j -> (h i) b j")).then_inc(m_in, 16)
                    sp.wait_ge(side_ready, FEATURES)
                    load(2, 0)
                    sp.wait_ge(side_ready, 2 * FEATURES)
                    load(3, 1)
                    with sp.Fori(0, NP // 2 - 2) as i:
                        for par in range(2):
                            p = 2 * i + par + 1
                            sp.wait_ge(side_ready, 2 * FEATURES + (FEATURES + FINISH) * (p - 1) + FEATURES)
                            load(p + 3, par)

                @block.tensor
                def _(pe):
                    def feature(count, k, q, par):
                        if k == T_Q1:
                            pe.wait_ge(zs_in[par], 32 * q + 64 - 32 * par)
                        if k == T_G1:
                            pe.wait_ge(mb_ready, q + 1)
                            pe.wait_ge(qs_ready, q + 1)
                        pe.wait_ge(side_free, count)
                        if k in (T_Q1, T_Q2, T_Q3, T_K1, T_K2, T_K3):
                            at = V_Q + 128 * (k - T_Q1) if k <= T_Q3 else V_K + 128 * (k - T_K1)
                            pe.matmul(ps[:, SIDE, 0:PW], whi[:, at:at + 128], zs[:, par], start=True, stop=False)
                            mm = pe.matmul(ps[:, SIDE, 0:PW], wlo[:, at:at + 128], zs[:, par], start=False, stop=True)
                        elif k in (T_G1, T_G2, T_G3):
                            n = 2 * (k - T_G1)
                            for b in range(2):
                                for m in (mbh, mbl):
                                    mm = pe.matmul(ps[:, SIDE, b * N:(b + 1) * N],
                                                   m[:, b, n:n + 2, :].rearrange("p s c -> p (s c)"),
                                                   qs[:, b * N:(b + 1) * N], start=m is mbh, stop=m is mbl)
                        else:
                            for t in range(4):
                                for m in (whi, wlo):
                                    mm = pe.matmul(ps[0:NT, SIDE, t * C:(t + 1) * C], zs[:, par, t * NT:(t + 1) * NT],
                                                   m[:, V_V:V_V + C], start=m is whi, stop=m is wlo)
                        mm.then_inc(side_ready, 1)

                    def finish(count, k, q, par):
                        if k == 0:
                            pe.wait_ge(oT_ready, 2 * q + 2)
                        pe.wait_ge(side_free, count)
                        if k < 2:
                            for t in range(2):
                                for og in range(2):
                                    at = (2 * t + og) * 128
                                    mm = pe.transpose(ps[0:NT, SIDE, at:at + 128],
                                                      oT[:, par, og, k * N + t * NT:k * N + (t + 1) * NT], ident[:])
                        elif k == 2:
                            for b in range(2):
                                mm = pe.transpose(ps[:, SIDE, b * NT:(b + 1) * NT],
                                                  otok[:, 2 * b:2 * b + 2, :].rearrange("p t c -> p (t c)"), ident[0:NT, 0:NT])
                        else:
                            for t in range(4):
                                mm = pe.matmul(ps[0:NT, SIDE, t * C:(t + 1) * C], oc[:, t * NT:(t + 1) * NT],
                                               wp[:], start=True, stop=True)
                        mm.then_inc(side_ready, 1)

                    def scores(s, par, o):
                        u, b, t = s // 4, s // 2 % 2, s % 2
                        dst = ps[0:NT, s % 4, o * N:(o + 1) * N]
                        terms = [(F_, k_, ft) for F_, k_ in ((Fh, fkh), (Fh, fkl), (Fl, fkh)) for ft in range(FT)]
                        for n, (F_, k_, ft) in enumerate(terms):
                            mm = pe.matmul(dst, F_[:, u % 2, o, ft, b * N + t * NT:b * N + (t + 1) * NT],
                                           k_[:, par, ft, b * N:(b + 1) * N], start=n == 0, stop=n == len(terms) - 1)
                        return mm

                    def turn(S, tb):
                        pe.wait_ge(exp_done, S + 1)
                        if not (isinstance(S, int) and S < 2):
                            pe.wait_ge(pt_ready, S - 1)
                        for mt in range(2):
                            for o in range(UH):
                                at = (UH * mt + o) * NT
                                mm = pe.transpose(ps[0:NT, T_BANK + tb, at:at + NT],
                                                  prob[:, tb, o, mt * NT:(mt + 1) * NT], ident[0:NT, 0:NT])
                        mm.then_inc(t_ready, 1)

                    def values(G, S, og, b, par):
                        pe.wait_ge(pt_ready, S + 1)
                        if b == 0:
                            pe.wait_ge(oT_ready, G)
                        for mt in range(2):
                            for j in range(OG):
                                mm = pe.matmul(ps[SLOT * j:SLOT * j + VW, O_BANK, b * N:(b + 1) * N],
                                               vx[:, par, 2 * b + mt, OG * og + j, :], probT[:, b, mt, j, :],
                                               start=mt == 0, stop=mt == 1)
                        if b == 1:
                            mm.then_inc(o_ready, 1)

                    def slot(p, par, s, first, last):
                        S = NS * p + s
                        u = s // 4
                        if s == 0:
                            pe.wait_ge(kl_ready, FT * p + FT)
                        if s % 4 == 0:
                            for on_pool, lo in lo_ready.items():
                                pe.wait_ge(lo, lows(p, TILES * u + FT - 1, on_pool))
                        if not (first and s < 4):
                            pe.wait_ge(exp_done, S - 3)
                        scores(s, par, 0)
                        slot_task(p, par, s, first, last, feature, finish)
                        if s % 4 == 0:
                            for on_pool, lo in lo_ready.items():
                                pe.wait_ge(lo, lows(p, TILES * u + TILES - 1, on_pool))
                        scores(s, par, 1).then_inc(l_ready, 1)
                        if s in (0, 2) and not first:
                            values(2 * p - 1, S - 3, 1, s // 2, 1 - par)
                        if s in (8, 10):
                            values(2 * p, S - 3, 0, (s - 8) // 2, par)
                        if not (first and s < 2):
                            turn(S - 2, s % 2)

                    def prologue():
                        pe.wait_ge(filled, 4)
                        for n, k in enumerate(PROLOGUE):
                            feature(n, k, 0, 0)

                    def epilogue():
                        turn(NS * NP - 2, 0)
                        values(2 * NP - 1, NS * NP - 3, 1, 0, 1)
                        turn(NS * NP - 1, 1)
                        values(2 * NP - 1, NS * NP - 1, 1, 1, 1)
                        for k in range(FINISH):
                            finish(task_base(NP - 1) + FINISH + k, k, NP - 1, 1)

                    pairs(pe, prologue, slot, epilogue)

                @block.scalar
                def _(act):
                    def scaled(p, k, par):
                        n, exists, shift, u, o, ft = tile_of(p, k)
                        if not exists:
                            return
                        if not (isinstance(n, int) and n < 4):
                            act.wait_ge(lo_ready[is_on_pool(k - 4)], lows(p, k - 4, is_on_pool(k - 4)))
                        head = UH * u + o
                        nc.scalar.activation(fx[:, k % 4], fq[:, (par + shift) % 2, ft, :], ACT.Copy,
                                             scale=mix[:, 0, ft, head:head + 1]).then_inc(part_ready, 1)

                    def feature(count, k, q, par):
                        if k not in (T_Q1, T_K1, T_G1):
                            return
                        act.wait_ge(side_ready, count + 1)
                        if k == T_G1:
                            nc.scalar.copy(ga[:], ps[:, SIDE, 0:PW]).then_inc(side_free, 1)
                            act.wait_ge(side_free, count + 1)
                            nc.scalar.activation(fg[:, par, 2, :], ga[:], ACT.Square).then_inc(tile2_ready[k], 1)
                        else:
                            bias = fb[:, 0:1] if k == T_Q1 else fb[:, FT:FT + 1]
                            tile2 = fq[:, par, 2, :] if k == T_Q1 else kx[:, 0, :]
                            nc.scalar.activation(qa[:], ps[:, SIDE, 0:PW], ACT.Identity, bias=bias).then_inc(side_free, 1)
                            act.wait_ge(side_free, count + 1)
                            if k == T_Q1:
                                nc.scalar.copy(qs[:], qa[:])
                            nc.scalar.activation(tile2[0:C], qa[0:C], ACT.Square)
                            nc.scalar.copy(tile2[C:], qa[C:]).then_inc(tile2_ready[k], 1)

                    def finish(count, k, q, par):
                        if k == 2:
                            act.wait_ge(side_ready, count + 1)
                            for t in range(2):
                                ins = nc.scalar.copy(oc[0:C, :].rearrange("c (b t n) -> c b t n", b=2, t=2)[:, :, t, :],
                                                     ps[t * C:(t + 1) * C, SIDE, 0:N].rearrange("c (b n) -> c b n", b=2))
                            ins.then_inc(side_free, 1)

                    def center_squares(q):
                        act.wait_ge(hc_ready, q + 1)
                        nc.scalar.copy(h_all[:, bass.ds(4 * q, 4), :], hn[:]).then_inc(h2_kept, 1)
                        act.wait_ge(h2_kept, q + 1)
                        nc.scalar.activation(hn[:], hc[:], ACT.Square).then_inc(hsq_ready, 1)

                    def exps(S, sp_, bank):
                        act.wait_ge(ebias_ready, S + 1)
                        if not (isinstance(S, int) and S < 2):
                            act.wait_ge(t_ready, S - 1)
                        for o in range(UH):
                            ins = nc.scalar.activation(prob[:, sp_, o, :], ps[0:NT, bank, o * N:(o + 1) * N],
                                                       ACT.Exp, bias=ebias[:, sp_, o:o + 1])
                        ins.then_inc(exp_done, 1)

                    def copy_turned(S, s):
                        act.wait_ge(t_ready, S + 1)
                        u, b, t = s // 4, s // 2 % 2, s % 2
                        j = UH * (u % 2)
                        nc.scalar.copy(probT[:, b, :, j:j + UH, t * NT:(t + 1) * NT],
                                       ps[0:NT, T_BANK + s % 2, 0:2 * UH * NT].rearrange("p (m o n) -> p m o n", m=2, o=UH)
                                       ).then_inc(pt_ready, 1)

                    def copy_out(G, par, og):
                        act.wait_ge(o_ready, G + 1)
                        nc.scalar.copy(oT[:, par, og, :], ps[:, O_BANK, 0:PW]).then_inc(oT_ready, 1)

                    def slot(p, par, s, first, last):
                        S = NS * p + s
                        if s == 10 and not last:
                            act.wait_ge(side_free, task_base(p) + T_G3 + 1)

                        steps(p, s, lambda p, k: scaled(p, k + 1, par))
                        if not (first and s == 0):
                            exps(S - 1, (s - 1) % 2, (s - 1) % 4)
                        if s == 3 and not first:
                            copy_out(2 * p - 1, 1 - par, 1)
                        if s == 11:
                            copy_out(2 * p, par, 0)
                        slot_task(p, par, s, first, last, feature, finish)
                        if not first and s == FEATURES + FINISH:
                            center_squares(p - 1)
                        if not (first and s < 2):
                            copy_turned(S - 2, (s - 2) % NS)

                    def prologue():
                        for k in range(2):
                            for g in range(G16):
                                rows = top_dram[k, :, 16 * g:16 * g + 16].rearrange("i b (h j) -> (b h) i j", h=H)
                                act.dma_start(av[:, 2 * g + k], rows).then_inc(top_in, 16)
                        for n, k in enumerate(PROLOGUE):
                            if k == T_G1:
                                act.wait_ge(b_step, PIVOTS_DONE)
                                nc.scalar.activation(rs[:], piv[:], ACT.Sqrt).then_inc(b_sqrt, 1)
                            feature(n, k, 0, 0)
                        act.wait_ge(side_free, FEATURES)
                        for n in range(-1, 7):
                            scaled(0, n + 1, 0)

                    def epilogue():
                        exps(NS * NP - 1, 1, 3)
                        copy_turned(NS * NP - 2, NS - 2)
                        copy_turned(NS * NP - 1, NS - 1)
                        copy_out(2 * NP - 1, 1, 1)
                        for k in range(FINISH):
                            finish(task_base(NP - 1) + FINISH + k, k, NP - 1, 1)
                        center_squares(NP - 1)

                    pairs(act, prologue, slot, epilogue)

                @block.gpsimd
                def _(pool):
                    gp = nc.gpsimd

                    def low(p, k, par):
                        n, exists, shift, u, o, ft = tile_of(p, k)
                        if exists and is_on_pool(k):
                            pool.wait_ge(hi_ready, n + 1)
                            gp.tensor_tensor(Fl[:, u % 2, o, ft, :], fx[:, k % 4], Fh[:, u % 2, o, ft, :].bitcast(F32),
                                             ALU.subtract).then_inc(lo_ready[True], 1)

                    def expand(q, third):
                        pieces = [(dst, src, rows, n, sh) for dst, src, rows in ((mbh, mch, 128), (mbl, mcl, C))
                                  for n, sh in enumerate((0, 0, 1, 2, 3, 4))]
                        for dst, src, rows, n, sh in pieces[4 * third:4 * third + 4]:
                            ins = gp.tensor_tensor(
                                dst[0:rows, :, n, :].rearrange("p b (h j) -> p b h j", h=H),
                                src[:].bitcast(F32)[:, bass.ds(2 * q, 2), sh:sh + D].unsqueeze(2)
                                .broadcast_to([rows, 2, H, D]),
                                bmask[0:rows].unsqueeze(1).unsqueeze(3).broadcast_to([rows, 2, H, D]), ALU.mult)
                        if third == 2:
                            ins.then_inc(mb_ready, 1)

                    def bias(S, sp_, u):
                        pool.wait_ge(nmax_ready, S + 1)
                        sh = shift_o[:, UH * u:UH * u + UH]
                        gp.tensor_tensor(nms[:, sp_], nmax[:, sp_], sh, ALU.subtract).then_inc(nms_ready, 1)
                        pool.wait_ge(nms_ready, S + 1)
                        if not (isinstance(S, int) and S < 2):
                            pool.wait_ge(exp_done, S - 1)
                        gp.tensor_tensor(ebias[:, sp_], nms[:, sp_], sh, ALU.add).then_inc(ebias_ready, 1)

                    def feature(count, k, q, par):
                        if k in (T_K2, T_K3):
                            for n, ft in ((0, 2), (1, 0)) if k == T_K2 else ((2, 1),):
                                pool.wait_ge(kh_ready, FT * q + n + 1)
                                gp.tensor_tensor(fkl[:, par, ft, :], kx[:, n % 2], fkh[:, par, ft, :].bitcast(F32),
                                                 ALU.subtract).then_inc(kl_ready, 1)

                    def slot(p, par, s, first, last):
                        S = NS * p + s
                        steps(p, s, lambda p, k: low(p, k - 1, par))
                        bias(S, s % 2, s // 4)
                        if s < 3 and not last:
                            expand(p + 1, s)
                        slot_task(p, par, s, first, last, feature, lambda *_: None)
                        if not first and s == FEATURES + FINISH - 1:
                            center(p - 1)
                        if not first and s == NS - 1:
                            keep_variance(p - 1)

                    def center(q):
                        pool.wait_ge(mean2_ready, q + 1)
                        gp.tensor_tensor(hc[:], hn[:], stat2[:, 1, :].unsqueeze(2).broadcast_to([NT, 4, C]),
                                         ALU.add).then_inc(hc_ready, 1)
                        gp.tensor_copy(mean2[:, bass.ds(4 * q, 4)], stat2[:, 1, :])

                    def keep_variance(q):
                        pool.wait_ge(var2_ready, q + 1)
                        gp.tensor_copy(var2[:, bass.ds(4 * q, 4)], stat2[:, 3, :]).then_inc(var2_kept, 1)

                    def prologue():
                        for n, k in enumerate(PROLOGUE):
                            feature(n, k, 0, 0)
                        pool.wait_ge(m_wrap, 3)
                        for third in range(3):
                            expand(0, third)
                        for n in range(0, 7):
                            low(0, n - 1, 0)

                    def epilogue():
                        center(NP - 1)
                        keep_variance(NP - 1)

                    pairs(pool, prologue, slot, epilogue)

                @block.vector
                def _(dve):
                    nv = nc.vector

                    def mixed(p, k, par):
                        n, exists, shift, u, o, ft = tile_of(p, k)
                        if exists:
                            dve.wait_ge(part_ready, n + 1)
                            head = UH * u + o
                            nv.scalar_tensor_tensor(out=fx[:, k % 4], in0=fg[:, (par + shift) % 2, ft, :],
                                                    scalar=mix[:, 1, ft, head:head + 1], in1=fx[:, k % 4],
                                                    op0=ALU.mult, op1=ALU.add).then_inc(mixed_ready, 1)

                    def high(p, k, par):
                        n, exists, shift, u, o, ft = tile_of(p, k)
                        if exists:
                            dve.wait_ge(mixed_ready, n + 1)
                            nv.tensor_copy(Fh[:, u % 2, o, ft, :], fx[:, k % 4]).then_inc(hi_ready, 1)

                    def low(p, k, par):
                        n, exists, shift, u, o, ft = tile_of(p, k)
                        if exists and not is_on_pool(k):
                            dve.wait_ge(hi_ready, n + 1)
                            nv.tensor_tensor(Fl[:, u % 2, o, ft, :], fx[:, k % 4], Fh[:, u % 2, o, ft, :].bitcast(F32),
                                             ALU.subtract).then_inc(lo_ready[False], 1)

                    def step(p, k, par):
                        mixed(p, k, par)
                        low(p, k - 2, par)
                        high(p, k - 1, par)

                    def split_k(q, par, n, ft):
                        nv.tensor_copy(fkh[:, par, ft, :], kx[:, n % 2]).then_inc(kh_ready, 1)

                    def feature(count, k, q, par):
                        found = {T_Q2: (fq[:, par, 0, :], qa, 1), T_Q3: (fq[:, par, 1, :], qa, 2),
                                 T_G2: (fg[:, par, 0, :], ga, None), T_G3: (fg[:, par, 1, :], ga, None),
                                 T_K2: (kx[:, 1, :], qa, FT + 1), T_K3: (kx[:, 0, :], qa, FT + 2)}.get(k)
                        if found:
                            dst, src, bias = found
                            dve.wait_ge(side_ready, count + 1)
                            dve.wait_ge(side_free, count)
                            if k in (T_Q2, T_G2, T_K2):
                                dve.wait_ge(tile2_ready[k - 1], q + 1)
                            if k == T_K3:
                                dve.wait_ge(kl_ready, FT * q + 1)
                            if bias is None:
                                nv.tensor_tensor(dst, ps[:, SIDE, 0:PW], src[:], ALU.mult).then_inc(side_free, 1)
                            else:
                                nv.scalar_tensor_tensor(out=dst, in0=ps[:, SIDE, 0:PW], scalar=fb[:, bias:bias + 1],
                                                        in1=src[:], op0=ALU.add, op1=ALU.mult).then_inc(side_free, 1)
                        if k == T_Q2:
                            nv.tensor_tensor(qs[C:], qa[C:], qs[C:].bitcast(F32), ALU.subtract).then_inc(qs_ready, 1)
                        if k == T_K2:
                            split_k(q, par, 0, 2)
                        if k in (T_K2, T_K3):
                            dve.wait_ge(side_free, count + 1)
                            split_k(q, par, k - T_K1, k - T_K2)
                        if k == T_V:
                            dve.wait_ge(side_ready, count + 1)
                            nv.tensor_tensor(vx[:, par, :, :, 0:D],
                                             ps[0:NT, SIDE, 0:4 * C].rearrange("p (t h d) -> p t h d", t=4, h=H),
                                             vb[:].rearrange("p (h d) -> p h d", h=H).unsqueeze(1)
                                             .broadcast_to([NT, 4, H, D]), ALU.add).then_inc(side_free, 1)

                    def finish(count, k, q, par):
                        if k < 2:
                            dve.wait_ge(side_ready, count + 1)
                            v = ps[0:NT, SIDE, :].rearrange("p (a v) -> p a v", v=SLOT)
                            nv.reciprocal(rden[:].unsqueeze(2), v[:, :, D:D + 1]).then_inc(rden_ready, 1)
                            dve.wait_ge(rden_ready, 2 * q + k + 1)
                            nv.tensor_tensor(otok[:, 2 * k:2 * k + 2, :].rearrange("p t (h d) -> p (t h) d", h=H), v[:, :, 0:D],
                                             rden[:].unsqueeze(2).broadcast_to([NT, 2 * H, D]), ALU.mult
                                             ).then_inc(side_free, 1)
                        if k == 3:
                            dve.wait_ge(side_ready, count + 1)
                            nv.tensor_tensor(hn[:], h_all[:, bass.ds(4 * q, 4), :],
                                             ps[0:NT, SIDE, 0:4 * C].rearrange("p (t c) -> p t c", c=C),
                                             ALU.add).then_inc(side_free, 1)
                            dve.wait_ge(side_free, count + 1)
                            nv.tensor_reduce(stat2[:, 0, :], hn[:], AX.X, ALU.add).then_inc(hsum_ready, 1)
                            dve.wait_ge(hsum_ready, q + 1)
                            nv.tensor_scalar(stat2[:, 1, :], stat2[:, 0, :], -1.0 / C, None, ALU.mult
                                             ).then_inc(mean2_ready, 1)

                    def variance(q):
                        dve.wait_ge(hsq_ready, q + 1)
                        nv.tensor_reduce(stat2[:, 2, :], hn[:], AX.X, ALU.add).then_inc(hssq_ready, 1)
                        dve.wait_ge(hssq_ready, q + 1)
                        nv.tensor_scalar(stat2[:, 3, :], stat2[:, 2, :], 1.0 / C, LN_EPS, ALU.mult, ALU.add
                                         ).then_inc(var2_ready, 1)

                    def row_max(S, sp_, bank):
                        dve.wait_ge(l_ready, S + 1)
                        if not (isinstance(S, int) and S < 2):
                            dve.wait_ge(nms_ready, S - 1)
                        nv.tensor_reduce(nmax[:, sp_], ps[0:NT, bank, 0:PW].rearrange("p (o n) -> p o n", o=UH),
                                         AX.X, ALU.max, negate=True).then_inc(nmax_ready, 1)

                    def slot(p, par, s, first, last):
                        S = NS * p + s

                        steps(p, s, lambda p, k: step(p, k, par))
                        slot_task(p, par, s, first, last, feature, finish)
                        if not first and s == NS - 1:
                            variance(p - 1)
                        row_max(S, s % 2, s % 4)

                    def grassmann():
                        steps = [0]

                        def link(ins):
                            steps[0] += 1
                            ins.then_inc(b_step, 1)
                            dve.wait_ge(b_step, steps[0])

                        link(nv.tensor_copy(gw[:, :, :, D:], eye8[:].rearrange("p (i j) -> p i j", i=D)
                                            .unsqueeze(1).broadcast_to([128, GP, D, D])))
                        dve.wait_ge(b_in, 16 * GP)
                        link(nv.tensor_copy(gw[:, :, :, 0:D], gl[:]))
                        for d in range(D - 1):
                            n = D - 1 - d
                            cols = slice(d + 1, d + 1 + D)
                            link(nv.reciprocal(piv[:, :, d:d + 1], gw[:, :, d, d:d + 1]))
                            link(nv.tensor_tensor(fac[:, :, 0:n], gw[:, :, d + 1:, d],
                                                  piv[:, :, d:d + 1].broadcast_to([128, GP, n]), ALU.mult))
                            link(nv.tensor_tensor(tmp[:, :, 0:n, :],
                                                  fac[:, :, 0:n].unsqueeze(3).broadcast_to([128, GP, n, D]),
                                                  gw[:, :, d:d + 1, cols].broadcast_to([128, GP, n, D]), ALU.mult))
                            link(nv.tensor_tensor(gw[:, :, d + 1:, cols], gw[:, :, d + 1:, cols], tmp[:, :, 0:n, :],
                                                  ALU.subtract))
                            if d >= 2:
                                feature(d - 2, PROLOGUE[d - 2], 0, 0)
                        link(nv.tensor_copy(piv[:], gw[:].rearrange("p g i j -> p g (i j)")[:, :, 0:128:17]))
                        assert steps[0] == PIVOTS_DONE, steps[0]
                        dve.wait_ge(b_sqrt, 1)
                        link(nv.reciprocal(rs[:], rs[:]))
                        link(nv.tensor_tensor(sg[:], rs[:], rs[:], ALU.mult))
                        link(nv.tensor_tensor(sg[:], sg[:], piv[:], ALU.mult))
                        link(nv.tensor_scalar(sg[:], sg[:], -0.5, 1.5, ALU.mult, ALU.add))
                        link(nv.tensor_tensor(rs[:], rs[:], sg[:], ALU.mult))
                        link(nv.tensor_tensor(ri[:], gw[:, :, :, D:].rearrange("p g j i -> p g i j"),
                                              rs[:].unsqueeze(2).broadcast_to([128, GP, D, D]), ALU.mult))

                        def add_product(first, dst, part, left, right, shape):
                            link(nv.tensor_tensor(dst if first else part, left.unsqueeze(3).broadcast_to(shape),
                                                  right.unsqueeze(2).broadcast_to(shape), ALU.mult))
                            if not first:
                                link(nv.tensor_tensor(dst, dst, part, ALU.add))

                        dve.wait_ge(top_in, 16 * GP)
                        for i in range(D):
                            add_product(i == 0, q8[:, :, :, i:], tmp[:, :, :, i:], av[:, :, :, i], ri[:, :, i, i:],
                                        [128, GP, D, D - i])
                            if i in (1, 3):
                                feature(5 + i // 2, PROLOGUE[5 + i // 2], 0, 0)
                        for d in range(D):
                            n = D - 1 - d
                            pivot = q8[:, :, d, d:d + 1]
                            link(nv.tensor_scalar(sn[:, :, d:d + 1], pivot, 0.0, -2.0, ALU.is_lt, ALU.mult))
                            if not n:
                                break
                            link(nv.scalar_tensor_tensor(out=fac[:, :, 7:8], in0=sn[:, :, d:d + 1], scalar=1.0, in1=pivot,
                                                         op0=ALU.add, op1=ALU.add))
                            link(nv.reciprocal(fac[:, :, 7:8], fac[:, :, 7:8]))
                            link(nv.tensor_tensor(fac[:, :, 0:n], q8[:, :, d + 1:, d],
                                                  fac[:, :, 7:8].broadcast_to([128, GP, n]), ALU.mult))
                            link(nv.tensor_tensor(tmp[:, :, 0:n, 0:n],
                                                  fac[:, :, 0:n].unsqueeze(3).broadcast_to([128, GP, n, n]),
                                                  q8[:, :, d:d + 1, d + 1:].broadcast_to([128, GP, n, n]), ALU.mult))
                            link(nv.tensor_tensor(q8[:, :, d + 1:, d + 1:], q8[:, :, d + 1:, d + 1:],
                                                  tmp[:, :, 0:n, 0:n], ALU.subtract))
                        link(nv.tensor_scalar(sg[:], sn[:], -1.0, -1.0, ALU.mult, ALU.add))
                        link(nv.tensor_tensor(ss[:], sg[:, 0::2, :], sg[:, 1::2, :], ALU.mult))
                        link(nv.tensor_tensor(mt[:], ri[:, 0::2, :, :],
                                              ss[:].unsqueeze(2).broadcast_to([128, G16, D, D]), ALU.mult))
                        for i in reversed(range(D)):
                            m = i + 1
                            add_product(i == D - 1, mm_[:, :, 0:m, 0:m], tmp[:, 0:G16, 0:m, 0:m], mt[:, :, 0:m, i],
                                        ri[:, 1::2, 0:m, i], [128, G16, m, m])
                        assert steps[0] == M_DONE, steps[0]
                        dve.wait_ge(m_in, 16 * 2)
                        nv.tensor_copy(mc[:, :, D:12], mc[:, :, 0:4]).then_inc(m_wrap, 1)
                        dve.wait_ge(m_wrap, 1)
                        nv.tensor_copy(mch[:], mc[:]).then_inc(m_wrap, 1)
                        dve.wait_ge(m_wrap, 2)
                        nv.tensor_tensor(mcl[:], mc[0:C], mch[0:C].bitcast(F32), ALU.subtract).then_inc(m_wrap, 1)

                    def prologue():
                        nv.memset(mbl[C:].bitcast(F32), 0.0).then_inc(filled, 1)
                        nv.memset(oc[C:C + 1, :], 1.0).then_inc(filled, 1)
                        nv.memset(vx[:, :, :, :, D:VW], 1.0).then_inc(filled, 1)
                        nv.memset(ps[:, O_BANK, :], 0.0).then_inc(filled, 1)
                        grassmann()
                        for n, k in enumerate(PROLOGUE):
                            if k in (T_G1, T_G2, T_G3):
                                feature(n, k, 0, 0)
                        for n in range(0, 7):
                            step(0, n, 0)

                    def epilogue():
                        for k in range(FINISH):
                            finish(task_base(NP - 1) + FINISH + k, k, NP - 1, 1)
                        variance(NP - 1)

                    pairs(dve, prologue, slot, epilogue)

        NCH = 4
        CH, CG = NTILE // NCH, NP // NCH
        with ExitStack() as st:
            yc = sb("yc", [NT, NTILE, C], stack=st)
            zs2 = sb("zs2", [NT, 2, 4, C], stack=st)
            z2 = sb("z2", [NT, 2, 4, C], stack=st)
            z2h = sb("z2h", [128, 2, N], F32R, stack=st)
            z2l = sb("z2l", [128, 2, N], F32R, stack=st)
            w1f = sb("w1f", [128, 2, HID], stack=st)
            w1h = sb("w1h", [128, 2, HID], F32R, stack=st)
            w1l = sb("w1l", [128, 2, HID], F32R, stack=st)
            hid = sb("hid", [128, 2, 2, PW], stack=st)
            hidh = sb("hidh", [128, 2, 2, PW], F32R, stack=st)
            hidl = sb("hidl", [128, 2, 2, PW], F32R, stack=st)
            wl = sb("wl", [128, 2, E + E * C], stack=st)
            wlh = sb("wlh", [128, 2, E + E * C], F32R, stack=st)
            wll = sb("wll", [128, 2, E + E * C], F32R, stack=st)
            lg = sb("lg", [NT, NTILE, E], stack=st)
            gmax = sb("gmax", [NT, 2], stack=st)
            score = sb("score", [NT, E], stack=st)
            pick = sb("pick", [NT, 2], stack=st)
            emask = sb("emask", [NT, E], stack=st)
            chosen = sb("chosen", [NT, 2, 2, E, C], stack=st)
            gexp = sb("gexp", [NT, CH, E], stack=st)
            gsum = sb("gsum", [NT, CH], stack=st)
            w1_in, wl_in, w1_ready, wl_ready = sem("w1_in"), sem("wl_in"), sem("w1_ready"), sem("wl_ready")
            d_std, d_rstd = sem("d_std"), sem("d_rstd")
            zs2_ready, z2_ready, z2T_ready = sem("zs2_ready"), sem("z2_ready"), sem("z2T_ready")
            z2h_ready, z2l_ready = sem("z2h_ready"), sem("z2l_ready")
            hid_ready, gelu_done, hidh_ready = sem("hid_ready"), sem("gelu_done"), sem("hidh_ready")
            hidl_ready = [sem("hidl_dve_ready"), sem("hidl_pool_ready")]
            y2_ready, y2_free, halved, added = sem("y2_ready"), sem("y2_free"), sem("halved"), sem("added")
            gexp_ready, gsum_ready, prob_ready, scaled_y = (
                sem("gexp_ready"), sem("gsum_ready"), sem("prob_ready"), sem("scaled_y"))
            d_pick, res_ready, stored = sem("d_pick"), sem("res_ready"), sem("stored")

            AHEAD = 4

            def groups(eng, lo, hi, group):
                a, b = max(lo, 2), max(lo, 2, min(hi, NP - AHEAD))
                for g in range(lo, min(a, hi)):
                    group(g, g % 2)
                if b > a:
                    with eng.Fori(0, (b - a) // 2) as i:
                        for par in range(2):
                            group(2 * i + a + par, par)
                for g in range(b, hi):
                    group(g, g % 2)

            def exists(g):
                return not isinstance(g, int) or g < NP

            def quarters(eng, group, quarter):
                done = 0
                for c in range(NCH):
                    upto = min(NP, CG * (c + 1) + 2)
                    groups(eng, done, upto, group)
                    done = upto
                    quarter(c)

            with nc.Block() as block:
                @block.vector
                def _(dve):
                    nv = nc.vector
                    dve.wait_ge(d_std, 1)
                    nv.reciprocal(var2[:], var2[:]).then_inc(d_rstd, 1)
                    dve.wait_ge(w1_in, 16)
                    nv.tensor_copy(w1h[:], w1f[:]).then_inc(w1_ready, 1)
                    dve.wait_ge(w1_ready, 1)
                    nv.tensor_tensor(w1l[:], w1f[:], w1h[:].bitcast(F32), ALU.subtract).then_inc(w1_ready, 1)

                    def split_z(g, par):
                        dve.wait_ge(z2h_ready, g + 1)
                        nv.tensor_tensor(z2l[:, par], ps[:, 0, 0:N], z2h[:, par].bitcast(F32), ALU.subtract
                                         ).then_inc(z2l_ready, 1)

                    def low(g, par):
                        dve.wait_ge(hidh_ready, 2 * g + 1)
                        if not (isinstance(g, int) and g < 2):
                            dve.wait_ge(y2_ready, 4 * g - 4)
                        nv.tensor_tensor(hidl[:, par, 0], hid[:, par, 0], hidh[:, par, 0].bitcast(F32), ALU.subtract
                                         ).then_inc(hidl_ready[0], 1)

                    def choose(g, k):
                        T = 4 * g + k
                        b = k % 2
                        dve.wait_ge(y2_ready, T + 1)
                        gates = ps[0:NT, 3 + 2 * b, 0:E]
                        gmx = gmax[:, b:b + 1]
                        nv.tensor_reduce(gmx, gates, AX.X, ALU.max).then_inc(d_pick, 1)
                        dve.wait_ge(d_pick, 4 * T + 1)
                        nv.scalar_tensor_tensor(out=score[:], in0=gates, scalar=gmx, in1=pri[:],
                                                op0=ALU.is_ge, op1=ALU.mult).then_inc(d_pick, 1)
                        nv.tensor_scalar(lg[:, bass.ds(T, 1), :].rearrange("p a e -> p (a e)"), gates, gmx, None, ALU.subtract)
                        dve.wait_ge(d_pick, 4 * T + 2)
                        nv.tensor_reduce(pick[:, b:b + 1], score[:], AX.X, ALU.max).then_inc(d_pick, 1)
                        dve.wait_ge(d_pick, 4 * T + 3)
                        nv.tensor_scalar(emask[:], pri[:], pick[:, b:b + 1], None, ALU.is_equal).then_inc(d_pick, 1)
                        dve.wait_ge(d_pick, 4 * T + 4)
                        if b == 0 and not (isinstance(g, int) and g == 0):
                            dve.wait_ge(added, 2 * g + k // 2 - 1)
                        nv.tensor_tensor(chosen[:, k // 2, b].rearrange("p (a e) c -> p a e c", a=2),
                                         ps[0:NT, 3 + 2 * b:5 + 2 * b, E:E + 4 * C].rearrange("p a (e c) -> p a e c", e=4),
                                         emask[:].rearrange("p (a e) -> p a e", a=2).unsqueeze(3).broadcast_to([NT, 2, 4, C]),
                                         ALU.mult).then_inc(y2_free, 1)

                    def group(g, par):
                        for k in range(4):
                            choose(g, k)
                            if k == 1 and exists(g + 1):
                                low(g + 1, 1 - par)
                            if k == 2 and exists(g + 2):
                                split_z(g + 2, par)

                    def quarter(c):
                        at = slice(c * CH, (c + 1) * CH)
                        dve.wait_ge(gexp_ready, c + 1)
                        nv.tensor_reduce(gsum[:], gexp[:], AX.X, ALU.add).then_inc(gsum_ready, 1)
                        dve.wait_ge(gsum_ready, c + 1)
                        nv.reciprocal(gsum[:], gsum[:]).then_inc(prob_ready, 1)
                        dve.wait_ge(scaled_y, c + 1)
                        nv.tensor_tensor(h_all[:, at, :], h_all[:, at, :], yc[:, at, :], ALU.add).then_inc(res_ready, 1)

                    split_z(0, 0)
                    dve.wait_ge(wl_in, 16)
                    nv.tensor_copy(wlh[:], wl[:]).then_inc(wl_ready, 1)
                    dve.wait_ge(wl_ready, 1)
                    nv.tensor_tensor(wll[:], wl[:], wlh[:].bitcast(F32), ALU.subtract).then_inc(wl_ready, 1)
                    low(0, 0)
                    split_z(1, 1)
                    quarters(dve, group, quarter)

                @block.gpsimd
                def _(pool):
                    gp = nc.gpsimd

                    def scale(g, par):
                        if not (isinstance(g, int) and g < 2):
                            pool.wait_ge(z2T_ready, g - 1)

                        def stat(ap):
                            return ap[:, bass.ds(4 * g, 4)].unsqueeze(2).broadcast_to([NT, 4, C])

                        gp.tensor_tensor(zs2[:, par], h_all[:, bass.ds(4 * g, 4), :], stat(mean2), ALU.add
                                         ).then_inc(zs2_ready, 1)
                        pool.wait_ge(zs2_ready, g + 1)
                        gp.tensor_tensor(z2[:, par], zs2[:, par], stat(var2), ALU.mult).then_inc(z2_ready, 1)

                    def low(g, par):
                        pool.wait_ge(hidh_ready, 2 * g + 2)
                        if not (isinstance(g, int) and g < 2):
                            pool.wait_ge(y2_ready, 4 * g - 4)
                        gp.tensor_tensor(hidl[:, par, 1], hid[:, par, 1], hidh[:, par, 1].bitcast(F32), ALU.subtract
                                         ).then_inc(hidl_ready[1], 1)

                    def add(g, k):
                        pool.wait_ge(y2_free, 4 * g + 2 * k + 2)
                        u = 2 * g + k
                        for n in (4, 2):
                            gp.tensor_tensor(chosen[:, k, :, 0:n], chosen[:, k, :, 0:n], chosen[:, k, :, n:2 * n], ALU.add
                                             ).then_inc(halved, 1)
                            pool.wait_ge(halved, 2 * u + (1 if n == 4 else 2))
                        gp.tensor_tensor(yc[:, bass.ds(4 * g + 2 * k, 2), :], chosen[:, k, :, 0], chosen[:, k, :, 1], ALU.add
                                         ).then_inc(added, 1)

                    def group(g, par):
                        if exists(g + 3):
                            scale(g + 3, 1 - par)
                        if exists(g + 1):
                            low(g + 1, 1 - par)
                        add(g, 0)
                        add(g, 1)

                    def quarter(c):
                        at = slice(c * CH, (c + 1) * CH)
                        pool.wait_ge(prob_ready, c + 1)
                        pool.wait_ge(added, 2 * CG * (c + 1))
                        gp.tensor_tensor(yc[:, at, :], yc[:, at, :], gsum[:].unsqueeze(2).broadcast_to([NT, CH, C]),
                                         ALU.mult).then_inc(scaled_y, 1)

                    pool.wait_ge(d_rstd, 1)
                    for g in range(3):
                        scale(g, g % 2)
                    low(0, 0)
                    quarters(pool, group, quarter)

                @block.scalar
                def _(act):
                    nc.scalar.activation(var2[:], var2[:], ACT.Sqrt).then_inc(d_std, 1)

                    def front(g, par):
                        act.wait_ge(z2T_ready, g + 1)
                        nc.scalar.copy(z2h[:, par], ps[:, 0, 0:N]).then_inc(z2h_ready, 1)
                        if not (isinstance(g, int) and g < 2):
                            for done in hidl_ready:
                                act.wait_ge(done, g - 1)
                            act.wait_ge(y2_ready, 4 * g - 4)
                        for c in range(2):
                            act.wait_ge(hid_ready, 2 * g + c + 1)
                            nc.scalar.activation(hid[:, par, c], ps[:, 1 + c, 0:PW], ACT.Gelu,
                                                 bias=fb[:, 2 * FT + c:2 * FT + c + 1]).then_inc(gelu_done, 1)
                            act.wait_ge(gelu_done, 2 * g + c + 1)
                            nc.scalar.copy(hidh[:, par, c], hid[:, par, c]).then_inc(hidh_ready, 1)

                    def quarter(c):
                        act.wait_ge(y2_free, CH * (c + 1))
                        if c:
                            act.wait_ge(gsum_ready, c)
                        nc.scalar.activation(gexp[:], lg[:, c * CH:(c + 1) * CH, :], ACT.Exp).then_inc(gexp_ready, 1)

                    quarters(act, front, quarter)

                @block.tensor
                def _(pe):
                    def turn(g, par):
                        pe.wait_ge(z2_ready, g + 1)
                        pe.wait_ge(z2l_ready, g)
                        for t in range(2):
                            mm = pe.transpose(ps[:, 0, t * NT:(t + 1) * NT],
                                              z2[:, par, 2 * t:2 * t + 2, :].rearrange("p t c -> p (t c)"), ident[0:NT, 0:NT])
                        mm.then_inc(z2T_ready, 1)

                    def first_layer(g, par, c):
                        pe.wait_ge(z2l_ready, g + 1)
                        if not (isinstance(g, int) and g == 0):
                            pe.wait_ge(gelu_done, 2 * g - 1 + c)
                        for t in range(2):
                            for zp, wp_ in ((z2l, w1h), (z2h, w1l), (z2h, w1h)):
                                mm = pe.matmul(ps[:, 1 + c, t * N:(t + 1) * N], wp_[:, t, 128 * c:128 * (c + 1)], zp[:, par],
                                               start=zp is z2l, stop=zp is z2h and wp_ is w1h)
                        mm.then_inc(hid_ready, 1)

                    def experts(g, par, k):
                        if not (isinstance(g, int) and g == 0 and k < 2):
                            pe.wait_ge(y2_free, 4 * g + k - 1)
                        at = (k % 2 * 2 + k // 2) * NT
                        for a, (lo, hi) in enumerate(((0, E + 4 * C), (E + 4 * C, E + 8 * C))):
                            off = 0 if a == 0 else E
                            dst = ps[0:NT, 3 + 2 * (k % 2) + a, off:off + hi - lo]
                            pe.matmul(dst, ones3[:], wb3[:, lo:hi], start=True, stop=False)
                            for hp, wp in ((hidl, wlh), (hidh, wll), (hidh, wlh)):
                                for c in range(2):
                                    mm = pe.matmul(dst, hp[:, par, c, at:at + NT], wp[:, c, lo:hi],
                                                   start=False, stop=hp is hidh and wp is wlh and c == 1)
                        mm.then_inc(y2_ready, 1)

                    def group(g, par):
                        for done in hidl_ready:
                            pe.wait_ge(done, g + 1)
                        for k in range(4):
                            experts(g, par, k)
                            if k < 2 and exists(g + 1):
                                first_layer(g + 1, 1 - par, k)
                            if k == 2 and exists(g + 2):
                                turn(g + 2, par)

                    turn(0, 0)
                    pe.wait_ge(w1_ready, 2)
                    for c in range(2):
                        first_layer(0, 0, c)
                    turn(1, 1)
                    pe.wait_ge(wl_ready, 2)
                    groups(pe, 0, NP, group)

                @block.sync
                def _(sp):
                    sp.dma_start(w1f[:], w1).then_inc(w1_in, 16)
                    sp.dma_start(wl[:], wall).then_inc(wl_in, 16)
                    nb = CH // 2
                    for c in range(NCH):
                        sp.wait_ge(res_ready, c + 1)
                        sp.dma_start(out[c * nb:(c + 1) * nb].rearrange("b (t p) c -> p (b t) c", t=2),
                                     h_all[:, c * CH:(c + 1) * CH, :]).then_inc(stored, 16)
                    sp.wait_ge(stored, 16 * NCH)


def kernel(**inputs):
    import concourse.bacc as bacc
    from concourse.bass_utils import run_bass_kernel_spmd as run

    a = {k: np.asarray(v) for k, v in inputs.items()}
    arrays = lay_out(a)
    B = a["x"].shape[0]
    nc = bacc.Bacc("TRN2", target_bir_lowering=False, num_devices=1)
    args = [nc.dram_tensor(n, v.shape, mybir.dt.from_np(v.dtype), kind="ExternalInput").ap()
            for n, v in arrays.items()]
    o = nc.dram_tensor("out_dram", (B, N, C), F32, kind="ExternalOutput").ap()
    audio_tower(nc, *args, o)
    r = run(nc, [arrays], core_ids=[0])
    return r.results[0]["out_dram"]


def lay_out(a):
    f = np.float32
    row = np.arange(128)
    half, h, d = row // C, row % C // D, row % D

    def with_bias(wm, bias):
        return np.concatenate([wm, bias[None]], 0)

    wqkv = with_bias(a["L0_attn_w_qkv"].T, a["L0_attn_b_qkv"])
    twice = h * D + d
    cols = [twice] + [h * D + (d + 2 * t + 1 + half) % D for t in range(2)]
    cols = np.concatenate(cols)
    wf = np.concatenate([wqkv[:, cols], wqkv[:, C + cols], wqkv[:, 2 * C:]], 1)
    w128 = np.concatenate([wf[:C], wf[:C]], 0)
    fbias = np.concatenate([wf[C, :2 * FT * 128].reshape(2 * FT, 128).T, a["L0_ffn_b1"].reshape(2, 128).T], 1)
    vbias = np.broadcast_to(wf[C, 2 * FT * 128:], (128, C))
    wqk = np.zeros((128, 4 * C), f)
    for t in range(2):
        wqk[t * C:(t + 1) * C, 2 * C * t:2 * C * (t + 1)] = wqkv[:C, 0:2 * C]
    wproj = with_bias(a["L0_attn_w_proj"].T, a["L0_attn_b_proj"])
    w1 = np.zeros((128, 2, HID), f)
    for t in range(2):
        w1[t * C:(t + 1) * C, t] = a["L0_ffn_W1"]
    kconv = a["L0_tok_kernel"].transpose(1, 0, 2).reshape(CIN, TAPS * C)
    chan = np.stack([a["L0_tok_bias"], a["L0_tok_beta"], a["L0_tok_moving_mean"], a["L0_tok_moving_var"]])
    chan = np.broadcast_to(chan, (128, 4, C))
    wall = np.concatenate([a["L0_ffn_Wg"]] + list(a["L0_ffn_Wd"]), 1).reshape(2, 128, E + E * C).transpose(1, 0, 2)
    wbias = np.concatenate([a["L0_ffn_bg"], a["L0_ffn_bd"].reshape(-1), wqkv[C, :2 * C], wqkv[C, :2 * C]])[None]

    low = half == 1
    channel = np.stack([np.stack([H + h, H + h, np.where(low, h, H + h)], 1), np.repeat(2 * H + h[:, None], FT, 1)], 1)
    pairs_counted = np.ones((128, 2, FT), f)
    pairs_counted[:, :, 0] = 2
    pairs_counted[~low, :, 1] = 2
    pairs_counted[low, 1, 2] = 0
    scales = np.broadcast_to(a["L0_attn_riem_scale"], (128, 2, FT)).copy()
    scales[:, 1] = a["L0_attn_grassman_scale"]
    scales[low, 0, 2] = a["L0_attn_scale"]
    mixw = a["L0_attn_conv_w"].T[channel]
    flat = channel.reshape(128, 2 * FT)
    mixbn = np.stack([a["L0_attn_bn_gamma"][flat], a["L0_attn_bn_var"][flat], scales.reshape(128, -1),
                      pairs_counted.reshape(128, -1)], 1)
    cw = np.broadcast_to(with_bias(a["L0_attn_conv_w"].T, a["L0_attn_conv_b"]).T, (128, H, 25))
    cbn = np.broadcast_to(np.stack([a["L0_attn_bn_gamma"], a["L0_attn_bn_var"], a["L0_attn_bn_mean"],
                                    a["L0_attn_bn_beta"]]), (128, 4, 24))
    consts = np.zeros((128, 224), f)
    consts[:, 0:128] = np.eye(128)
    consts[:, 144:208] = np.eye(D).reshape(-1)
    consts[row, 216 + h] = 1
    consts[:, 208:216] = np.arange(E, 0, -1)
    named = dict(x=a["x"], wproj=wproj, w128=w128, wqk=wqk, w1=w1, fbias=fbias, vbias=vbias, kconv=kconv, chan=chan, wall=wall,
                 wbias=wbias, mixw=mixw, mixbn=mixbn, cw=cw, cbn=cbn, consts=consts)
    return {f"in_{k}_dram": np.ascontiguousarray(v) for k, v in named.items()}
```
